# Optimizing a Trainium2 kernel written in Bass

```python
import numpy as np
import jax
import jax.numpy as jnp

def _softmax(x, axis=-1):
    return jax.nn.softmax(x, axis=axis)

def _gelu(x):
    return jax.nn.gelu(x, approximate=True)

def _silu(x):
    return jax.nn.silu(x)

def _sigmoid(x):
    return jax.nn.sigmoid(x)

def _layernorm(x, axis=-1, eps=1e-05):
    m = jnp.mean(x, axis=axis, keepdims=True)
    v = jnp.var(x, axis=axis, keepdims=True)
    return (x - m) / jnp.sqrt(v + eps)

def _scatter_add(tgt, idx, src, axis=0):
    return tgt.at[idx].add(src)

def _segment_sum(src, seg, n):
    return jax.ops.segment_sum(src, seg, n)
kernel_name = 'mk_adaln_ffn_d2_seqx_r4_4645cf'

def setup_inputs(seed: int=0):
    np.random.seed(seed)
    _w = jnp.asarray

    def _rec_inputs():
        import jax
        import jax.numpy as jnp
        _rk = jax.random.key(seed)
        x = 4.136e-05 + 0.9999 * jax.random.normal(jax.random.fold_in(_rk, 1), (16, 256, 256), jnp.float32)
        _lenS = 256 - jax.random.randint(jax.random.fold_in(_rk, 7), (16,), 0, max(1, 256 // 4) + 1, jnp.int32)
        _lenS2 = 256 - jax.random.randint(jax.random.fold_in(_rk, 8), (16,), 0, max(1, 256 // 4) + 1, jnp.int32)
        cond_1024 = -0.00499425 + 1.0058 * jax.random.normal(jax.random.fold_in(_rk, 11), (16, 256), jnp.float32)
        return (x, cond_1024)
    x, cond_1024 = _rec_inputs()

    def _L0_cond_setup():
        import jax, jax.numpy as jnp
        import numpy as np
        B, N, D, C = (32, 64, 256, 256)
        key = jax.random.key(seed)
        k1, k2, k3, k4 = jax.random.split(key, 4)
        scale = 1.0 / np.sqrt(D)
        return {'encoded_utterance': jax.random.normal(k1, (B, D), dtype=jnp.float32), 'element_embeddings': jax.random.normal(k2, (B, N, D), dtype=jnp.float32), 'weight_matrix': jax.random.normal(k3, (2 * D, C), dtype=jnp.float32) * scale, 'W_proj': jax.random.normal(k4, (D, D), dtype=jnp.float32) * scale, 'b_proj': jnp.zeros((D,), dtype=jnp.float32)}
    _L0_cond_all = _L0_cond_setup()
    _L0_cond_in = {k: v for k, v in _L0_cond_all.items() if k in ('weight_matrix', 'W_proj', 'b_proj')}
    del _L0_cond_all

    def _L0_ffn_setup():
        import jax, jax.numpy as jnp
        import numpy as np
        BLOCK = 32
        W_BITS = 4
        ACT_BITS = 16

        def act_qdq(x):
            qmax = 2.0 ** (ACT_BITS - 1) - 1.0
            scale = jnp.maximum(jnp.max(jnp.abs(x)) / qmax, 1e-12)
            return jnp.clip(jnp.round(x / scale), -qmax - 1.0, qmax) * scale

        def fixed_qdq_u16(x):
            scale = 1.0 / 65536.0
            return jnp.clip(jnp.round(x / scale), 0.0, 65535.0) * scale

        def lpbq_dequant(w):
            O, I = w.shape
            qmax = 2.0 ** (W_BITS - 1) - 1.0
            wb = w.reshape(O, I // BLOCK, BLOCK)
            s = jnp.maximum(jnp.max(jnp.abs(wb), axis=-1, keepdims=True) / qmax, 1e-12)
            wq = jnp.clip(jnp.round(wb / s), -qmax - 1.0, qmax) * s
            return wq.reshape(O, I)
        key = jax.random.key(seed)
        k1, k2, k3, k4 = jax.random.split(key, 4)
        B, S, H, I = (2, 1024, 256, 768)
        x = jax.random.normal(k1, (B, S, H), jnp.float32)
        w_gate = jax.random.normal(k2, (I, H), jnp.float32) * 0.02
        w_up = jax.random.normal(k3, (I, H), jnp.float32) * 0.02
        w_down = jax.random.normal(k4, (H, I), jnp.float32) * 0.02
        return {'x': x, 'w_gate': w_gate, 'w_up': w_up, 'w_down': w_down}
    _L0_ffn_all = _L0_ffn_setup()
    _L0_ffn_in = {k: v for k, v in _L0_ffn_all.items() if k in ('w_gate', 'w_up', 'w_down')}
    del _L0_ffn_all

    def _L1_cond_setup():
        import jax, jax.numpy as jnp
        import numpy as np
        B, T, D_IN, V_IN, E = (64, 128, 256, 256, 256)
        key = jax.random.key(seed)
        ks = jax.random.split(key, 16)
        s = 0.01
        return {'video': jax.random.normal(ks[0], (B, V_IN), jnp.float32), 'seq': jax.random.normal(ks[1], (B, T, D_IN), jnp.float32), 'W_z': jax.random.normal(ks[2], (D_IN, E), jnp.float32) * s, 'U_z': jax.random.normal(ks[3], (E, E), jnp.float32) * s, 'C_z': jax.random.normal(ks[4], (V_IN, E), jnp.float32) * s, 'b_z': jnp.zeros((E,), jnp.float32), 'W_r': jax.random.normal(ks[5], (D_IN, E), jnp.float32) * s, 'U_r': jax.random.normal(ks[6], (E, E), jnp.float32) * s, 'C_r': jax.random.normal(ks[7], (V_IN, E), jnp.float32) * s, 'b_r': jnp.zeros((E,), jnp.float32), 'W': jax.random.normal(ks[8], (D_IN, E), jnp.float32) * s, 'U': jax.random.normal(ks[9], (E, E), jnp.float32) * s, 'C': jax.random.normal(ks[10], (V_IN, E), jnp.float32) * s, 'b': jnp.zeros((E,), jnp.float32)}
    _L1_cond_all = _L1_cond_setup()
    _L1_cond_in = {k: v for k, v in _L1_cond_all.items() if k in ('W_z', 'U_z', 'C_z', 'b_z', 'W_r', 'U_r', 'C_r', 'b_r', 'W', 'U', 'C', 'b')}
    del _L1_cond_all

    def _L1_ffn_setup():
        import jax, jax.numpy as jnp
        import numpy as np
        N_EXP = 8
        TOP_K = 2
        CAPACITY_FACTOR = 1.25
        key = jax.random.key(seed)
        ks = jax.random.split(key, 5)
        B, T, D = (4, 256, 256)
        H = 4 * D
        E = N_EXP
        x = jax.random.normal(ks[0], (B, T, D), jnp.float32)
        gate_w = jax.random.normal(ks[1], (D, E), jnp.float32) * 0.02
        c_fc = jax.random.normal(ks[2], (E, D, H), jnp.float32) * 0.02
        fc_bias = jnp.zeros((E, 1, H), jnp.float32)
        c_proj = jax.random.normal(ks[3], (E, H, D), jnp.float32) * 0.02
        proj_bias = jnp.zeros((E, 1, D), jnp.float32)
        return dict(x=x, gate_w=gate_w, c_fc=c_fc, fc_bias=fc_bias, c_proj=c_proj, proj_bias=proj_bias)
    _L1_ffn_all = _L1_ffn_setup()
    _L1_ffn_in = {k: v for k, v in _L1_ffn_all.items() if k in ('gate_w', 'c_fc', 'fc_bias', 'c_proj', 'proj_bias')}
    del _L1_ffn_all
    return {'x': x, 'cond_1024': cond_1024, 'L0_cond_weight_matrix': _L0_cond_in['weight_matrix'], 'L0_cond_W_proj': _L0_cond_in['W_proj'], 'L0_cond_b_proj': _L0_cond_in['b_proj'], 'L0_ffn_w_gate': _L0_ffn_in['w_gate'], 'L0_ffn_w_up': _L0_ffn_in['w_up'], 'L0_ffn_w_down': _L0_ffn_in['w_down'], 'L1_cond_W_z': _L1_cond_in['W_z'], 'L1_cond_U_z': _L1_cond_in['U_z'], 'L1_cond_C_z': _L1_cond_in['C_z'], 'L1_cond_b_z': _L1_cond_in['b_z'], 'L1_cond_W_r': _L1_cond_in['W_r'], 'L1_cond_U_r': _L1_cond_in['U_r'], 'L1_cond_C_r': _L1_cond_in['C_r'], 'L1_cond_b_r': _L1_cond_in['b_r'], 'L1_cond_W': _L1_cond_in['W'], 'L1_cond_U': _L1_cond_in['U'], 'L1_cond_C': _L1_cond_in['C'], 'L1_cond_b': _L1_cond_in['b'], 'L1_ffn_gate_w': _L1_ffn_in['gate_w'], 'L1_ffn_c_fc': _L1_ffn_in['c_fc'], 'L1_ffn_fc_bias': _L1_ffn_in['fc_bias'], 'L1_ffn_c_proj': _L1_ffn_in['c_proj'], 'L1_ffn_proj_bias': _L1_ffn_in['proj_bias']}

def reference(x, cond_1024, L0_cond_weight_matrix, L0_cond_W_proj, L0_cond_b_proj, L0_ffn_w_gate, L0_ffn_w_up, L0_ffn_w_down, L1_cond_W_z, L1_cond_U_z, L1_cond_C_z, L1_cond_b_z, L1_cond_W_r, L1_cond_U_r, L1_cond_C_r, L1_cond_b_r, L1_cond_W, L1_cond_U, L1_cond_C, L1_cond_b, L1_ffn_gate_w, L1_ffn_c_fc, L1_ffn_fc_bias, L1_ffn_c_proj, L1_ffn_proj_bias):
    import jax
    import jax.numpy as jnp

    def _L0_cond_ref(encoded_utterance, element_embeddings, weight_matrix, W_proj, b_proj):
        import jax, jax.numpy as jnp
        import numpy as np
        B, N, D, C = (32, 64, 256, 256)
        u = jax.nn.gelu(encoded_utterance @ W_proj + b_proj, approximate=False)
        W_u, W_e = (weight_matrix[:D], weight_matrix[D:])
        logits = (u @ W_u)[:, None, :] + jnp.einsum('bnd,dc->bnc', element_embeddings, W_e)
        return logits

    def _L0_ffn_ref(x, w_gate, w_up, w_down):
        import jax, jax.numpy as jnp
        import numpy as np
        BLOCK = 32
        W_BITS = 4
        ACT_BITS = 16

        def act_qdq(x):
            qmax = 2.0 ** (ACT_BITS - 1) - 1.0
            scale = jnp.maximum(jnp.max(jnp.abs(x)) / qmax, 1e-12)
            return jnp.clip(jnp.round(x / scale), -qmax - 1.0, qmax) * scale

        def fixed_qdq_u16(x):
            scale = 1.0 / 65536.0
            return jnp.clip(jnp.round(x / scale), 0.0, 65535.0) * scale

        def lpbq_dequant(w):
            O, I = w.shape
            qmax = 2.0 ** (W_BITS - 1) - 1.0
            wb = w.reshape(O, I // BLOCK, BLOCK)
            s = jnp.maximum(jnp.max(jnp.abs(wb), axis=-1, keepdims=True) / qmax, 1e-12)
            wq = jnp.clip(jnp.round(wb / s), -qmax - 1.0, qmax) * s
            return wq.reshape(O, I)
        x = act_qdq(x)
        up = act_qdq(x @ lpbq_dequant(w_up).T)
        gate = act_qdq(x @ lpbq_dequant(w_gate).T)
        sig = fixed_qdq_u16(jax.nn.sigmoid(gate))
        gate = act_qdq(gate * sig)
        o = act_qdq(gate * up)
        return o @ lpbq_dequant(w_down).T

    def _L1_cond_ref(video, seq, W_z, U_z, C_z, b_z, W_r, U_r, C_r, b_r, W, U, C, b):
        import jax, jax.numpy as jnp
        import numpy as np
        B, T, D_IN, V_IN, E = (64, 128, 256, 256, 256)
        vz = video @ C_z + b_z
        vr = video @ C_r + b_r
        vh = video @ C + b
        xz = jnp.einsum('btd,de->bte', seq, W_z)
        xr = jnp.einsum('btd,de->bte', seq, W_r)
        xh = jnp.einsum('btd,de->bte', seq, W)

        def step(h, xs):
            xzt, xrt, xht = xs
            z = jax.nn.sigmoid(xzt + h @ U_z + vz)
            r = jax.nn.sigmoid(xrt + h @ U_r + vr)
            hh = jnp.tanh(xht + r * h @ U + vh)
            h_new = (1.0 - z) * h + z * hh
            return (h_new, h_new)
        h0 = jnp.zeros((seq.shape[0], U.shape[0]), seq.dtype)
        xs = (jnp.swapaxes(xz, 0, 1), jnp.swapaxes(xr, 0, 1), jnp.swapaxes(xh, 0, 1))
        _, out_t = jax.lax.scan(step, h0, xs)
        return jnp.swapaxes(out_t, 0, 1)

    def _L1_ffn_ref(x, gate_w, c_fc, fc_bias, c_proj, proj_bias):
        import jax, jax.numpy as jnp
        import numpy as np
        N_EXP = 8
        TOP_K = 2
        CAPACITY_FACTOR = 1.25
        B, T, D = x.shape
        n = B * T
        E, k = (N_EXP, TOP_K)
        cap = int(CAPACITY_FACTOR * n * k / E)
        xt = x.reshape(n, D)
        logits = xt @ gate_w
        top_logits, top_idx = jax.lax.top_k(logits, k)
        masked = jnp.full_like(logits, -jnp.inf)
        masked = masked.at[jnp.arange(n)[:, None], top_idx].set(top_logits)
        router_probs = jax.nn.softmax(masked, axis=-1)
        exp_mask = jax.nn.one_hot(top_idx, E, dtype=jnp.int32)
        exp_mask = jnp.transpose(exp_mask, (1, 0, 2))
        exp_rank = jnp.cumsum(exp_mask.reshape(k * n, E), axis=0) - 1
        exp_rank = exp_rank.reshape(k, n, E)
        exp_mask = exp_mask * (exp_rank < cap).astype(jnp.int32)
        used_capacity = jnp.sum(exp_mask, axis=(0, 1))
        exp_rank = jnp.sum(exp_mask * exp_rank, axis=-1)
        exp_weights = exp_mask.astype(x.dtype) * router_probs[None]
        rank_oh = jax.nn.one_hot(exp_rank, cap, dtype=x.dtype)
        cb_weight = jnp.einsum('kne,knc->nec', exp_weights, rank_oh)
        sec_mask = (cb_weight != 0).astype(x.dtype)
        exp_batches = jnp.einsum('nec,nd->ecd', sec_mask, xt)
        h = jnp.einsum('ecd,edh->ech', exp_batches, c_fc) + fc_bias
        h = jax.nn.gelu(h, approximate=False)
        exp_out = jnp.einsum('ech,ehd->ecd', h, c_proj) + proj_bias
        out = jnp.einsum('nec,ecd->nd', cb_weight, exp_out)
        return out.reshape(B, T, D)
    x = x + _L0_ffn_ref(_L0_cond_ref(cond_1024, x, L0_cond_weight_matrix, L0_cond_W_proj, L0_cond_b_proj), L0_ffn_w_gate, L0_ffn_w_up, L0_ffn_w_down)
    x = x + _L1_ffn_ref(_L1_cond_ref(cond_1024, x, L1_cond_W_z, L1_cond_U_z, L1_cond_C_z, L1_cond_b_z, L1_cond_W_r, L1_cond_U_r, L1_cond_C_r, L1_cond_b_r, L1_cond_W, L1_cond_U, L1_cond_C, L1_cond_b), L1_ffn_gate_w, L1_ffn_c_fc, L1_ffn_fc_bias, L1_ffn_c_proj, L1_ffn_proj_bias)
    return x

_drawn_inputs = setup_inputs


def setup_inputs(seed=0):
    import zlib

    import numpy as np

    out = dict(_drawn_inputs(seed))
    spreads = {'L0_cond_b_proj': (0.0, 0.8),
     'L1_cond_b_z': (0.0, 0.635),
     'L1_cond_b_r': (0.0, 0.8),
     'L1_cond_b': (0.0, 0.1),
     'L1_ffn_fc_bias': (0.0, 0.388),
     'L1_ffn_proj_bias': (0.0, 0.1)}
    factors = {'L1_cond_W_z': 3.929,
     'L1_cond_U_z': 8.0,
     'L1_cond_C_z': 4.147,
     'L1_cond_W_r': 8.0,
     'L1_cond_U_r': 23.522,
     'L1_cond_C_r': 8.0,
     'L1_cond_U': 2.807,
     'L1_ffn_c_fc': 4.359}
    for name, (base, spread) in spreads.items():
        noise = np.random.default_rng([zlib.crc32(name.encode()), seed]).standard_normal(out[name].shape)
        drawn = base * np.exp(spread * noise) if base else spread * noise
        out[name] = jnp.asarray(drawn.astype(out[name].dtype))
    for name, factor in factors.items():
        out[name] = (out[name] * factor).astype(out[name].dtype)
    return out
```

```python
from contextlib import ExitStack

import numpy as np

import concourse.bass as bass
from concourse import mybir

F32 = mybir.dt.float32
F16 = mybir.dt.float16
I16 = mybir.dt.int16
U16 = mybir.dt.uint16
U32 = mybir.dt.uint32
ALU = mybir.AluOpType
ACT = mybir.ActivationFunctionType
X = mybir.AxisListType.X

P = 128
BATCH, STEPS, D = 16, 256, 256
N = BATCH * STEPS
K = D // P
F = 768
FO = F // P
BLK = 512
NB = N // BLK
NT = N // P
QBLOCK = 32
WCOLS = 3 * K * F
E, TOPK = 8, 2
H = 4 * D
HM = H // P
CAP = int(1.25 * N * TOPK / E)
CT = CAP // P
SLOT_TILES = E * CT
QMAX = 32767.0
TINY = 1e-12
SC = 256.0
INV2 = 1.0 / (SC * SC)
TILE_STEPS = P // BATCH
ROW = 2 * D + 2 * E
DUMMY = P

C_ID, C_BLESS, C_BSAME, C_TLESS, C_IOTA, C_EIDX, C_EOFF, C_TILE, C_P1, C_DUM, C_END = np.cumsum(
    [0, P, P, P, P, P, E, E, NT, 1, 1])


def constants():
    c = np.zeros((P, C_END), np.float32)
    p = np.arange(P)
    b, t = p % BATCH, p // BATCH
    c[:, C_ID:C_ID + P] = np.eye(P)
    c[:, C_BLESS:C_BLESS + P] = b[:, None] < b[None, :]
    c[:, C_BSAME:C_BSAME + P] = b[:, None] == b[None, :]
    c[:, C_TLESS:C_TLESS + P] = (b[:, None] == b[None, :]) & (t[:, None] < t[None, :])
    c[:, C_IOTA:C_IOTA + P] = p[None, :]
    c[:, C_EIDX:C_EIDX + E] = E - np.arange(E)
    c[:, C_EOFF:C_EOFF + E] = CAP * np.arange(E)
    c[:, C_TILE:C_TILE + NT] = np.arange(NT)
    c[:, C_P1] = p + 1
    c[:, C_DUM] = N + 1 + p
    return c


class Chain:

    def __init__(self, eng, sem, base=0):
        self.eng, self.sem, self.base, self.n = eng, sem, base, 0

    def link(self, ins):
        ins.then_inc(self.sem, 1)
        self.n += 1

    def wait(self):
        self.eng.wait_ge(self.sem, self.base + self.n)

    def step(self, ins):
        self.link(ins)
        self.wait()


class Space:

    def __init__(self, nc, ctx, tag):
        self.nc, self.ctx, self.tag = nc, ctx, tag

    def sb(self, name, shape, dt):
        return self.ctx.enter_context(self.nc.sbuf_tensor(f"{self.tag}_{name}", shape, dt))

    def ps(self, name, shape, dt=F32):
        return self.ctx.enter_context(self.nc.psum_tensor(f"{self.tag}_ps_{name}", shape, dt))

    def sem(self, name):
        return self.ctx.enter_context(self.nc.semaphore(f"{self.tag}_{name}"))


def pair_products(wh, wl, xh, xl):
    return ((wh, xh), (wl, xh), (wh, xl))


def stage_logits(nc, a, keep):
    x0h, x0l, wTh, wTl, scal, cst = keep["x0h"], keep["x0l"], keep["wTh"], keep["wTl"], keep["scal"], keep["cst"]
    with ExitStack() as ctx:
        s = Space(nc, ctx, "lg")
        condT = s.sb("condT", [P, K, BATCH], F32)
        wcond = s.sb("wcond", [P, 2 * K, D], F32)
        wproj = s.sb("wproj", [P, K, D], F32)
        bproj = s.sb("bproj", [P, K], F32)
        uT = s.sb("uT", [P, K, BATCH], F32)
        vT = s.sb("vT", [P, K, BATCH], F32)
        xin = s.sb("xin", [P, 2, K, BLK], F32)
        L = s.sb("L", [P, K, N], F32)
        wraw = s.sb("wraw", [P, WCOLS], F32)
        wint = s.sb("wint", [P, WCOLS], I16)
        wscale = s.sb("wscale", [P, 4, WCOLS // QBLOCK], F32)
        blkmax = s.sb("blkmax", [P, NB], F32)
        allmax = s.sb("allmax", [P, 2], F32)
        q = s.sb("q", [P, K, BLK], I16)
        ps_set = s.ps("set", [P, BLK])
        ps_L = [[s.ps(f"ps_L{p}{m}", [P, BLK]) for m in range(K)] for p in range(2)]
        ps_w = [s.ps(f"ps_w{i}", [P, BLK]) for i in range(2)]
        d_small, d_w = s.sem("d_small"), s.sem("d_w")
        d_x = [s.sem(f"d_x{i}") for i in range(2)]
        u_mm, u_done, v_mm, v_done = s.sem("u_mm"), s.sem("u_done"), s.sem("v_mm"), s.sem("v_done")
        L_mm, L_read, dq, w_deq = s.sem("L_mm"), s.sem("L_read"), s.sem("dq"), s.sem("w_deq")
        w_tr, w_hi, w_lo = s.sem("w_tr"), s.sem("w_hi"), s.sem("w_lo")
        mx_own, mx_all, sc_own, sc_done = s.sem("mx_own"), s.sem("mx_all"), s.sem("sc_own"), s.sem("sc_done")
        q_done, hi_done, lo_done, pad = s.sem("q_done"), s.sem("hi_done"), s.sem("lo_done"), s.sem("pad")
        NG = WCOLS // BLK

        def source(n):
            if n < 2 * K * FO:
                mat, k, o = n // (K * FO), n % (K * FO) // FO, n % FO
                return (mat * FO + o) * D + k * P
            k, o = (n - 2 * K * FO) // K, n % K
            return 2 * FO * D + o * F + k * P

        with nc.Block() as block:
            @block.sync
            def _(sp):
                sp.dma_start(cst[:], a["consts"]).then_inc(d_small, 16)
                sp.dma_start(condT[:], a["condT"].rearrange("(k p) b -> p k b", p=P)).then_inc(d_small, 16)
                sp.dma_start(wproj[:], a["W_proj"].rearrange("(k p) n -> p k n", p=P)).then_inc(d_small, 16)
                sp.dma_start(wcond[:], a["weight_matrix"].rearrange("(k p) n -> p k n", p=P)).then_inc(d_small, 16)
                sp.dma_start(bproj[:], a["b_proj"]).then_inc(d_small, 16)
                xT = a["xT"].rearrange("(k p) n -> p k n", p=P)
                with sp.Fori(0, NB // 2) as i:
                    for par in range(2):
                        sp.wait_ge(L_mm, 2 * i + par + 1)
                        sp.dma_start(xin[:, par], xT[:, :, bass.ds((2 * i + par) * BLK, BLK)]).then_inc(d_x[par], 16)

            @block.scalar
            def _(act):
                up = wraw[:, 0:FO * D].rearrange("p (o n) -> p o n", o=FO)
                gate = wraw[:, FO * D:2 * FO * D].rearrange("p (o n) -> p o n", o=FO)
                down = wraw[:, 2 * FO * D:].rearrange("p (o n) -> p o n", o=K)
                act.dma_start(up, a["w_up"].rearrange("(o p) n -> p o n", p=P)).then_inc(d_w, 16)
                act.dma_start(gate, a["w_gate"].rearrange("(o p) n -> p o n", p=P)).then_inc(d_w, 16)
                act.dma_start(down, a["w_down"].rearrange("(o p) n -> p o n", p=P)).then_inc(d_w, 16)
                act.wait_ge(u_mm, 1)
                for m in range(K):
                    act.activation(uT[:, m], ps_set[:, m * BATCH:(m + 1) * BATCH], ACT.Gelu,
                                   bias=bproj[:, m:m + 1]).then_inc(u_done, 1)
                act.wait_ge(v_mm, 1)
                act.activation(vT[:], ps_set[:, K * BATCH:2 * K * BATCH], ACT.Copy).then_inc(v_done, 1)
                for g in range(NG):
                    act.wait_ge(w_tr, g + 1)
                    act.activation(wTh[:, g * BLK:(g + 1) * BLK], ps_w[g % 2][:], ACT.Copy).then_inc(w_hi, 1)
                with act.Fori(0, NB) as j:
                    act.wait_ge(q_done, j + 1)
                    act.activation(x0h[:, :, bass.ds(j * BLK, BLK)], q[:],
                                   ACT.Copy).then_inc(hi_done, 1)

            @block.tensor
            def _(pe):
                pe.wait_ge(d_small, 80)
                for m in range(K):
                    for k in range(K):
                        i = pe.matmul(ps_set[:, m * BATCH:(m + 1) * BATCH], wproj[:, k, m * P:(m + 1) * P], condT[:, k],
                                      start=(k == 0), stop=(k == K - 1))
                i.then_inc(u_mm, 1)
                pe.wait_ge(u_done, K)
                for m in range(K):
                    for k in range(K):
                        c0 = (K + m) * BATCH
                        i = pe.matmul(ps_set[:, c0:c0 + BATCH], wcond[:, k, m * P:(m + 1) * P], uT[:, k],
                                      start=(k == 0), stop=(k == K - 1))
                i.then_inc(v_mm, 1)
                pe.sem_inc(L_mm, 2)
                with pe.Fori(0, NB // 2) as i2:
                    for par in range(2):
                        pe.wait_ge(d_x[par], 16 * i2 + 16)
                        pe.wait_ge(L_read, 2 * i2 + par + 1)
                        for m in range(K):
                            for k in range(K):
                                i = pe.matmul(ps_L[par][m][:], wcond[:, K + k, m * P:(m + 1) * P], xin[:, par, k],
                                              start=(k == 0), stop=(k == K - 1))
                        i.then_inc(L_mm, 1)
                pe.wait_ge(w_deq, 1)
                for g in range(NG):
                    if g >= 2:
                        pe.wait_ge(w_lo, g - 1)
                    for n in range(4):
                        c0 = source(4 * g + n)
                        i = pe.transpose(ps_w[g % 2][:, n * P:(n + 1) * P], wraw[:, c0:c0 + P], cst[:, C_ID:C_ID + P])
                    i.then_inc(w_tr, 1)

            @block.gpsimd
            def _(pool):
                pool.memset(x0h[:, :, N:N + P], 0.0).then_inc(pad, 1)
                pool.memset(x0l[:, :, N:N + P], 0.0).then_inc(pad, 1)
                pool.wait_ge(mx_own, 1)
                pool.partition_all_reduce(allmax[:, 1:2], allmax[:, 0:1], P, bass.bass_isa.ReduceOp.max).then_inc(mx_all, 1)
                pool.wait_ge(pad, 2)

            @block.vector
            def _(dve):
                c = Chain(dve, dq)
                dve.sem_inc(L_read, 2)
                dve.wait_ge(d_w, 48)
                w3 = wraw[:].rearrange("p (g n) -> p g n", n=QBLOCK)
                i3 = wint[:].rearrange("p (g n) -> p g n", n=QBLOCK)
                wide = [P, WCOLS // QBLOCK, QBLOCK]
                c.step(dve.tensor_reduce(wscale[:, 0], w3, X, ALU.max, apply_absolute_value=True))
                c.step(dve.tensor_scalar(wscale[:, 1], wscale[:, 0], 1.0 / 7.0, TINY, ALU.mult, ALU.max))
                c.step(dve.reciprocal(wscale[:, 2], wscale[:, 1]))
                c.step(dve.tensor_scalar(wscale[:, 3], wscale[:, 1], SC, None, ALU.mult))
                c.step(dve.tensor_tensor(w3, w3, wscale[:, 2].unsqueeze(2).to_broadcast(wide), ALU.mult))
                c.step(dve.tensor_scalar(wint[:], wraw[:], 7.0, -8.0, ALU.min, ALU.max))
                dve.tensor_tensor(w3, i3, wscale[:, 3].unsqueeze(2).to_broadcast(wide), ALU.mult).then_inc(w_deq, 1)
                dve.wait_ge(v_done, 1)
                with dve.Fori(0, NB // 2) as i2:
                    for par in range(2):
                        j = 2 * i2 + par
                        dve.wait_ge(L_mm, j + 3)
                        for m in range(K):
                            out = L[:, m, bass.ds(j * BLK, BLK)].rearrange("p (t b) -> p t b", b=BATCH)
                            o = dve.tensor_tensor(out, ps_L[par][m][:].rearrange("p (t b) -> p t b", b=BATCH),
                                                  vT[:, m].unsqueeze(1).to_broadcast([P, BLK // BATCH, BATCH]), ALU.add)
                        o.then_inc(L_read, 1)
                        dve.wait_ge(L_read, j + 3)
                        dve.tensor_reduce(blkmax[:, bass.ds(j, 1)], L[:, :, bass.ds(j * BLK, BLK)], mybir.AxisListType.XY, ALU.max,
                                          apply_absolute_value=True).then_inc(sc_own, 1)
                for g in range(NG):
                    dve.wait_ge(w_hi, g + 1)
                    dve.tensor_tensor(wTl[:, g * BLK:(g + 1) * BLK], ps_w[g % 2][:], wTh[:, g * BLK:(g + 1) * BLK],
                                      ALU.subtract).then_inc(w_lo, 1)
                dve.wait_ge(sc_own, NB)
                dve.tensor_reduce(allmax[:, 0:1], blkmax[:], X, ALU.max).then_inc(mx_own, 1)
                dve.wait_ge(mx_all, 1)
                c = Chain(dve, sc_done)
                c.step(dve.tensor_scalar(scal[:, S_X:S_X + 1], allmax[:, 1:2], 1.0 / QMAX, TINY, ALU.mult, ALU.max))
                c.step(dve.reciprocal(scal[:, S_TMP:S_TMP + 1], scal[:, S_X:S_X + 1]))
                dve.sem_inc(lo_done, 1)
                with dve.Fori(0, NB) as j:
                    dve.wait_ge(lo_done, j + 1)
                    dve.tensor_scalar(q[:], L[:, :, bass.ds(j * BLK, BLK)], scal[:, S_TMP:S_TMP + 1], QMAX, ALU.mult,
                                      ALU.min).then_inc(q_done, 1)
                    dve.wait_ge(hi_done, j + 1)
                    dve.tensor_tensor(x0l[:, :, bass.ds(j * BLK, BLK)], q[:], x0h[:, :, bass.ds(j * BLK, BLK)],
                                      ALU.subtract).then_inc(lo_done, 1)


(S_X, S_TMP, S_PU, S_PG, S_UP, S_GATE, S_CUP, S_CGATE, S_G2, S_C2, S_O, S_CO, S_XU, S_ALLU, S_ALLG, S_US2, S_DN, S_R, S_G65,
 S_MXA, S_MXB, S_END) = range(22)


def column(scal, n):
    return scal[:, n:n + 1]


def stage_gate_up(nc, a, keep):
    x0h, x0l, wTh, wTl, scal = keep["x0h"], keep["x0l"], keep["wTh"], keep["wTl"], keep["scal"]
    qup, R = keep["qup"], keep["R"]
    RING = 6
    with ExitStack() as ctx:
        s = Space(nc, ctx, "gu")
        unitmax = s.sb("unitmax", [P, 2, NB, FO], F32)
        rmax = s.sb("rmax", [P, NB * FO], F32)
        gq = [s.sb(f"gq{i}", [P, BLK], I16) for i in range(2)]
        sg = [s.sb(f"sg{i}", [P, BLK], F32) for i in range(2)]
        sq = [s.sb(f"sq{i}", [P, BLK], U16) for i in range(2)]
        ps = [s.ps(f"p{i}", [P, BLK]) for i in range(RING)]
        mm0, rd_up, rd_gate, mm1, rd1 = s.sem("mm0"), s.sem("rd_up"), s.sem("rd_gate"), s.sem("mm1"), s.sem("rd1")
        upmax, own_max, all_max = s.sem("upmax"), s.sem("own_max"), s.sem("all_max")
        v_sc, sc_ready, sig_done, R_done, rm, sq_done, r_all, up_int = (
            s.sem(n) for n in ("v_sc", "sc_ready", "sig_done", "R_done", "rm", "sq_done", "r_all", "up_int"))

        def unit(pe, j, mat, o, bank, done):
            n = 0
            cols = bass.ds(j * BLK, BLK)
            for k in range(K):
                w0 = (mat * K + k) * F + o * P
                for w, x in pair_products(wTh[:, w0:w0 + P], wTl[:, w0:w0 + P], x0h[:, k, cols], x0l[:, k, cols]):
                    ins = pe.matmul(ps[bank][:], w, x, start=(n == 0), stop=(n == 3 * K - 1))
                    n += 1
            ins.then_inc(done, 1)

        with nc.Block() as block:
            @block.tensor
            def _(pe):
                with pe.Fori(0, NB) as j:
                    for o in range(FO):
                        pe.wait_ge(rd_up, FO * j + o + 1)
                        unit(pe, j, 0, o, 2 * o % RING, mm0)
                        pe.wait_ge(rd_gate, FO * j + o + 1)
                        unit(pe, j, 1, o, (2 * o + 1) % RING, mm0)
                pe.wait_ge(rd_up, NB * FO + RING // 2)
                pe.wait_ge(rd_gate, NB * FO + RING // 2)
                with pe.Fori(0, NB) as j:
                    for o in range(FO):
                        pe.wait_ge(rd1, FO * j + o + 1)
                        unit(pe, j, 1, o, o, mm1)

            @block.gpsimd
            def _(pool):
                pool.wait_ge(own_max, 1)
                pool.partition_all_reduce(scal[:, S_ALLU:S_ALLG + 1], scal[:, S_PU:S_PG + 1], P,
                                          bass.bass_isa.ReduceOp.max).then_inc(all_max, 1)
                pool.wait_ge(r_all, 1)
                pool.partition_all_reduce(column(scal, S_MXB), column(scal, S_MXA), P,
                                          bass.bass_isa.ReduceOp.max).then_inc(all_max, 1)

            @block.scalar
            def _(act):
                act.sem_inc(rd_up, RING // 2)
                act.sem_inc(rd1, RING)
                with act.Fori(0, NB) as j:
                    for o in range(FO):
                        act.wait_ge(mm0, 2 * (FO * j + o) + 1)
                        act.activation(R[:, o, bass.ds(j * BLK, BLK)], ps[2 * o % RING][:], ACT.Copy).then_inc(rd_up, 1)
                act.wait_ge(sc_ready, 1)
                with act.Fori(0, NB) as j:
                    cols = bass.ds(j * BLK, BLK)
                    act.activation(qup[:, 0:FO // 2, cols], R[:, 0:FO // 2, cols], ACT.Copy, scale=column(scal, S_CUP)).then_inc(up_int, 1)
                    for o in range(FO):
                        g = o % 2
                        act.wait_ge(mm1, FO * j + o + 1)
                        act.wait_ge(R_done, FO * j + o + 1)
                        act.activation(gq[g][:], ps[o][:], ACT.Copy, scale=column(scal, S_CGATE)).then_inc(rd1, 1)
                        act.wait_ge(rd1, FO * j + o + RING + 1)
                        act.activation(sg[g][:], gq[g][:], ACT.Sigmoid, scale=column(scal, S_GATE)).then_inc(sig_done, 1)

            @block.vector
            def _(dve):
                dve.sem_inc(rd_gate, RING // 2)
                dve.sem_inc(R_done, 2)
                with dve.Fori(0, NB) as j:
                    for o in range(FO):
                        dve.wait_ge(rd_up, FO * j + o + 1 + RING // 2)
                        dve.tensor_reduce(unitmax[:, 0, bass.ds(j, 1), o:o + 1], R[:, o, bass.ds(j * BLK, BLK)], X, ALU.max,
                                          apply_absolute_value=True).then_inc(upmax, 1)
                        dve.wait_ge(mm0, 2 * (FO * j + o) + 2)
                        dve.tensor_reduce(unitmax[:, 1, bass.ds(j, 1), o:o + 1], ps[(2 * o + 1) % RING][:], X, ALU.max,
                                          apply_absolute_value=True).then_inc(rd_gate, 1)
                dve.wait_ge(upmax, NB * FO)
                dve.wait_ge(rd_gate, RING // 2 + NB * FO)
                dve.tensor_reduce(scal[:, S_PU:S_PG + 1], unitmax[:], mybir.AxisListType.XY, ALU.max).then_inc(own_max, 1)
                dve.wait_ge(all_max, 1)
                c = Chain(dve, v_sc)
                c.step(dve.tensor_scalar(column(scal, S_XU), column(scal, S_X), 1.0 / SC, None, ALU.mult))
                c.step(dve.tensor_scalar(scal[:, S_UP:S_GATE + 1], scal[:, S_ALLU:S_ALLG + 1], column(scal, S_XU), 1.0 / QMAX,
                                         ALU.mult, ALU.mult))
                c.step(dve.tensor_scalar(scal[:, S_UP:S_GATE + 1], scal[:, S_UP:S_GATE + 1], TINY, None, ALU.max))
                c.step(dve.reciprocal(scal[:, S_CUP:S_CGATE + 1], scal[:, S_UP:S_GATE + 1]))
                c.step(dve.tensor_scalar(scal[:, S_CUP:S_CGATE + 1], scal[:, S_CUP:S_CGATE + 1], column(scal, S_XU), None, ALU.mult))
                dve.tensor_scalar(column(scal, S_G65), column(scal, S_GATE), 1.0 / 65536.0, None, ALU.mult).then_inc(sc_ready, 1)
                dve.wait_ge(sc_ready, 1)
                with dve.Fori(0, NB) as j:
                    cols = bass.ds(j * BLK, BLK)
                    dve.tensor_scalar(qup[:, FO // 2:FO, cols], R[:, FO // 2:FO, cols], column(scal, S_CUP), QMAX, ALU.mult, ALU.min)
                    for o in range(FO):
                        g = o % 2
                        n = FO * j + o
                        dve.wait_ge(sig_done, n + 1)
                        dve.tensor_scalar(sq[g][:], sg[g][:], 65536.0, 65535.0, ALU.mult, ALU.min).then_inc(sq_done, 1)
                        if o == 0:
                            dve.wait_ge(up_int, j + 1)
                        dve.wait_ge(sq_done, n + 1)
                        dve.tensor_tensor(R[:, o, cols], gq[g][:], sq[g][:], ALU.mult).then_inc(R_done, 1)
                        dve.wait_ge(R_done, n + 3)
                        dve.tensor_reduce(rmax[:, bass.ds(n, 1)], R[:, o, cols], X, ALU.max, apply_absolute_value=True).then_inc(rm, 1)
                dve.wait_ge(rm, NB * FO)
                dve.tensor_reduce(column(scal, S_MXA), rmax[:], X, ALU.max).then_inc(r_all, 1)
                dve.wait_ge(all_max, 2)
                c.step(dve.tensor_scalar(column(scal, S_G2), column(scal, S_MXB), column(scal, S_G65), 1.0 / QMAX, ALU.mult, ALU.mult))
                c.step(dve.tensor_scalar(column(scal, S_G2), column(scal, S_G2), TINY, None, ALU.max))
                c.step(dve.reciprocal(column(scal, S_R), column(scal, S_G2)))
                c.step(dve.tensor_tensor(column(scal, S_C2), column(scal, S_R), column(scal, S_G65), ALU.mult))
                c.step(dve.tensor_tensor(column(scal, S_US2), column(scal, S_G2), column(scal, S_UP), ALU.mult))


def stage_product(nc, a, keep):
    scal, qup, R = keep["scal"], keep["qup"], keep["R"]
    PIECE = 1536
    NP = FO * N // PIECE
    with ExitStack() as ctx:
        s = Space(nc, ctx, "pr")
        q2 = [s.sb(f"q2{i}", [P, PIECE], I16) for i in range(2)]
        pmax = s.sb("pmax", [P, NP], F32)
        q2_done, p_done, pm, all_own, all_max, v_sc = (s.sem(n) for n in ("q2_done", "p_done", "pm", "all_own", "all_max", "v_sc"))
        Rf = R[:].rearrange("p o n -> p (o n)")
        uf = qup[:].rearrange("p o n -> p (o n)")
        with nc.Block() as block:
            @block.scalar
            def _(act):
                with act.Fori(0, NP // 2) as i:
                    for par in range(2):
                        n = 2 * i + par
                        act.wait_ge(p_done, n + 1)
                        act.activation(q2[par][:], Rf[:, bass.ds(n * PIECE, PIECE)], ACT.Copy,
                                       scale=column(scal, S_C2)).then_inc(q2_done, 1)

            @block.gpsimd
            def _(pool):
                pool.wait_ge(all_own, 1)
                pool.partition_all_reduce(column(scal, S_MXB), column(scal, S_MXA), P,
                                          bass.bass_isa.ReduceOp.max).then_inc(all_max, 1)

            @block.vector
            def _(dve):
                dve.sem_inc(p_done, 2)
                with dve.Fori(0, NP // 2) as i:
                    for par in range(2):
                        n = 2 * i + par
                        cols = bass.ds(n * PIECE, PIECE)
                        dve.wait_ge(q2_done, n + 1)
                        dve.tensor_tensor(Rf[:, cols], q2[par][:], uf[:, cols], ALU.mult).then_inc(p_done, 1)
                        dve.wait_ge(p_done, n + 3)
                        dve.tensor_reduce(pmax[:, bass.ds(n, 1)], Rf[:, cols], X, ALU.max, apply_absolute_value=True).then_inc(pm, 1)
                dve.wait_ge(pm, NP)
                dve.tensor_reduce(column(scal, S_MXA), pmax[:], X, ALU.max).then_inc(all_own, 1)
                dve.wait_ge(all_max, 1)
                c = Chain(dve, v_sc)
                c.step(dve.tensor_scalar(column(scal, S_O), column(scal, S_MXB), column(scal, S_US2), 1.0 / QMAX, ALU.mult, ALU.mult))
                c.step(dve.tensor_scalar(column(scal, S_O), column(scal, S_O), TINY, None, ALU.max))
                c.step(dve.reciprocal(column(scal, S_R), column(scal, S_O)))
                c.step(dve.tensor_tensor(column(scal, S_CO), column(scal, S_R), column(scal, S_US2), ALU.mult))
                c.step(dve.tensor_scalar(column(scal, S_DN), column(scal, S_O), 1.0 / SC, None, ALU.mult))


def stage_down(nc, a, keep):
    x1h, x1l, wTh, wTl, scal, R, cst = (keep[n] for n in ("x0h", "x0l", "wTh", "wTl", "scal", "R", "cst"))
    D0 = 2 * K * F
    with ExitStack() as ctx:
        s = Space(nc, ctx, "dn")
        xin = [s.sb(f"xin{i}", [P, K, BLK], F32) for i in range(2)]
        qo = s.sb("qo", [P, FO, BLK], I16)
        qh = [s.sb(f"qh{i}", [P, FO, BLK], F16) for i in range(2)]
        ql = [s.sb(f"ql{i}", [P, FO, BLK], F16) for i in range(2)]
        x1 = [s.sb(f"x1{i}", [P, K, BLK], F32) for i in range(2)]
        rows = s.sb("rows", [P, 4, D], F32)
        ps_d = [[s.ps(f"d{p}{m}", [P, BLK]) for m in range(K)] for p in range(2)]
        ps_t = [s.ps(f"t{i}", [P, 2, D]) for i in range(2)]
        d_x = [s.sem(f"d_x{i}") for i in range(2)]
        d_out, stored = s.sem("d_out"), s.sem("stored")
        qo_done, qh_done, ql_done, mm, x1_done, hi_done, lo_done, tr, rows_done = (
            s.sem(n) for n in ("qo_done", "qh_done", "ql_done", "mm", "x1_done", "hi_done", "lo_done", "tr", "rows_done"))

        def blocks(eng, one):
            one(0, 0)
            with eng.Fori(0, (NB - 4) // 2) as i:
                one(2 * i + 1, 1)
                one(2 * i + 2, 0)
            for j in range(NB - 3, NB):
                one(j, j % 2)

        def before(j, n):
            return not isinstance(j, int) or j + n < NB

        with nc.Block() as block:
            @block.sync
            def _(sp):
                xT = a["xT"].rearrange("(k p) n -> p k n", p=P)
                sp.sem_inc(stored, 1)
                sp.dma_start(a["out"][N:N + DUMMY, :], cst[:, 0:D]).then_inc(d_out, 16)
                sp.wait_ge(d_out, 16)
                for par in range(2):
                    sp.dma_start(xin[par][:], xT[:, :, par * BLK:(par + 1) * BLK]).then_inc(d_x[par], 16)

                def one(j, par):
                    sp.wait_ge(rows_done, j + 2)
                    sp.dma_start(a["out"][bass.ds(j * BLK, BLK), :].rearrange("(c p) n -> p c n", p=P), rows[:]).then_inc(d_out, 16)
                    if before(j, 2):
                        sp.wait_ge(x1_done, j + 1)
                        sp.dma_start(xin[par][:], xT[:, :, bass.ds((j + 2) * BLK, BLK)]).then_inc(d_x[par], 16)
                    sp.wait_ge(d_out, 16 * j + 32)
                    sp.sem_inc(stored, 1)
                blocks(sp, one)

            @block.scalar
            def _(act):
                def integers(j):
                    act.wait_ge(ql_done, j + 1)
                    act.activation(qo[:], R[:, :, bass.ds(j * BLK, BLK)], ACT.Copy, scale=column(scal, S_CO)).then_inc(qo_done, 1)

                def rows_out(j):
                    act.wait_ge(tr, j + 2)
                    act.wait_ge(stored, j + 1)
                    for h in range(2):
                        r = act.activation(rows[:, 2 * h:2 * h + 2], ps_t[h][:], ACT.Copy)
                    r.then_inc(rows_done, 1)

                def one(j, par):
                    if before(j, 2):
                        integers(j + 2)
                    act.wait_ge(x1_done, j + 1)
                    act.activation(x1h[:, :, bass.ds(j * BLK, BLK)], x1[par][:], ACT.Copy, scale=SC).then_inc(hi_done, 1)
                    if not isinstance(j, int) or j > 0:
                        rows_out(j - 1)

                act.sem_inc(rows_done, 1)
                integers(0)
                integers(1)
                blocks(act, one)
                rows_out(NB - 1)

            @block.tensor
            def _(pe):
                def rows_back(j, par):
                    pe.wait_ge(x1_done, j + 1)
                    pe.wait_ge(rows_done, j + 1)
                    for c in range(4):
                        for k in range(K):
                            ins = pe.transpose(ps_t[c // 2][:, c % 2, k * P:(k + 1) * P], x1[par][:, k, c * P:(c + 1) * P],
                                               cst[:, C_ID:C_ID + P])
                    ins.then_inc(tr, 1)

                def one(j, par):
                    pe.wait_ge(ql_done, j + 2)
                    for m in range(K):
                        n = 0
                        for k in range(FO):
                            w0 = D0 + k * D + m * P
                            for w, x in pair_products(wTh[:, w0:w0 + P], wTl[:, w0:w0 + P], qh[par][:, k], ql[par][:, k]):
                                ins = pe.matmul(ps_d[par][m][:], w, x, start=(n == 0), stop=(n == 3 * FO - 1))
                                n += 1
                    ins.then_inc(mm, 1)
                    if not isinstance(j, int) or j > 0:
                        rows_back(j - 1, 1 - par)

                pe.sem_inc(mm, 1)
                pe.sem_inc(tr, 1)
                blocks(pe, one)
                rows_back(NB - 1, (NB - 1) % 2)

            @block.vector
            def _(dve):
                def split(j, par):
                    dve.wait_ge(qo_done, j + 1)
                    if not isinstance(j, int) or j > 0:
                        dve.wait_ge(mm, j)
                    dve.tensor_copy(qh[par][:], qo[:]).then_inc(qh_done, 1)
                    dve.wait_ge(qh_done, j + 1)
                    dve.tensor_tensor(ql[par][:], qo[:], qh[par][:], ALU.subtract).then_inc(ql_done, 1)

                def one(j, par):
                    if before(j, 1):
                        split(j + 1, 1 - par)
                    dve.wait_ge(mm, j + 2)
                    dve.wait_ge(d_x[par], 8 * (j - par) + 16)
                    dve.wait_ge(tr, j if not isinstance(j, int) else max(j, 1))
                    for m in range(K):
                        o = dve.scalar_tensor_tensor(out=x1[par][:, m], in0=ps_d[par][m][:], scalar=column(scal, S_DN),
                                                     in1=xin[par][:, m], op0=ALU.mult, op1=ALU.add)
                    o.then_inc(x1_done, 1)
                    dve.wait_ge(x1_done, j + 1)
                    dve.wait_ge(hi_done, j + 1)
                    dve.scalar_tensor_tensor(out=x1l[:, :, bass.ds(j * BLK, BLK)], in0=x1[par][:], scalar=SC,
                                             in1=x1h[:, :, bass.ds(j * BLK, BLK)], op0=ALU.mult, op1=ALU.subtract)\
                       .then_inc(lo_done, 1)

                dve.sem_inc(ql_done, 1)
                split(0, 0)
                blocks(dve, one)
                dve.wait_ge(lo_done, NB)


def stage_gru(nc, a, keep):
    x1h, x1l, cst, Lg = keep["x0h"], keep["x0l"], keep["cst"], keep["Lg"]
    table = keep["table"]
    G = 3
    R_, Z_, C_ = range(G)
    NC2 = NT // 2
    with ExitStack() as ctx:
        s = Space(nc, ctx, "gru")
        condT = s.sb("condT", [P, K, BATCH], F32)
        raw = s.sb("raw", [P, 2, G, K, D], F32)
        cond_w = s.sb("cond_w", [P, G, K, D], F32)
        bias = s.sb("bias", [P, G * K], F32)
        gwraw = s.sb("gwraw", [P, K, E], F32)
        wh, wl = s.sb("wh", [P, 2, G, K, D], F16), s.sb("wl", [P, 2, G, K, D], F16)
        gwh, gwl = s.sb("gwh", [P, K, E], F16), s.sb("gwl", [P, K, E], F16)
        idh, idsc = s.sb("idh", [P, P], F16), s.sb("idsc", [P, P], F16)
        vf = s.sb("vf", [P, G * K, BATCH], F32)
        vh, vl = s.sb("vh", [P, G * K, BATCH], F16), s.sb("vl", [P, G * K, BATCH], F16)
        xc = [s.sb(f"xc{p}", [P, 2, K, P], F16) for p in range(2)]
        hh = [s.sb(f"hh{p}", [P, K, P], F16) for p in range(2)]
        hl = [s.sb(f"hl{p}", [P, K, P], F16) for p in range(2)]
        Hf = s.sb("Hf", [P, K, BATCH], F32)
        r, z, th, rv, zc, av, mv = (s.sb(n, [P, K, BATCH], F32) for n in ("r", "z", "th", "rv", "zc", "av", "mv"))
        rhh, rhl = s.sb("rhh", [P, K, BATCH], F16), s.sb("rhl", [P, K, BATCH], F16)
        rows = [s.sb(f"rows{p}", [P, 2 * D], F16) for p in range(2)]
        psg = [[s.ps(f"g{g}{p}", [P, BLK]) for p in range(2)] for g in range(G)]
        ps_t = s.ps("t", [P, 2 * BLK], F16)
        ps_l = s.ps("l", [P, BLK])
        d_in, d_tab, rows_free = s.sem("d_in"), s.sem("d_tab"), s.sem("rows_free")
        v_mm, setup, xc_ready, proj_done = s.sem("v_mm"), s.sem("setup"), s.sem("xc_ready"), s.sem("proj_done")
        r_mm, z_mm, c_mm, r_done, z_done, t_done = (s.sem(n) for n in ("r_mm", "z_mm", "c_mm", "r_done", "z_done", "t_done"))
        rh_hi, rh_lo, h_hi, h_lo, dv = (s.sem(n) for n in ("rh_hi", "rh_lo", "h_hi", "h_lo", "dv"))
        tile_mm, lg_read, row_done, init = s.sem("tile_mm"), s.sem("lg_read"), s.sem("row_done"), s.sem("init")

        def cols(step):
            return slice(step * BATCH, (step + 1) * BATCH)

        with nc.Block() as block:
            @block.sync
            def _(sp):
                sp.dma_start(condT[:], a["condT"].rearrange("(k p) b -> p k b", p=P)).then_inc(d_in, 16)
                sp.dma_start(bias[:], a["b_gru"]).then_inc(d_in, 16)
                sp.dma_start(gwraw[:], a["gate_w"].rearrange("(k p) e -> p k e", p=P)).then_inc(d_in, 16)
                for g in range(G):
                    sp.dma_start(cond_w[:, g], a["C_gru"][g].rearrange("(k p) n -> p k n", p=P)).then_inc(d_in, 16)
                    sp.dma_start(raw[:, 0, g], a["U_gru"][g].rearrange("(k p) n -> p k n", p=P)).then_inc(d_in, 16)
                    sp.dma_start(raw[:, 1, g], a["W_gru"][g].rearrange("(k p) n -> p k n", p=P)).then_inc(d_in, 16)
                sp.sem_inc(rows_free, 2)
                with sp.Fori(0, NC2) as i:
                    for par in range(2):
                        c = 2 * i + par
                        sp.wait_ge(row_done, c + 2)
                        sp.dma_start(table[bass.ds(c * P, P), 0:2 * D], rows[par][:].bitcast(U16)).then_inc(d_tab, 16)
                        sp.wait_ge(d_tab, 16 * c + 16)
                        sp.sem_inc(rows_free, 1)
                sp.wait_ge(row_done, NT + 2)
                sp.dma_start(table[NT * P:(NT + 1) * P, 0:2 * D], rows[0][:].bitcast(U16)).then_inc(d_tab, 16)
                sp.wait_ge(d_tab, 16 * (NT + 1))

            @block.gpsimd
            def _(pool):
                def fetch(c, par):
                    pool.tensor_copy(xc[par][:, 0], x1h[:, :, bass.ds(c * P, P)])
                    pool.tensor_copy(xc[par][:, 1], x1l[:, :, bass.ds(c * P, P)]).then_inc(xc_ready, 1)
                fetch(0, 0)
                with pool.Fori(0, NC2) as i:
                    for par in range(2):
                        c = 2 * i + par
                        pool.wait_ge(proj_done, c + 1)
                        fetch(c + 1, 1 - par)

            @block.tensor
            def _(pe):
                def share_of_x(par, lo, hi):
                    n = 0
                    for g in range(G):
                        for m in range(K):
                            out = psg[g][par][:, m * P:(m + 1) * P]
                            ms = slice(m * P, (m + 1) * P)
                            todo = [(w, x) for k in range(K) for w, x in
                                    pair_products(wh[:, 1, g, k, ms], wl[:, 1, g, k, ms], xc[par][:, 0, k], xc[par][:, 1, k])]
                            for v in (vh, vl):
                                todo.append((idsc[:], v[:, g * K + m].unsqueeze(1).to_broadcast([P, TILE_STEPS, BATCH])))
                            for j, (w, x) in enumerate(todo):
                                if lo <= n < hi:
                                    o = out.rearrange("p (t b) -> p t b", b=BATCH) if j >= 3 * K else out
                                    ins = pe.matmul(o, w, x, start=(m == 0 and j == 0), stop=True, skip_group_check=True)
                                n += 1
                    if hi == n:
                        ins.then_inc(proj_done, 1)

                def recurrence(g, par, step, high, low, low_ready):
                    outs = [psg[g][par][:, m * P + step * BATCH:m * P + (step + 1) * BATCH] for m in range(K)]
                    for m in range(K):
                        for k in range(K):
                            for w in (wh, wl):
                                pe.matmul(outs[m], w[:, 0, g, k, m * P:(m + 1) * P], high(k), start=False, stop=True,
                                          skip_group_check=True)
                    if low_ready:
                        pe.wait_ge(*low_ready)
                    for m in range(K):
                        for k in range(K):
                            ins = pe.matmul(outs[m], wh[:, 0, g, k, m * P:(m + 1) * P], low(k), start=False, stop=True,
                                            skip_group_check=True)
                    return ins

                def finished_tile(par):
                    for q, h in enumerate((hh[par], hl[par])):
                        for k in range(K):
                            pe.transpose(ps_t[:, (q * K + k) * P:(q * K + k + 1) * P], h[:, k], idh[:])
                    n = 0
                    for k in range(K):
                        for h, w in ((hh, gwh), (hl, gwh), (hh, gwl)):
                            ins = pe.matmul(ps_l[:, 0:E], h[par][:, k], w[:, k], start=(n == 0), stop=(n == 3 * K - 1))
                            n += 1
                    ins.then_inc(tile_mm, 1)

                pe.wait_ge(d_in, 192)
                for g in range(G):
                    for m in range(K):
                        for k in range(K):
                            c0 = (g * K + m) * BATCH
                            ins = pe.matmul(ps_l[:, c0:c0 + BATCH], cond_w[:, g, k, m * P:(m + 1) * P], condT[:, k],
                                            start=(k == 0), stop=(k == K - 1))
                ins.then_inc(v_mm, 1)
                pe.wait_ge(setup, 1)
                pe.sem_inc(proj_done, 1)
                pe.wait_ge(xc_ready, 1)
                share_of_x(0, 0, 48)
                with pe.Fori(0, NC2) as i:
                    for par in range(2):
                        c = 2 * i + par
                        for st in range(TILE_STEPS):
                            t = TILE_STEPS * c + st
                            hp, hc = (par, cols(st - 1)) if st else (1 - par, cols(TILE_STEPS - 1))
                            pe.wait_ge(h_hi, t + 1)
                            recurrence(R_, par, st, lambda k: hh[hp][:, k, hc], lambda k: hl[hp][:, k, hc], (h_lo, t + 1))\
                                .then_inc(r_mm, 1)
                            recurrence(Z_, par, st, lambda k: hh[hp][:, k, hc], lambda k: hl[hp][:, k, hc], None)\
                                .then_inc(z_mm, 1)
                            pe.wait_ge(rh_hi, t + 1)
                            recurrence(C_, par, st, lambda k: rhh[:, k], lambda k: rhl[:, k], (rh_lo, t + 1)).then_inc(c_mm, 1)
                            if st == 0:
                                pe.wait_ge(xc_ready, c + 2)
                            if st == 1:
                                pe.wait_ge(lg_read, c + 1)
                                pe.wait_ge(row_done, c + 1)
                                finished_tile(1 - par)
                            else:
                                n = st - (st > 1)
                                share_of_x(1 - par, 7 * n, min(7 * n + 7, 48))
                pe.wait_ge(h_lo, STEPS + 1)
                pe.wait_ge(h_hi, STEPS + 1)
                pe.wait_ge(lg_read, NT + 1)
                pe.wait_ge(row_done, NT + 1)
                finished_tile(1)

            @block.scalar
            def _(act):
                def gate(g, par, st):
                    return psg[g][par][:, 0:K * P].rearrange("p (m t b) -> p m t b", m=K, b=BATCH)[:, :, st]

                def rows_piece(par, q):
                    return act.activation(rows[par][:, q * P:(q + 1) * P], ps_t[:, q * P:(q + 1) * P], ACT.Copy)

                act.sem_inc(row_done, 1)
                with act.Fori(0, NC2) as i:
                    for par in range(2):
                        c = 2 * i + par
                        for st in range(TILE_STEPS):
                            t = TILE_STEPS * c + st
                            act.wait_ge(r_mm, t + 1)
                            act.activation(r[:], gate(R_, par, st), ACT.Sigmoid, scale=INV2).then_inc(r_done, 1)
                            act.wait_ge(z_mm, t + 1)
                            act.activation(z[:], gate(Z_, par, st), ACT.Sigmoid, scale=INV2).then_inc(z_done, 1)
                            if 2 <= st < 6:
                                if st == 2:
                                    act.wait_ge(tile_mm, c + 1)
                                    act.wait_ge(rows_free, c + 1)
                                p = rows_piece(par, st - 2)
                                if st == 5:
                                    p.then_inc(row_done, 1)
                            act.wait_ge(c_mm, t + 1)
                            act.activation(th[:], gate(C_, par, st), ACT.Tanh, scale=INV2).then_inc(t_done, 1)
                act.wait_ge(tile_mm, NT + 1)
                act.wait_ge(rows_free, NT + 1)
                for q in range(2 * K):
                    p = rows_piece(0, q)
                p.then_inc(row_done, 1)

            @block.vector
            def _(dve):
                c_ = Chain(dve, init)
                dve.wait_ge(d_in, 192)
                c_.link(dve.tensor_scalar(wh[:], raw[:], SC, None, ALU.mult))
                c_.link(dve.tensor_scalar(gwh[:], gwraw[:], SC, None, ALU.mult))
                c_.link(dve.tensor_copy(idh[:], cst[:, C_ID:C_ID + P]))
                c_.link(dve.tensor_scalar(idsc[:], cst[:, C_ID:C_ID + P], SC, None, ALU.mult))
                c_.link(dve.memset(Hf[:], 0.0))
                c_.link(dve.memset(hh[1][:], 0.0))
                c_.step(dve.memset(hl[1][:], 0.0))
                c_.link(dve.scalar_tensor_tensor(out=wl[:].rearrange("p a g k d -> p (a g k d)"), in0=raw[:].rearrange("p a g k d -> p (a g k d)"),
                                                 scalar=SC, in1=wh[:].rearrange("p a g k d -> p (a g k d)"),
                                                 op0=ALU.mult, op1=ALU.subtract))
                c_.link(dve.scalar_tensor_tensor(out=gwl[:], in0=gwraw[:], scalar=SC, in1=gwh[:], op0=ALU.mult, op1=ALU.subtract))
                dve.wait_ge(v_mm, 1)
                for n in range(G * K):
                    o = dve.tensor_scalar(vf[:, n], ps_l[:, n * BATCH:(n + 1) * BATCH], bias[:, n:n + 1], SC, ALU.add, ALU.mult)
                c_.step(o)
                c_.step(dve.tensor_copy(vh[:], vf[:]))
                c_.wait()
                dve.tensor_tensor(vl[:], vf[:], vh[:], ALU.subtract).then_inc(setup, 1)
                dve.sem_inc(h_hi, 1)
                dve.sem_inc(h_lo, 1)
                dve.sem_inc(lg_read, 1)

                def logits(c):
                    dve.wait_ge(tile_mm, c + 1)
                    dve.tensor_scalar(Lg[:, bass.ds(c, 1)], ps_l[:, 0:E].unsqueeze(1), INV2, None, ALU.mult).then_inc(lg_read, 1)

                with dve.Fori(0, NC2) as i:
                    for par in range(2):
                        c = 2 * i + par
                        for st in range(TILE_STEPS):
                            t = TILE_STEPS * c + st
                            dve.wait_ge(r_done, t + 1)
                            dve.tensor_tensor(rhh[:], r[:], Hf[:], ALU.mult).then_inc(rh_hi, 1)
                            dve.tensor_tensor(rv[:], r[:], Hf[:], ALU.mult).then_inc(dv, 1)
                            dve.wait_ge(dv, 5 * t + 1)
                            dve.tensor_tensor(rhl[:], rv[:], rhh[:], ALU.subtract).then_inc(rh_lo, 1)
                            dve.wait_ge(z_done, t + 1)
                            dve.tensor_scalar(zc[:], z[:], -1.0, 1.0, ALU.mult, ALU.add).then_inc(dv, 1)
                            dve.wait_ge(dv, 5 * t + 2)
                            dve.tensor_tensor(av[:], zc[:], Hf[:], ALU.mult).then_inc(dv, 1)
                            if st == 3:
                                logits(c)
                            dve.wait_ge(t_done, t + 1)
                            dve.scalar_tensor_tensor(out=mv[:], in0=z[:], scalar=SC, in1=th[:], op0=ALU.mult, op1=ALU.mult)\
                                .then_inc(dv, 1)
                            dve.wait_ge(dv, 5 * t + 4)
                            dve.tensor_tensor(hh[par][:, :, cols(st)], mv[:], av[:], ALU.add).then_inc(h_hi, 1)
                            dve.tensor_tensor(Hf[:], mv[:], av[:], ALU.add).then_inc(dv, 1)
                            dve.wait_ge(dv, 5 * t + 5)
                            dve.tensor_tensor(hl[par][:, :, cols(st)], Hf[:], hh[par][:, :, cols(st)], ALU.subtract)\
                                .then_inc(h_lo, 1)
                logits(NT)
                dve.wait_ge(lg_read, NT + 2)


def stage_route(nc, a, keep):
    cst, Lg, table, gidx, sidx = keep["cst"], keep["Lg"], keep["table"], keep["gidx"], keep["sidx"]
    NQ = TOPK * NT
    QB = 16
    PAD = NT // 2
    with ExitStack() as ctx:
        s = Space(nc, ctx, "rt")
        M = s.sb("M", [P, TOPK, NT, E], F16)
        best = s.sb("best", [P, TOPK, NT], F32)
        first = s.sb("first", [P, TOPK, NT], F32)
        eq, L2 = s.sb("eq", [P, NT, E], F32), s.sb("L2", [P, NT, E], F32)
        pr = s.sb("pr", [P, 4, NT], F32)
        prob, prob2 = s.sb("prob", [P, NT, E], F32), s.sb("prob2", [P, NT, E], F32)
        masks = s.sb("masks", [P, 4, P], F16)
        total, totalf = s.sb("total", [P, TOPK, E], F16), s.sb("totalf", [P, TOPK, E], F32)
        scan = [s.sb(f"scan{i}", [P, TOPK, PAD + NT + 1, E], F16) for i in range(2)]
        rank, V = s.sb("rank", [P, TOPK, NT, E], F32), s.sb("V", [P, TOPK, NT, E], F32)
        slot, own = s.sb("slot", [P, NQ], F32), s.sb("own", [P, NQ], F32)
        hi_i = s.sb("hi_i", [P, NQ], I16)
        lo = s.sb("lo", [P, NQ], F32)
        io16, lo16, hi16, tile16 = (s.sb(n, [P, w], F16) for n, w in (("io16", P), ("lo16", NQ), ("hi16", NQ), ("tile16", NT)))
        onelo = [s.sb(f"onelo{i}", [P, QB, P], F16) for i in range(2)]
        onehi = s.sb("onehi", [P, QB, SLOT_TILES], F16)
        val = [s.sb(f"val{i}", [P, QB, 2, SLOT_TILES], F16) for i in range(2)]
        I, empty = s.sb("I", [P, SLOT_TILES], F32), s.sb("empty", [P, SLOT_TILES], F32)
        gI = s.sb("gI", [P, SLOT_TILES], F32)
        ps_r, ps_i = s.ps("ps_r", [P, BLK]), s.ps("ps_i", [P, BLK])
        ch, exp_in, exp_done, prob_ready, d_prob = (s.sem(n) for n in ("ch", "exp_in", "exp_done", "prob_ready", "d_prob"))
        count_in, ranked, ones_ready, ones_used = (s.sem(n) for n in ("count_in", "ranked", "ones_ready", "ones_used"))
        wide = [P, NT, E]
        L = Lg[:, 1:]
        rounds = [1 << d for d in range(NT.bit_length() - 1)]

        with nc.Block() as block:
            @block.sync
            def _(sp):
                sp.wait_ge(prob_ready, 1)
                sp.dma_start(table[P:, 2 * D:].rearrange("(i p) c -> p i c", p=P), prob2[:].bitcast(U16)).then_inc(d_prob, 16)
                sp.wait_ge(d_prob, 16)

            @block.scalar
            def _(act):
                act.wait_ge(exp_in, 1)
                act.activation(pr[:, 1], pr[:, 0], ACT.Exp).then_inc(exp_done, 1)

            @block.tensor
            def _(pe):
                pe.wait_ge(count_in, 1)
                last = scan[len(rounds) % 2]
                pe.matmul(ps_r[:], masks[:, 2], M[:].rearrange("p k i e -> p (k i e)"), start=True, stop=False, skip_group_check=True)
                for k in range(TOPK):
                    out = ps_r[:, k * NT * E:(k + 1) * NT * E].rearrange("p (i e) -> p i e", e=E)
                    pe.matmul(out, masks[:, 1], last[:, k, PAD:PAD + NT], start=False, stop=False, skip_group_check=True)
                    pe.matmul(out, masks[:, 0], total[:, k].unsqueeze(1).to_broadcast(wide), start=False, stop=False,
                              skip_group_check=True)
                pe.matmul(out, masks[:, 3], total[:, 0].unsqueeze(1).to_broadcast(wide), start=False, stop=True,
                          skip_group_check=True).then_inc(ranked, 1)
                for b in range(NQ // QB):
                    pe.wait_ge(ones_ready, b + 1)
                    for q in range(QB):
                        ins = pe.matmul(ps_i[:, 0:2 * SLOT_TILES], onelo[b % 2][:, q], val[b % 2][:, q].rearrange("p a n -> p (a n)"),
                                        start=(b == 0 and q == 0), stop=(b == NQ // QB - 1 and q == QB - 1))
                    ins.then_inc(ones_used, 1)

            @block.vector
            def _(dve):
                c = Chain(dve, ch)

                def row(col, shape):
                    return cst[:, col:col + E].unsqueeze(1).to_broadcast(shape)

                c.link(dve.tensor_copy(masks[:, 0:3], cst[:, C_BLESS:C_BLESS + 3 * P].rearrange("p (a n) -> p a n", a=3)))
                c.link(dve.memset(masks[:, 3], 1.0))
                for i in range(2):
                    c.link(dve.memset(scan[i][:], 0.0))
                c.link(dve.tensor_copy(io16[:], cst[:, C_IOTA:C_IOTA + P]))
                c.link(dve.tensor_copy(tile16[:], cst[:, C_TILE:C_TILE + NT]))
                for k, src in ((0, L), (1, L2[:])):
                    c.step(dve.tensor_reduce(best[:, k], src, X, ALU.max))
                    c.step(dve.tensor_tensor(eq[:], src, best[:, k].unsqueeze(2).to_broadcast(wide), ALU.is_equal))
                    c.step(dve.tensor_tensor(eq[:], eq[:], row(C_EIDX, wide), ALU.mult))
                    c.step(dve.tensor_reduce(first[:, k], eq[:], X, ALU.max))
                    c.step(dve.tensor_tensor(M[:, k], eq[:], first[:, k].unsqueeze(2).to_broadcast(wide), ALU.is_equal))
                    if k == 0:
                        c.step(dve.scalar_tensor_tensor(out=L2[:], in0=M[:, 0], scalar=-3e38, in1=L, op0=ALU.mult, op1=ALU.add))
                dve.tensor_tensor(pr[:, 0], best[:, 1], best[:, 0], ALU.subtract).then_inc(exp_in, 1)
                c.step(dve.tensor_reduce(totalf[:], M[:].rearrange("p k i e -> p k e i"), X, ALU.add))
                c.link(dve.tensor_copy(total[:], totalf[:]))
                for k in range(TOPK):
                    c.link(dve.tensor_copy(scan[0][:, k, PAD + 1:], M[:, k]))
                c.wait()
                for n, d in enumerate(rounds):
                    for k in range(TOPK):
                        c.link(dve.tensor_tensor(scan[(n + 1) % 2][:, k, PAD:PAD + NT], scan[n % 2][:, k, PAD:PAD + NT],
                                                 scan[n % 2][:, k, PAD - d:PAD + NT - d], ALU.add))
                    c.wait()
                dve.sem_inc(count_in, 1)
                dve.wait_ge(exp_done, 1)
                c.step(dve.tensor_scalar(pr[:, 2], pr[:, 1], 1.0, None, ALU.add))
                c.step(dve.reciprocal(pr[:, 3], pr[:, 2]))
                c.step(dve.tensor_tensor(pr[:, 2], pr[:, 1], pr[:, 3], ALU.mult))
                c.link(dve.tensor_tensor(prob[:], M[:, 0], pr[:, 3].unsqueeze(2).to_broadcast(wide), ALU.mult))
                c.step(dve.tensor_tensor(eq[:], M[:, 1], pr[:, 2].unsqueeze(2).to_broadcast(wide), ALU.mult))
                dve.tensor_tensor(prob2[:], prob[:], eq[:], ALU.add).then_inc(prob_ready, 1)
                dve.wait_ge(ranked, 1)
                c.step(dve.tensor_copy(rank[:].rearrange("p k i e -> p (k i e)"), ps_r[:]))
                rq, Vq, Mq = (x[:].rearrange("p k i e -> p (k i) e") for x in (rank, V, M))
                wq = [P, NQ, E]
                c.step(dve.tensor_tensor(Vq, rq, row(C_EOFF, wq), ALU.add))
                c.step(dve.tensor_tensor(Vq, Vq, Mq, ALU.mult))
                c.link(dve.tensor_reduce(slot[:], Vq, X, ALU.add))
                c.step(dve.tensor_tensor(rq, rq, Mq, ALU.mult))
                c.step(dve.tensor_reduce(own[:], rq, X, ALU.add))
                c.step(dve.tensor_scalar(own[:], own[:], float(CAP), 2.0 * E * CAP, ALU.is_ge, ALU.mult))
                c.step(dve.tensor_tensor(slot[:], slot[:], own[:], ALU.add))
                c.step(dve.tensor_scalar(hi_i[:], slot[:], -(P - 1) / 2, 1.0 / P, ALU.add, ALU.mult))
                c.link(dve.tensor_copy(hi16[:], hi_i[:]))
                c.step(dve.scalar_tensor_tensor(out=lo16[:], in0=hi_i[:], scalar=-float(P), in1=slot[:], op0=ALU.mult, op1=ALU.add))
                for b in range(NQ // QB):
                    qs = slice(b * QB, (b + 1) * QB)
                    i0 = b * QB % NT
                    if b >= 2:
                        dve.wait_ge(ones_used, b - 1)
                    c.link(dve.tensor_tensor(onelo[b % 2][:], io16[:].unsqueeze(1).to_broadcast([P, QB, P]),
                                             lo16[:, qs].unsqueeze(2).to_broadcast([P, QB, P]), ALU.is_equal))
                    w = [P, QB, SLOT_TILES]
                    c.step(dve.tensor_tensor(onehi[:], io16[:, 0:SLOT_TILES].unsqueeze(1).to_broadcast(w),
                                             hi16[:, qs].unsqueeze(2).to_broadcast(w), ALU.is_equal))
                    c.link(dve.tensor_tensor(val[b % 2][:, :, 0], onehi[:],
                                             tile16[:, i0:i0 + QB].unsqueeze(2).to_broadcast(w), ALU.mult))
                    c.step(dve.tensor_scalar(val[b % 2][:, :, 1], onehi[:], cst[:, C_P1:C_P1 + 1], None, ALU.mult))
                    dve.sem_inc(ones_ready, 1)
                dve.wait_ge(ones_used, NQ // QB)
                c.step(dve.tensor_copy(gI[:], ps_i[:, SLOT_TILES:2 * SLOT_TILES]))
                c.step(dve.scalar_tensor_tensor(out=I[:], in0=ps_i[:, 0:SLOT_TILES], scalar=float(P), in1=gI[:],
                                                op0=ALU.mult, op1=ALU.add))
                c.link(dve.tensor_scalar(empty[:], I[:], 0.0, cst[:, C_DUM:C_DUM + 1], ALU.is_equal, ALU.mult))
                c.step(dve.tensor_scalar(gI[:], I[:], -1.0, 0.0, ALU.add, ALU.max))
                c.link(dve.tensor_scalar(gidx[:], gI[:], float(P), None, ALU.add))
                c.step(dve.scalar_tensor_tensor(out=sidx[:], in0=I[:], scalar=-1.0, in1=empty[:], op0=ALU.add, op1=ALU.add))


def stage_experts(nc, a, keep):
    table, gidx, sidx, cst, out = keep["table"], keep["gidx"], keep["sidx"], keep["cst"], a["out"]
    GROUPS = [(0, 4), (4, 4), (8, CT - 8)]
    RFC, RG, RY = 4, 3, 4
    UNITS = len(GROUPS) * HM
    with ExitStack() as ctx:
        s = Space(nc, ctx, "ex")
        fcb = s.sb("fcb", [P, E * HM], F32)
        pjb = s.sb("pjb", [P, E * D], F32)
        idh = s.sb("idh", [P, P], F16)
        wst = [s.sb("wst_fc", [P, K, H], F32), s.sb("wst_pj", [P, HM, D], F32)]
        wh = [[s.sb(f"wh{p}_fc", [P, K, H], F16), s.sb(f"wh{p}_pj", [P, HM, D], F16)] for p in range(2)]
        wl = [[s.sb(f"wl{p}_fc", [P, K, H], F16), s.sb(f"wl{p}_pj", [P, HM, D], F16)] for p in range(2)]
        gi = [s.sb(f"gi{p}", [P, CT], U32) for p in range(2)]
        si = [s.sb(f"si{p}", [P, CT], U32) for p in range(2)]
        got = [s.sb(f"got{p}", [P, CT, ROW], U16) for p in range(2)]
        fb = [s.sb(f"fb{p}", [P, HM], F32) for p in range(2)]
        weight = [s.sb(f"weight{p}", [P, CT, 1], F32) for p in range(2)]
        xg = s.sb("xg", [P, 2, K, CAP], F16)
        gel = [s.sb(f"gel{i}", [P, BLK], F32) for i in range(RG)]
        Gh = [s.sb(f"Gh{i}", [P, HM, BLK], F16) for i in range(2)]
        Gl = [s.sb(f"Gl{i}", [P, HM, BLK], F16) for i in range(2)]
        y1 = [s.sb(f"y1{i}", [P, D], F32) for i in range(2)]
        y = [s.sb(f"y{i}", [P, D], F32) for i in range(RY)]
        ps_x = [s.ps(f"x{i}", [P, 2 * BLK], F16) for i in range(2)]
        ps_f = [s.ps(f"f{i}", [P, BLK]) for i in range(RFC)]
        ps_y = [s.ps(f"y{i}", [P, BLK]) for i in range(2)]
        d_b, d_w, d_s = s.sem("d_b"), s.sem("d_w"), s.sem("d_s")
        d_g = [s.sem(f"d_g{p}") for p in range(2)]
        idx_in, w_hi, w_lo, xt_mm, xt_done = (s.sem(n) for n in ("idx_in", "w_hi", "w_lo", "xt_mm", "xt_done"))
        fc_mm, gel_done, g_hi, g_lo, y_mm, y1_done, y_done, idr, stored, fb_in, w_in = (
            s.sem(n) for n in ("fc_mm", "gel_done", "g_hi", "g_lo", "y_mm", "y1_done", "y_done", "idr", "stored", "fb_in", "w_in"))

        def order(T, fc, proj):
            T(0), T(1), fc(0), T(2), fc(1), proj(0), fc(2), proj(1), proj(2)

        with nc.Block() as block:
            @block.sync
            def _(sp):
                sp.dma_start(fcb[:], a["fc_bias"]).then_inc(d_b, 16)
                sp.dma_start(pjb[:], a["proj_bias"].partition_broadcast(P)).then_inc(d_b, 16)
                with sp.Fori(0, E + 1) as e:
                    sp.wait_ge(w_lo, 2 * e + 1)
                    sp.dma_start(wst[0][:], a["c_fc"][bass.ds(e % E, 1)].squeeze(0).rearrange("(k p) n -> p k n", p=P)).then_inc(d_w, 16)
                    sp.dma_start(wst[1][:], a["c_proj"][bass.ds(e % E, 1)].squeeze(0).rearrange("(k p) n -> p k n", p=P)).then_inc(d_w, 16)

            @block.gpsimd
            def _(pool):
                def gathers(e, p):
                    n = e % E * CT
                    pool.tensor_copy(gi[p][:], gidx[:, bass.ds(n, CT)]).then_inc(idx_in, 1)
                    pool.tensor_copy(si[p][:], sidx[:, bass.ds(n, CT)]).then_inc(idx_in, 1)
                    pool.wait_ge(idx_in, 2 * e + 2)
                    pool.tensor_copy(fb[p][:], fcb[:, bass.ds(e % E * HM, HM)]).then_inc(fb_in, 1)
                    for t in range(CT):
                        pool.indirect_dma_start(out=got[p][:, t], out_offset=None, in_=table,
                                                in_offset=bass.IndirectOffsetOnAxis(ap=gi[p][:, t:t + 1], axis=0))\
                            .then_inc(d_g[p], 16)

                def scatters(e, p):
                    for t in range(CT):
                        n = e * CT + t
                        pool.wait_ge(y_done, n + 3)
                        pool.sem_inc(stored, 1)
                        pool.indirect_dma_start(out=out, out_offset=bass.IndirectOffsetOnAxis(ap=si[p][:, t:t + 1], axis=0),
                                                in_=y[(p * CT + t) % RY][:], in_offset=None, compute_op=ALU.add).then_inc(d_s, 16)
                        pool.wait_ge(d_s, 16 * n + 16)

                def weights(e, visit, p):
                    pool.wait_ge(d_g[p], 16 * CT * visit)
                    pool.tensor_copy(weight[p][:], got[p][:, :, 2 * D:].bitcast(F32)[:, :, bass.ds(e % E, 1)]).then_inc(w_in, 1)

                pool.wait_ge(d_b, 32)
                pool.sem_inc(stored, RY - 1)
                gathers(0, 0)
                weights(0, 1, 0)
                with pool.Fori(0, E // 2) as i:
                    for p in range(2):
                        e = 2 * i + p
                        gathers(e + 1, 1 - p)
                        scatters(e, p)
                        weights(e + 1, i + 1 + p, 1 - p)

            @block.tensor
            def _(pe):
                pe.sem_inc(y_mm, CT + 1)
                pe.wait_ge(idr, 1)
                with pe.Fori(0, E // 2) as i:
                    for p in range(2):
                        e = 2 * i + p

                        def T(g):
                            t0, nt = GROUPS[g]
                            if g == 0:
                                pe.wait_ge(d_g[p], 16 * CT * (i + 1))
                            for t in range(t0, t0 + nt):
                                pe.wait_ge(xt_done, CT * e + t + 1)
                                for j in range(2 * K):
                                    ins = pe.transpose(ps_x[t % 2][:, j * P:(j + 1) * P], got[p][:, t, j * P:(j + 1) * P].bitcast(F16), idh[:])
                                ins.then_inc(xt_mm, 1)

                        def fc(g):
                            t0, nt = GROUPS[g]
                            pe.wait_ge(xt_done, CT * e + t0 + nt + 2)
                            if g == 0:
                                pe.wait_ge(w_lo, 2 * e + 3)
                            cols = slice(t0 * P, (t0 + nt) * P)
                            for m in range(HM):
                                u = g * HM + m
                                pe.wait_ge(gel_done, UNITS * e + u + 1)
                                ms, n = slice(m * P, (m + 1) * P), 0
                                for k in range(K):
                                    for w, x in pair_products(wh[p][0][:, k, ms], wl[p][0][:, k, ms], xg[:, 0, k, cols], xg[:, 1, k, cols]):
                                        ins = pe.matmul(ps_f[u % RFC][:, 0:nt * P], w, x, start=(n == 0), stop=(n == 3 * K - 1))
                                        n += 1
                                ins.then_inc(fc_mm, 1)

                        def proj(g):
                            t0, nt = GROUPS[g]
                            gb = (p + g) % 2
                            pe.wait_ge(g_lo, UNITS * e + (g + 1) * HM + RG)
                            for t in range(t0, t0 + nt):
                                pe.wait_ge(y1_done, CT * e + t + 1)
                                cs, n = slice((t - t0) * P, (t - t0 + 1) * P), 0
                                for k in range(HM):
                                    for x, w in ((Gh, wh), (Gl, wh), (Gh, wl)):
                                        ins = pe.matmul(ps_y[t % 2][:, 0:D], x[gb][:, k, cs], w[p][1][:, k], start=(n == 0),
                                                        stop=(n == 3 * HM - 1))
                                        n += 1
                                ins.then_inc(y_mm, 1)

                        order(T, fc, proj)

            @block.scalar
            def _(act):
                def split_high(e, p):
                    act.wait_ge(d_w, 32 * e + 32)
                    act.wait_ge(y_mm, CT * e + 1)
                    for j in range(2):
                        act.activation(wh[p][j][:], wst[j][:], ACT.Copy, scale=SC).then_inc(w_hi, 1)

                act.sem_inc(gel_done, RFC)
                act.sem_inc(y_done, 2)
                act.wait_ge(d_b, 32)
                split_high(0, 0)
                with act.Fori(0, E // 2) as i:
                    for p in range(2):
                        e = 2 * i + p

                        def fc(g):
                            w = GROUPS[g][1] * P
                            if g == 0:
                                act.wait_ge(fb_in, e + 1)
                            for m in range(HM):
                                u = g * HM + m
                                act.wait_ge(fc_mm, UNITS * e + u + 1)
                                act.wait_ge(g_lo, UNITS * e + u + 1)
                                act.activation(gel[u % RG][:, 0:w], ps_f[u % RFC][:, 0:w], ACT.Gelu, scale=INV2,
                                               bias=fb[p][:, m:m + 1]).then_inc(gel_done, 1)
                            if g == 1:
                                split_high(e + 1, 1 - p)

                        def proj(g):
                            t0, nt = GROUPS[g]
                            if g == 0:
                                act.wait_ge(w_in, e + 1)
                            for t in range(t0, t0 + nt):
                                act.wait_ge(y1_done, CT * e + t + 3)
                                act.wait_ge(stored, CT * e + t + 1)
                                act.activation(y[(p * CT + t) % RY][:], y1[t % 2][:], ACT.Copy,
                                               scale=weight[p][:, t]).then_inc(y_done, 1)

                        order(lambda g: None, fc, proj)

            @block.vector
            def _(dve):
                def split_low(e, p):
                    for j in range(2):
                        dve.wait_ge(w_hi, 2 * e + j + 1)
                        flat = [x[:].rearrange("p a b -> p (a b)") for x in (wl[p][j], wst[j], wh[p][j])]
                        dve.scalar_tensor_tensor(out=flat[0], in0=flat[1], scalar=SC, in1=flat[2], op0=ALU.mult,
                                                 op1=ALU.subtract).then_inc(w_lo, 1)

                dve.sem_inc(w_lo, 1)
                dve.sem_inc(xt_done, 2)
                dve.sem_inc(g_lo, RG)
                dve.sem_inc(y1_done, 2)
                dve.tensor_copy(idh[:], cst[:, C_ID:C_ID + P]).then_inc(idr, 1)
                dve.wait_ge(d_b, 32)
                split_low(0, 0)
                with dve.Fori(0, E // 2) as i:
                    for p in range(2):
                        e = 2 * i + p

                        def T(g):
                            t0, nt = GROUPS[g]
                            for t in range(t0, t0 + nt):
                                dve.wait_ge(xt_mm, CT * e + t + 1)
                                dve.tensor_copy(xg[:, :, :, t * P:(t + 1) * P],
                                                ps_x[t % 2][:, 0:2 * K * P].rearrange("p (a k n) -> p a k n", a=2, k=K))\
                                    .then_inc(xt_done, 1)

                        def fc(g):
                            w, gb = GROUPS[g][1] * P, (p + g) % 2
                            dve.wait_ge(y_mm, 1 + CT * e + (CT - GROUPS[2][1], CT, CT + GROUPS[0][1])[g])
                            for m in range(HM):
                                u = g * HM + m
                                dve.wait_ge(gel_done, UNITS * e + u + 1 + RFC)
                                dve.tensor_scalar(Gh[gb][:, m, 0:w], gel[u % RG][:, 0:w], SC, None, ALU.mult).then_inc(g_hi, 1)
                                dve.wait_ge(g_hi, UNITS * e + u + 1)
                                dve.scalar_tensor_tensor(out=Gl[gb][:, m, 0:w], in0=gel[u % RG][:, 0:w], scalar=SC,
                                                         in1=Gh[gb][:, m, 0:w], op0=ALU.mult, op1=ALU.subtract).then_inc(g_lo, 1)
                            if g == 1:
                                split_low(e + 1, 1 - p)

                        def proj(g):
                            t0, nt = GROUPS[g]
                            for t in range(t0, t0 + nt):
                                dve.wait_ge(y_mm, CT * e + t + 2 + CT)
                                dve.wait_ge(y_done, CT * e + t + 1)
                                dve.scalar_tensor_tensor(out=y1[t % 2][:], in0=ps_y[t % 2][:, 0:D], scalar=INV2,
                                                         in1=pjb[:, bass.ds(e * D, D)], op0=ALU.mult, op1=ALU.add).then_inc(y1_done, 1)

                        order(T, fc, proj)


def adaln_ffn_moe_kernel(nc, a, stages=99):
    with ExitStack() as ctx:
        s = s0 = Space(nc, ctx, "all")
        keep = {
            "cst": s.sb("cst", [P, C_END], F32),
            "scal": s.sb("scal", [P, S_END], F32),
            "x0h": s.sb("x0h", [P, K, N + P], F16),
            "x0l": s.sb("x0l", [P, K, N + P], F16),
        }
        with ExitStack() as inner:
            s = Space(nc, inner, "ffn")
            keep["wTh"] = s.sb("wTh", [P, WCOLS], F16)
            keep["wTl"] = s.sb("wTl", [P, WCOLS], F16)
            stage_logits(nc, a, keep)
            keep["R"] = s.sb("R", [P, FO, N], F32)
            with ExitStack() as inner2:
                keep["qup"] = Space(nc, inner2, "ffn").sb("qup", [P, FO, N], I16)
                stage_gate_up(nc, a, keep)
                stage_product(nc, a, keep)
            stage_down(nc, a, keep)
        if stages > 4:
            keep["Lg"] = s0.sb("Lg", [P, NT + 1, E], F32)
            keep["gidx"], keep["sidx"] = (s0.sb(n, [P, SLOT_TILES], U32) for n in ("gidx", "sidx"))
            keep["table"] = nc.dram_tensor("state_rows", (P * (NT + 1), ROW), U16, kind="Internal").ap()
            stage_gru(nc, a, keep)
        if stages > 5:
            stage_route(nc, a, keep)
        if stages > 6:
            stage_experts(nc, a, keep)


def laid_out(v):
    c = np.ascontiguousarray
    cols = lambda b: c(b.reshape(-1, P).T)
    return {
        "xT": c(v["x"].transpose(2, 1, 0).reshape(D, N)),
        "condT": c(v["cond_1024"].T),
        "weight_matrix": c(v["L0_cond_weight_matrix"]),
        "W_proj": c(v["L0_cond_W_proj"]),
        "b_proj": cols(v["L0_cond_b_proj"]),
        "w_gate": c(v["L0_ffn_w_gate"]),
        "w_up": c(v["L0_ffn_w_up"]),
        "w_down": c(v["L0_ffn_w_down"]),
        "W_gru": c(np.stack([v["L1_cond_W_r"], v["L1_cond_W_z"], v["L1_cond_W"]])),
        "U_gru": c(np.stack([v["L1_cond_U_r"], v["L1_cond_U_z"], v["L1_cond_U"]])),
        "C_gru": c(np.stack([v["L1_cond_C_r"], v["L1_cond_C_z"], v["L1_cond_C"]])),
        "b_gru": c(np.concatenate([cols(v[n]) for n in ("L1_cond_b_r", "L1_cond_b_z", "L1_cond_b")], axis=1)),
        "gate_w": c(v["L1_ffn_gate_w"]),
        "c_fc": c(v["L1_ffn_c_fc"]),
        "fc_bias": cols(v["L1_ffn_fc_bias"]),
        "c_proj": c(v["L1_ffn_c_proj"]),
        "proj_bias": c(v["L1_ffn_proj_bias"].reshape(1, E * D)),
        "consts": constants(),
    }


def kernel(**inputs):
    import concourse.bacc as bacc
    from concourse.bass_utils import run_bass_kernel_spmd

    nc = bacc.Bacc("TRN2", target_bir_lowering=False, num_devices=1)
    given = laid_out({n: np.asarray(v) for n, v in inputs.items()})
    arrays = {f"in_{n}_dram": v for n, v in given.items()}
    a = {n: nc.dram_tensor(f"in_{n}_dram", v.shape, mybir.dt.from_np(v.dtype), kind="ExternalInput").ap()
         for n, v in given.items()}
    a["out"] = nc.dram_tensor("out_0_dram", (N + DUMMY, D), F32, kind="ExternalOutput").ap()
    adaln_ffn_moe_kernel(nc, a)
    r = run_bass_kernel_spmd(nc, [arrays], core_ids=[0])
    got = r.results[0]["out_0_dram"]
    return np.ascontiguousarray(got[:N].reshape(STEPS, BATCH, D).transpose(1, 0, 2))
```

```python
from contextlib import ExitStack

import numpy as np

import concourse.bass as bass
from concourse import mybir

F32 = mybir.dt.float32
F16 = mybir.dt.float16
I16 = mybir.dt.int16
U16 = mybir.dt.uint16
U32 = mybir.dt.uint32
ALU = mybir.AluOpType
ACT = mybir.ActivationFunctionType
X = mybir.AxisListType.X

P = 128
BATCH, STEPS, D = 16, 256, 256
N = BATCH * STEPS
K = D // P
F = 768
FO = F // P
BLK = 512
NB = N // BLK
NT = N // P
QBLOCK = 32
WCOLS = 3 * K * F
E, TOPK = 8, 2
H = 4 * D
HM = H // P
CAP = int(1.25 * N * TOPK / E)
CT = CAP // P
SLOT_TILES = E * CT
QMAX = 32767.0
TINY = 1e-12
SC = 256.0
INV2 = 1.0 / (SC * SC)
TILE_STEPS = P // BATCH
ROW = 2 * D + 2 * E
DUMMY = P

C_ID, C_BLESS, C_BSAME, C_TLESS, C_IOTA, C_EIDX, C_EOFF, C_TILE, C_P1, C_DUM, C_END = np.cumsum(
    [0, P, P, P, P, P, E, E, NT, 1, 1])


def constants():
    c = np.zeros((P, C_END), np.float32)
    p = np.arange(P)
    b, t = p % BATCH, p // BATCH
    c[:, C_ID:C_ID + P] = np.eye(P)
    c[:, C_BLESS:C_BLESS + P] = b[:, None] < b[None, :]
    c[:, C_BSAME:C_BSAME + P] = b[:, None] == b[None, :]
    c[:, C_TLESS:C_TLESS + P] = (b[:, None] == b[None, :]) & (t[:, None] < t[None, :])
    c[:, C_IOTA:C_IOTA + P] = p[None, :]
    c[:, C_EIDX:C_EIDX + E] = E - np.arange(E)
    c[:, C_EOFF:C_EOFF + E] = CAP * np.arange(E)
    c[:, C_TILE:C_TILE + NT] = np.arange(NT)
    c[:, C_P1] = p + 1
    c[:, C_DUM] = N + 1 + p
    return c


class Chain:

    def __init__(self, eng, sem, base=0):
        self.eng, self.sem, self.base, self.n = eng, sem, base, 0

    def link(self, ins):
        ins.then_inc(self.sem, 1)
        self.n += 1

    def wait(self):
        self.eng.wait_ge(self.sem, self.base + self.n)

    def step(self, ins):
        self.link(ins)
        self.wait()


class Space:

    def __init__(self, nc, ctx, tag):
        self.nc, self.ctx, self.tag = nc, ctx, tag

    def sb(self, name, shape, dt):
        return self.ctx.enter_context(self.nc.sbuf_tensor(f"{self.tag}_{name}", shape, dt))

    def ps(self, name, shape, dt=F32):
        return self.ctx.enter_context(self.nc.psum_tensor(f"{self.tag}_ps_{name}", shape, dt))

    def sem(self, name):
        return self.ctx.enter_context(self.nc.semaphore(f"{self.tag}_{name}"))


def pair_products(wh, wl, xh, xl):
    return ((wh, xh), (wl, xh), (wh, xl))


def stage_logits(nc, a, keep):
    x0h, x0l, wTh, wTl, scal, cst = keep["x0h"], keep["x0l"], keep["wTh"], keep["wTl"], keep["scal"], keep["cst"]
    with ExitStack() as ctx:
        s = Space(nc, ctx, "lg")
        condT = s.sb("condT", [P, K, BATCH], F32)
        wcond = s.sb("wcond", [P, 2 * K, D], F32)
        wproj = s.sb("wproj", [P, K, D], F32)
        bproj = s.sb("bproj", [P, K], F32)
        uT = s.sb("uT", [P, K, BATCH], F32)
        vT = s.sb("vT", [P, K, BATCH], F32)
        xin = s.sb("xin", [P, 2, K, BLK], F32)
        L = keep["R"][:, 0:K]
        wraw = keep["R"][:].rearrange("p o n -> p (o n)")[:, K * N:K * N + WCOLS]
        wint = s.sb("wint", [P, WCOLS], I16)
        wscale = s.sb("wscale", [P, 4, WCOLS // QBLOCK], F32)
        blkmax = s.sb("blkmax", [P, NB], F32)
        allmax = s.sb("allmax", [P, 2], F32)
        q = s.sb("q", [P, K, BLK], I16)
        ps_set = s.ps("set", [P, BLK])
        ps_L = [[s.ps(f"ps_L{p}{m}", [P, BLK]) for m in range(K)] for p in range(2)]
        ps_w = [s.ps(f"ps_w{i}", [P, BLK]) for i in range(2)]
        d_small, d_w = s.sem("d_small"), s.sem("d_w")
        d_x = [s.sem(f"d_x{i}") for i in range(2)]
        u_mm, u_done, v_mm, v_done = s.sem("u_mm"), s.sem("u_done"), s.sem("v_mm"), s.sem("v_done")
        L_mm, L_read, dq, w_deq = s.sem("L_mm"), s.sem("L_read"), s.sem("dq"), s.sem("w_deq")
        w_tr, w_hi, w_lo = s.sem("w_tr"), s.sem("w_hi"), s.sem("w_lo")
        mx_own, mx_all, sc_own, sc_done = s.sem("mx_own"), s.sem("mx_all"), s.sem("sc_own"), s.sem("sc_done")
        q_done, hi_done, lo_done, pad = s.sem("q_done"), s.sem("hi_done"), s.sem("lo_done"), s.sem("pad")
        NG = WCOLS // BLK

        def source(n):
            if n < 2 * K * FO:
                mat, k, o = n // (K * FO), n % (K * FO) // FO, n % FO
                return (mat * FO + o) * D + k * P
            k, o = (n - 2 * K * FO) // K, n % K
            return 2 * FO * D + o * F + k * P

        with nc.Block() as block:
            @block.sync
            def _(sp):
                sp.dma_start(cst[:], a["consts"]).then_inc(d_small, 16)
                sp.dma_start(condT[:], a["condT"].rearrange("(k p) b -> p k b", p=P)).then_inc(d_small, 16)
                sp.dma_start(wproj[:], a["W_proj"].rearrange("(k p) n -> p k n", p=P)).then_inc(d_small, 16)
                sp.dma_start(wcond[:], a["weight_matrix"].rearrange("(k p) n -> p k n", p=P)).then_inc(d_small, 16)
                sp.dma_start(bproj[:], a["b_proj"]).then_inc(d_small, 16)
                xT = a["xT"].rearrange("(k p) n -> p k n", p=P)
                with sp.Fori(0, NB // 2) as i:
                    for par in range(2):
                        sp.wait_ge(L_mm, 2 * i + par + 1)
                        sp.dma_start(xin[:, par], xT[:, :, bass.ds((2 * i + par) * BLK, BLK)]).then_inc(d_x[par], 16)

            @block.scalar
            def _(act):
                up = wraw[:, 0:FO * D].rearrange("p (o n) -> p o n", o=FO)
                gate = wraw[:, FO * D:2 * FO * D].rearrange("p (o n) -> p o n", o=FO)
                down = wraw[:, 2 * FO * D:].rearrange("p (o n) -> p o n", o=K)
                act.dma_start(up, a["w_up"].rearrange("(o p) n -> p o n", p=P)).then_inc(d_w, 16)
                act.dma_start(gate, a["w_gate"].rearrange("(o p) n -> p o n", p=P)).then_inc(d_w, 16)
                act.dma_start(down, a["w_down"].rearrange("(o p) n -> p o n", p=P)).then_inc(d_w, 16)
                act.wait_ge(u_mm, 1)
                for m in range(K):
                    act.activation(uT[:, m], ps_set[:, m * BATCH:(m + 1) * BATCH], ACT.Gelu,
                                   bias=bproj[:, m:m + 1]).then_inc(u_done, 1)
                act.wait_ge(v_mm, 1)
                act.activation(vT[:], ps_set[:, K * BATCH:2 * K * BATCH], ACT.Copy).then_inc(v_done, 1)
                for g in range(NG):
                    act.wait_ge(w_tr, g + 1)
                    act.activation(wTh[:, g * BLK:(g + 1) * BLK], ps_w[g % 2][:], ACT.Copy).then_inc(w_hi, 1)
                with act.Fori(0, NB) as j:
                    act.wait_ge(q_done, j + 1)
                    act.activation(x0h[:, :, bass.ds(j * BLK, BLK)], q[:],
                                   ACT.Copy).then_inc(hi_done, 1)

            @block.tensor
            def _(pe):
                pe.wait_ge(d_small, 80)
                for m in range(K):
                    for k in range(K):
                        i = pe.matmul(ps_set[:, m * BATCH:(m + 1) * BATCH], wproj[:, k, m * P:(m + 1) * P], condT[:, k],
                                      start=(k == 0), stop=(k == K - 1))
                i.then_inc(u_mm, 1)
                pe.wait_ge(u_done, K)
                for m in range(K):
                    for k in range(K):
                        c0 = (K + m) * BATCH
                        i = pe.matmul(ps_set[:, c0:c0 + BATCH], wcond[:, k, m * P:(m + 1) * P], uT[:, k],
                                      start=(k == 0), stop=(k == K - 1))
                i.then_inc(v_mm, 1)
                pe.sem_inc(L_mm, 2)
                with pe.Fori(0, NB // 2) as i2:
                    for par in range(2):
                        pe.wait_ge(d_x[par], 16 * i2 + 16)
                        pe.wait_ge(L_read, 2 * i2 + par + 1)
                        for m in range(K):
                            for k in range(K):
                                i = pe.matmul(ps_L[par][m][:], wcond[:, K + k, m * P:(m + 1) * P], xin[:, par, k],
                                              start=(k == 0), stop=(k == K - 1))
                        i.then_inc(L_mm, 1)
                pe.wait_ge(w_deq, 1)
                for g in range(NG):
                    if g >= 2:
                        pe.wait_ge(w_lo, g - 1)
                    for n in range(4):
                        c0 = source(4 * g + n)
                        i = pe.transpose(ps_w[g % 2][:, n * P:(n + 1) * P], wraw[:, c0:c0 + P], cst[:, C_ID:C_ID + P])
                    i.then_inc(w_tr, 1)

            @block.gpsimd
            def _(pool):
                pool.memset(x0h[:, :, N:N + P], 0.0).then_inc(pad, 1)
                pool.memset(x0l[:, :, N:N + P], 0.0).then_inc(pad, 1)
                pool.wait_ge(mx_own, 1)
                pool.partition_all_reduce(allmax[:, 1:2], allmax[:, 0:1], P, bass.bass_isa.ReduceOp.max).then_inc(mx_all, 1)
                pool.wait_ge(pad, 2)

            @block.vector
            def _(dve):
                c = Chain(dve, dq)
                dve.sem_inc(L_read, 2)
                dve.wait_ge(d_w, 48)
                w3 = wraw.rearrange("p (g n) -> p g n", n=QBLOCK)
                i3 = wint[:].rearrange("p (g n) -> p g n", n=QBLOCK)
                wide = [P, WCOLS // QBLOCK, QBLOCK]
                c.step(dve.tensor_reduce(wscale[:, 0], w3, X, ALU.max, apply_absolute_value=True))
                c.step(dve.tensor_scalar(wscale[:, 1], wscale[:, 0], 1.0 / 7.0, TINY, ALU.mult, ALU.max))
                c.step(dve.reciprocal(wscale[:, 2], wscale[:, 1]))
                c.step(dve.tensor_scalar(wscale[:, 3], wscale[:, 1], SC, None, ALU.mult))
                c.step(dve.tensor_tensor(w3, w3, wscale[:, 2].unsqueeze(2).to_broadcast(wide), ALU.mult))
                c.step(dve.tensor_scalar(wint[:], wraw, 7.0, -8.0, ALU.min, ALU.max))
                dve.tensor_tensor(w3, i3, wscale[:, 3].unsqueeze(2).to_broadcast(wide), ALU.mult).then_inc(w_deq, 1)
                dve.wait_ge(v_done, 1)
                with dve.Fori(0, NB // 2) as i2:
                    for par in range(2):
                        j = 2 * i2 + par
                        dve.wait_ge(L_mm, j + 3)
                        for m in range(K):
                            out = L[:, m, bass.ds(j * BLK, BLK)].rearrange("p (t b) -> p t b", b=BATCH)
                            o = dve.tensor_tensor(out, ps_L[par][m][:].rearrange("p (t b) -> p t b", b=BATCH),
                                                  vT[:, m].unsqueeze(1).to_broadcast([P, BLK // BATCH, BATCH]), ALU.add)
                        o.then_inc(L_read, 1)
                        dve.wait_ge(L_read, j + 3)
                        dve.tensor_reduce(blkmax[:, bass.ds(j, 1)], L[:, :, bass.ds(j * BLK, BLK)], mybir.AxisListType.XY, ALU.max,
                                          apply_absolute_value=True).then_inc(sc_own, 1)
                for g in range(NG):
                    dve.wait_ge(w_hi, g + 1)
                    dve.tensor_tensor(wTl[:, g * BLK:(g + 1) * BLK], ps_w[g % 2][:], wTh[:, g * BLK:(g + 1) * BLK],
                                      ALU.subtract).then_inc(w_lo, 1)
                dve.wait_ge(sc_own, NB)
                dve.tensor_reduce(allmax[:, 0:1], blkmax[:], X, ALU.max).then_inc(mx_own, 1)
                dve.wait_ge(mx_all, 1)
                c = Chain(dve, sc_done)
                c.step(dve.tensor_scalar(scal[:, S_X:S_X + 1], allmax[:, 1:2], 1.0 / QMAX, TINY, ALU.mult, ALU.max))
                c.step(dve.reciprocal(scal[:, S_TMP:S_TMP + 1], scal[:, S_X:S_X + 1]))
                dve.sem_inc(lo_done, 1)
                with dve.Fori(0, NB) as j:
                    dve.wait_ge(lo_done, j + 1)
                    dve.tensor_scalar(q[:], L[:, :, bass.ds(j * BLK, BLK)], scal[:, S_TMP:S_TMP + 1], QMAX, ALU.mult,
                                      ALU.min).then_inc(q_done, 1)
                    dve.wait_ge(hi_done, j + 1)
                    dve.tensor_tensor(x0l[:, :, bass.ds(j * BLK, BLK)], q[:], x0h[:, :, bass.ds(j * BLK, BLK)],
                                      ALU.subtract).then_inc(lo_done, 1)


(S_X, S_TMP, S_PU, S_PG, S_UP, S_GATE, S_CUP, S_CGATE, S_G2, S_C2, S_O, S_CO, S_XU, S_ALLU, S_ALLG, S_US2, S_DN, S_R, S_G65,
 S_MXA, S_MXB, S_END) = range(22)


def column(scal, n):
    return scal[:, n:n + 1]


def stage_gate_up(nc, a, keep):
    x0h, x0l, wTh, wTl, scal = keep["x0h"], keep["x0l"], keep["wTh"], keep["wTl"], keep["scal"]
    qup, R = keep["qup"], keep["R"]
    RING = 6
    with ExitStack() as ctx:
        s = Space(nc, ctx, "gu")
        unitmax = s.sb("unitmax", [P, 2, NB, FO], F32)
        rmax = s.sb("rmax", [P, NB * FO], F32)
        gq = [s.sb(f"gq{i}", [P, BLK], I16) for i in range(2)]
        sg = [s.sb(f"sg{i}", [P, BLK], F32) for i in range(2)]
        sq = [s.sb(f"sq{i}", [P, BLK], U16) for i in range(2)]
        ps = [s.ps(f"p{i}", [P, BLK]) for i in range(RING)]
        mm0, rd_up, rd_gate, mm1, rd1 = s.sem("mm0"), s.sem("rd_up"), s.sem("rd_gate"), s.sem("mm1"), s.sem("rd1")
        upmax, own_max, all_max = s.sem("upmax"), s.sem("own_max"), s.sem("all_max")
        v_sc, sc_ready, sig_done, R_done, rm, sq_done, r_all, up_int = (
            s.sem(n) for n in ("v_sc", "sc_ready", "sig_done", "R_done", "rm", "sq_done", "r_all", "up_int"))

        def unit(pe, j, mat, o, bank, done):
            n = 0
            cols = bass.ds(j * BLK, BLK)
            for k in range(K):
                w0 = (mat * K + k) * F + o * P
                for w, x in pair_products(wTh[:, w0:w0 + P], wTl[:, w0:w0 + P], x0h[:, k, cols], x0l[:, k, cols]):
                    ins = pe.matmul(ps[bank][:], w, x, start=(n == 0), stop=(n == 3 * K - 1))
                    n += 1
            ins.then_inc(done, 1)

        with nc.Block() as block:
            @block.tensor
            def _(pe):
                with pe.Fori(0, NB) as j:
                    for o in range(FO):
                        pe.wait_ge(rd_up, FO * j + o + 1)
                        unit(pe, j, 0, o, 2 * o % RING, mm0)
                        pe.wait_ge(rd_gate, FO * j + o + 1)
                        unit(pe, j, 1, o, (2 * o + 1) % RING, mm0)
                pe.wait_ge(rd_up, NB * FO + RING // 2)
                pe.wait_ge(rd_gate, NB * FO + RING // 2)
                with pe.Fori(0, NB) as j:
                    for o in range(FO):
                        pe.wait_ge(rd1, FO * j + o + 1)
                        unit(pe, j, 1, o, o, mm1)

            @block.gpsimd
            def _(pool):
                pool.wait_ge(own_max, 1)
                pool.partition_all_reduce(scal[:, S_ALLU:S_ALLG + 1], scal[:, S_PU:S_PG + 1], P,
                                          bass.bass_isa.ReduceOp.max).then_inc(all_max, 1)
                pool.wait_ge(r_all, 1)
                pool.partition_all_reduce(column(scal, S_MXB), column(scal, S_MXA), P,
                                          bass.bass_isa.ReduceOp.max).then_inc(all_max, 1)

            @block.scalar
            def _(act):
                act.sem_inc(rd_up, RING // 2)
                act.sem_inc(rd1, RING)
                with act.Fori(0, NB) as j:
                    for o in range(FO):
                        act.wait_ge(mm0, 2 * (FO * j + o) + 1)
                        act.activation(R[:, o, bass.ds(j * BLK, BLK)], ps[2 * o % RING][:], ACT.Copy).then_inc(rd_up, 1)
                act.wait_ge(sc_ready, 1)
                with act.Fori(0, NB) as j:
                    cols = bass.ds(j * BLK, BLK)
                    act.activation(qup[:, 0:FO // 2, cols], R[:, 0:FO // 2, cols], ACT.Copy, scale=column(scal, S_CUP)).then_inc(up_int, 1)
                    for o in range(FO):
                        g = o % 2
                        act.wait_ge(mm1, FO * j + o + 1)
                        act.wait_ge(R_done, FO * j + o + 1)
                        act.activation(gq[g][:], ps[o][:], ACT.Copy, scale=column(scal, S_CGATE)).then_inc(rd1, 1)
                        act.wait_ge(rd1, FO * j + o + RING + 1)
                        act.activation(sg[g][:], gq[g][:], ACT.Sigmoid, scale=column(scal, S_GATE)).then_inc(sig_done, 1)

            @block.vector
            def _(dve):
                dve.sem_inc(rd_gate, RING // 2)
                dve.sem_inc(R_done, 2)
                with dve.Fori(0, NB) as j:
                    for o in range(FO):
                        dve.wait_ge(rd_up, FO * j + o + 1 + RING // 2)
                        dve.tensor_reduce(unitmax[:, 0, bass.ds(j, 1), o:o + 1], R[:, o, bass.ds(j * BLK, BLK)], X, ALU.max,
                                          apply_absolute_value=True).then_inc(upmax, 1)
                        dve.wait_ge(mm0, 2 * (FO * j + o) + 2)
                        dve.tensor_reduce(unitmax[:, 1, bass.ds(j, 1), o:o + 1], ps[(2 * o + 1) % RING][:], X, ALU.max,
                                          apply_absolute_value=True).then_inc(rd_gate, 1)
                dve.wait_ge(upmax, NB * FO)
                dve.wait_ge(rd_gate, RING // 2 + NB * FO)
                dve.tensor_reduce(scal[:, S_PU:S_PG + 1], unitmax[:], mybir.AxisListType.XY, ALU.max).then_inc(own_max, 1)
                dve.wait_ge(all_max, 1)
                c = Chain(dve, v_sc)
                c.step(dve.tensor_scalar(column(scal, S_XU), column(scal, S_X), 1.0 / SC, None, ALU.mult))
                c.step(dve.tensor_scalar(scal[:, S_UP:S_GATE + 1], scal[:, S_ALLU:S_ALLG + 1], column(scal, S_XU), 1.0 / QMAX,
                                         ALU.mult, ALU.mult))
                c.step(dve.tensor_scalar(scal[:, S_UP:S_GATE + 1], scal[:, S_UP:S_GATE + 1], TINY, None, ALU.max))
                c.step(dve.reciprocal(scal[:, S_CUP:S_CGATE + 1], scal[:, S_UP:S_GATE + 1]))
                c.step(dve.tensor_scalar(scal[:, S_CUP:S_CGATE + 1], scal[:, S_CUP:S_CGATE + 1], column(scal, S_XU), None, ALU.mult))
                dve.tensor_scalar(column(scal, S_G65), column(scal, S_GATE), 1.0 / 65536.0, None, ALU.mult).then_inc(sc_ready, 1)
                dve.wait_ge(sc_ready, 1)
                with dve.Fori(0, NB) as j:
                    cols = bass.ds(j * BLK, BLK)
                    dve.tensor_scalar(qup[:, FO // 2:FO, cols], R[:, FO // 2:FO, cols], column(scal, S_CUP), QMAX, ALU.mult, ALU.min)
                    for o in range(FO):
                        g = o % 2
                        n = FO * j + o
                        dve.wait_ge(sig_done, n + 1)
                        dve.tensor_scalar(sq[g][:], sg[g][:], 65536.0, 65535.0, ALU.mult, ALU.min).then_inc(sq_done, 1)
                        if o == 0:
                            dve.wait_ge(up_int, j + 1)
                        dve.wait_ge(sq_done, n + 1)
                        dve.tensor_tensor(R[:, o, cols], gq[g][:], sq[g][:], ALU.mult).then_inc(R_done, 1)
                        dve.wait_ge(R_done, n + 3)
                        dve.tensor_reduce(rmax[:, bass.ds(n, 1)], R[:, o, cols], X, ALU.max, apply_absolute_value=True).then_inc(rm, 1)
                dve.wait_ge(rm, NB * FO)
                dve.tensor_reduce(column(scal, S_MXA), rmax[:], X, ALU.max).then_inc(r_all, 1)
                dve.wait_ge(all_max, 2)
                c.step(dve.tensor_scalar(column(scal, S_G2), column(scal, S_MXB), column(scal, S_G65), 1.0 / QMAX, ALU.mult, ALU.mult))
                c.step(dve.tensor_scalar(column(scal, S_G2), column(scal, S_G2), TINY, None, ALU.max))
                c.step(dve.reciprocal(column(scal, S_R), column(scal, S_G2)))
                c.step(dve.tensor_tensor(column(scal, S_C2), column(scal, S_R), column(scal, S_G65), ALU.mult))
                c.step(dve.tensor_tensor(column(scal, S_US2), column(scal, S_G2), column(scal, S_UP), ALU.mult))


def stage_product(nc, a, keep):
    scal, qup, R = keep["scal"], keep["qup"], keep["R"]
    PIECE = 1536
    NP = FO * N // PIECE
    with ExitStack() as ctx:
        s = Space(nc, ctx, "pr")
        q2 = [s.sb(f"q2{i}", [P, PIECE], I16) for i in range(2)]
        pmax = s.sb("pmax", [P, NP], F32)
        q2_done, p_done, pm, all_own, all_max, v_sc = (s.sem(n) for n in ("q2_done", "p_done", "pm", "all_own", "all_max", "v_sc"))
        Rf = R[:].rearrange("p o n -> p (o n)")
        uf = qup[:].rearrange("p o n -> p (o n)")
        with nc.Block() as block:
            @block.scalar
            def _(act):
                with act.Fori(0, NP // 2) as i:
                    for par in range(2):
                        n = 2 * i + par
                        act.wait_ge(p_done, n + 1)
                        act.activation(q2[par][:], Rf[:, bass.ds(n * PIECE, PIECE)], ACT.Copy,
                                       scale=column(scal, S_C2)).then_inc(q2_done, 1)

            @block.gpsimd
            def _(pool):
                pool.wait_ge(all_own, 1)
                pool.partition_all_reduce(column(scal, S_MXB), column(scal, S_MXA), P,
                                          bass.bass_isa.ReduceOp.max).then_inc(all_max, 1)

            @block.vector
            def _(dve):
                dve.sem_inc(p_done, 2)
                with dve.Fori(0, NP // 2) as i:
                    for par in range(2):
                        n = 2 * i + par
                        cols = bass.ds(n * PIECE, PIECE)
                        dve.wait_ge(q2_done, n + 1)
                        dve.tensor_tensor(Rf[:, cols], q2[par][:], uf[:, cols], ALU.mult).then_inc(p_done, 1)
                        dve.wait_ge(p_done, n + 3)
                        dve.tensor_reduce(pmax[:, bass.ds(n, 1)], Rf[:, cols], X, ALU.max, apply_absolute_value=True).then_inc(pm, 1)
                dve.wait_ge(pm, NP)
                dve.tensor_reduce(column(scal, S_MXA), pmax[:], X, ALU.max).then_inc(all_own, 1)
                dve.wait_ge(all_max, 1)
                c = Chain(dve, v_sc)
                c.step(dve.tensor_scalar(column(scal, S_O), column(scal, S_MXB), column(scal, S_US2), 1.0 / QMAX, ALU.mult, ALU.mult))
                c.step(dve.tensor_scalar(column(scal, S_O), column(scal, S_O), TINY, None, ALU.max))
                c.step(dve.reciprocal(column(scal, S_R), column(scal, S_O)))
                c.step(dve.tensor_tensor(column(scal, S_CO), column(scal, S_R), column(scal, S_US2), ALU.mult))
                c.step(dve.tensor_scalar(column(scal, S_DN), column(scal, S_O), 1.0 / SC, None, ALU.mult))


GATES = 3
SHARED = 3 * BLK


def gru_operands(keep):
    def view(o, start, shape, dt=F32):
        width = int(np.prod(shape)) // (2 if dt is F16 else 1)
        assert start + width <= SHARED
        flat = keep["R"][:, o, start:start + width]
        names = " ".join("abcd"[:len(shape)])
        return (flat.bitcast(F16) if dt is F16 else flat).rearrange(f"p ({names}) -> p {names}", **dict(zip("abcd", shape)))

    weight = (GATES, K, D)
    keep["raw"] = [view(n, 0, weight) for n in range(2)]
    keep["cond_w"] = view(2, 0, weight)
    keep["wh"], keep["wl"] = (view(o, 0, (2,) + weight, F16) for o in (3, 4))
    share = (GATES * K, BATCH)
    keep["vf"], keep["vh"], keep["vl"] = view(5, 0, share), view(5, 96, share, F16), view(5, 144, share, F16)
    keep["idsc"], keep["condT"], keep["bias"] = view(5, 192, (P,), F16), view(5, 256, (K, BATCH)), view(5, 288, (GATES * K,))
    keep["gwraw"], keep["gwh"], keep["gwl"] = view(5, 296, (K, E)), view(5, 312, (K, E), F16), view(5, 320, (K, E), F16)


def stage_down(nc, a, keep):
    raw, cond_w, wh, wl, condT, bias, gwraw, gwh, gwl, idh, idsc, vf, vh, vl = (
        keep[n] for n in ("raw", "cond_w", "wh", "wl", "condT", "bias", "gwraw", "gwh", "gwl", "idh", "idsc", "vf", "vh", "vl"))
    x1h, x1l, wTh, wTl, scal, R, cst = (keep[n] for n in ("x0h", "x0l", "wTh", "wTl", "scal", "R", "cst"))
    D0 = 2 * K * F
    with ExitStack() as ctx:
        s = Space(nc, ctx, "dn")
        xin = [s.sb(f"xin{i}", [P, K, BLK], F32) for i in range(2)]
        qo = s.sb("qo", [P, FO, BLK], I16)
        qh = [s.sb(f"qh{i}", [P, FO, BLK], F16) for i in range(2)]
        ql = [s.sb(f"ql{i}", [P, FO, BLK], F16) for i in range(2)]
        x1 = [s.sb(f"x1{i}", [P, K, BLK], F32) for i in range(2)]
        rows = s.sb("rows", [P, 4, D], F32)
        ps_d = [[s.ps(f"d{p}{m}", [P, BLK]) for m in range(K)] for p in range(2)]
        ps_t = [s.ps(f"t{i}", [P, 2, D]) for i in range(2)]
        ps_v = s.ps("v", [P, BLK])
        d_g, d_c, g_hi, g_scaled, g_lo, bias_sc, v_mm, v_done = (
            s.sem(n) for n in ("d_g", "d_c", "g_hi", "g_scaled", "g_lo", "bias_sc", "v_mm", "v_done"))
        d_x = [s.sem(f"d_x{i}") for i in range(2)]
        d_out, stored = s.sem("d_out"), s.sem("stored")
        qo_done, qh_done, ql_done, mm, x1_done, hi_done, lo_done, tr, rows_done = (
            s.sem(n) for n in ("qo_done", "qh_done", "ql_done", "mm", "x1_done", "hi_done", "lo_done", "tr", "rows_done"))

        def blocks(eng, one):
            one(0, 0)
            with eng.Fori(0, (NB - 4) // 2) as i:
                one(2 * i + 1, 1)
                one(2 * i + 2, 0)
            for j in range(NB - 3, NB):
                one(j, j % 2)

        def before(j, n):
            return not isinstance(j, int) or j + n < NB

        with nc.Block() as block:
            @block.sync
            def _(sp):
                xT = a["xT"].rearrange("(k p) n -> p k n", p=P)
                sp.sem_inc(stored, 1)
                sp.dma_start(a["out"][N:N + DUMMY, :], cst[:, 0:D]).then_inc(d_out, 16)
                sp.wait_ge(d_out, 16)
                for par in range(2):
                    sp.dma_start(xin[par][:], xT[:, :, par * BLK:(par + 1) * BLK]).then_inc(d_x[par], 16)

                def one(j, par):
                    sp.wait_ge(rows_done, j + 2)
                    sp.dma_start(a["out"][bass.ds(j * BLK, BLK), :].rearrange("(c p) n -> p c n", p=P), rows[:]).then_inc(d_out, 16)
                    if before(j, 2):
                        sp.wait_ge(x1_done, j + 1)
                        sp.dma_start(xin[par][:], xT[:, :, bass.ds((j + 2) * BLK, BLK)]).then_inc(d_x[par], 16)
                    sp.wait_ge(d_out, 16 * j + 32)
                    sp.sem_inc(stored, 1)
                blocks(sp, one)

            @block.scalar
            def _(act):
                def integers(j):
                    act.wait_ge(ql_done, j + 1)
                    act.activation(qo[:], R[:, :, bass.ds(j * BLK, BLK)], ACT.Copy, scale=column(scal, S_CO)).then_inc(qo_done, 1)

                def rows_out(j):
                    act.wait_ge(tr, j + 2)
                    act.wait_ge(stored, j + 1)
                    for h in range(2):
                        r = act.activation(rows[:, 2 * h:2 * h + 2], ps_t[h][:], ACT.Copy)
                    r.then_inc(rows_done, 1)

                def one(j, par):
                    if before(j, 2):
                        integers(j + 2)
                    act.wait_ge(x1_done, j + 1)
                    act.activation(x1h[:, :, bass.ds(j * BLK, BLK)], x1[par][:], ACT.Copy, scale=SC).then_inc(hi_done, 1)
                    if isinstance(j, int) and j == NB - 2:
                        act.wait_ge(v_mm, 1)
                        act.wait_ge(bias_sc, 1)
                        for n in range(GATES * K):
                            act.activation(vf[:, n], ps_v[:, n * BATCH:(n + 1) * BATCH], ACT.Identity, scale=SC,
                                           bias=bias[:, n:n + 1]).then_inc(v_done, 1)
                    if not isinstance(j, int) or j > 0:
                        rows_out(j - 1)

                act.sem_inc(rows_done, 1)
                integers(0)
                integers(1)
                blocks(act, one)
                rows_out(NB - 1)

            @block.gpsimd
            def _(pool):
                pool.wait_ge(qo_done, SHARED // BLK)
                pool.dma_start(condT[:], a["condT"].rearrange("(k p) b -> p k b", p=P)).then_inc(d_c, 16)
                pool.dma_start(bias[:], a["b_gru"]).then_inc(d_c, 16)
                pool.dma_start(gwraw[:], a["gate_w"].rearrange("(k p) e -> p k e", p=P)).then_inc(d_c, 16)
                pool.tensor_copy(idh[:], cst[:, C_ID:C_ID + P]).then_inc(g_hi, 1)
                pool.tensor_scalar(idsc[:], cst[:, C_ID:C_ID + P], SC, None, ALU.mult).then_inc(g_hi, 1)
                for g in range(GATES):
                    pool.dma_start(cond_w[:, g], a["C_gru"][g].rearrange("(k p) n -> p k n", p=P)).then_inc(d_c, 16)
                for g in range(GATES):
                    pool.dma_start(raw[0][:, g], a["U_gru"][g].rearrange("(k p) n -> p k n", p=P)).then_inc(d_g, 16)
                    pool.dma_start(raw[1][:, g], a["W_gru"][g].rearrange("(k p) n -> p k n", p=P)).then_inc(d_g, 16)
                pool.wait_ge(d_c, 48 + 16 * GATES)
                pool.tensor_scalar(bias[:], bias[:], SC, None, ALU.mult).then_inc(bias_sc, 1)
                pool.wait_ge(d_g, 32 * GATES)
                parts = [(raw[0], wh[:, 0], wl[:, 0]), (raw[1], wh[:, 1], wl[:, 1]), (gwraw[:], gwh[:], gwl[:])]
                for full, high, low in parts:
                    pool.tensor_scalar(high, full, SC, None, ALU.mult).then_inc(g_hi, 1)
                pool.wait_ge(g_hi, 2 + len(parts))
                for full, high, low in parts:
                    pool.tensor_scalar(full, full, SC, None, ALU.mult).then_inc(g_scaled, 1)
                for n, (full, high, low) in enumerate(parts):
                    pool.wait_ge(g_scaled, n + 1)
                    pool.tensor_tensor(low, full, high, ALU.subtract).then_inc(g_lo, 1)
                pool.wait_ge(v_done, GATES * K)
                pool.tensor_copy(vh[:], vf[:]).then_inc(g_hi, 1)
                pool.wait_ge(g_hi, 3 + len(parts))
                pool.tensor_tensor(vl[:], vf[:], vh[:], ALU.subtract).then_inc(g_lo, 1)
                pool.wait_ge(g_lo, len(parts) + 1)

            @block.tensor
            def _(pe):
                def rows_back(j, par):
                    pe.wait_ge(x1_done, j + 1)
                    pe.wait_ge(rows_done, j + 1)
                    for c in range(4):
                        for k in range(K):
                            ins = pe.transpose(ps_t[c // 2][:, c % 2, k * P:(k + 1) * P], x1[par][:, k, c * P:(c + 1) * P],
                                               cst[:, C_ID:C_ID + P])
                    ins.then_inc(tr, 1)

                def one(j, par):
                    pe.wait_ge(ql_done, j + 2)
                    for m in range(K):
                        n = 0
                        for k in range(FO):
                            w0 = D0 + k * D + m * P
                            for w, x in pair_products(wTh[:, w0:w0 + P], wTl[:, w0:w0 + P], qh[par][:, k], ql[par][:, k]):
                                ins = pe.matmul(ps_d[par][m][:], w, x, start=(n == 0), stop=(n == 3 * FO - 1))
                                n += 1
                    ins.then_inc(mm, 1)
                    if not isinstance(j, int) or j > 0:
                        rows_back(j - 1, 1 - par)
                    if isinstance(j, int) and j == NB - 3:
                        pe.wait_ge(d_c, 48 + 16 * GATES)
                        for g in range(GATES):
                            for m in range(K):
                                for k in range(K):
                                    c0 = (g * K + m) * BATCH
                                    ins = pe.matmul(ps_v[:, c0:c0 + BATCH], cond_w[:, g, k, m * P:(m + 1) * P], condT[:, k],
                                                    start=(k == 0), stop=(k == K - 1))
                        ins.then_inc(v_mm, 1)

                pe.sem_inc(mm, 1)
                pe.sem_inc(tr, 1)
                blocks(pe, one)
                rows_back(NB - 1, (NB - 1) % 2)

            @block.vector
            def _(dve):
                def split(j, par):
                    dve.wait_ge(qo_done, j + 1)
                    if not isinstance(j, int) or j > 0:
                        dve.wait_ge(mm, j)
                    dve.tensor_copy(qh[par][:], qo[:]).then_inc(qh_done, 1)
                    dve.wait_ge(qh_done, j + 1)
                    dve.tensor_tensor(ql[par][:], qo[:], qh[par][:], ALU.subtract).then_inc(ql_done, 1)

                def one(j, par):
                    if before(j, 1):
                        split(j + 1, 1 - par)
                    dve.wait_ge(mm, j + 2)
                    dve.wait_ge(d_x[par], 8 * (j - par) + 16)
                    dve.wait_ge(tr, j if not isinstance(j, int) else max(j, 1))
                    for m in range(K):
                        o = dve.scalar_tensor_tensor(out=x1[par][:, m], in0=ps_d[par][m][:], scalar=column(scal, S_DN),
                                                     in1=xin[par][:, m], op0=ALU.mult, op1=ALU.add)
                    o.then_inc(x1_done, 1)
                    dve.wait_ge(x1_done, j + 1)
                    dve.wait_ge(hi_done, j + 1)
                    dve.scalar_tensor_tensor(out=x1l[:, :, bass.ds(j * BLK, BLK)], in0=x1[par][:], scalar=SC,
                                             in1=x1h[:, :, bass.ds(j * BLK, BLK)], op0=ALU.mult, op1=ALU.subtract)\
                       .then_inc(lo_done, 1)

                dve.sem_inc(ql_done, 1)
                split(0, 0)
                blocks(dve, one)
                dve.wait_ge(lo_done, NB)


def stage_gru(nc, a, keep):
    x1h, x1l, cst, Lg = keep["x0h"], keep["x0l"], keep["cst"], keep["Lg"]
    table = keep["table"]
    G = GATES
    R_, Z_, C_ = range(G)
    NC2 = NT // 2
    with ExitStack() as ctx:
        s = Space(nc, ctx, "gru")
        wh, wl, gwh, gwl, idh, idsc, vh, vl = (keep[n] for n in ("wh", "wl", "gwh", "gwl", "idh", "idsc", "vh", "vl"))
        xc = [s.sb(f"xc{p}", [P, 2, K, P], F16) for p in range(2)]
        hh = [s.sb(f"hh{p}", [P, K, P], F16) for p in range(2)]
        hl = [s.sb(f"hl{p}", [P, K, P], F16) for p in range(2)]
        Hf = s.sb("Hf", [P, K, BATCH], F32)
        r, z, th, rv, zc, av, mv = (s.sb(n, [P, K, BATCH], F32) for n in ("r", "z", "th", "rv", "zc", "av", "mv"))
        rhh, rhl = s.sb("rhh", [P, K, BATCH], F16), s.sb("rhl", [P, K, BATCH], F16)
        rows = [s.sb(f"rows{p}", [P, 2 * D], F16) for p in range(2)]
        psg = [[s.ps(f"g{g}{p}", [P, BLK]) for p in range(2)] for g in range(G)]
        ps_t = s.ps("t", [P, 2 * BLK], F16)
        ps_l = s.ps("l", [P, BLK])
        d_tab, rows_free = s.sem("d_tab"), s.sem("rows_free")
        xc_ready, proj_done = s.sem("xc_ready"), s.sem("proj_done")
        r_mm, z_mm, c_mm, r_done, z_done, t_done = (s.sem(n) for n in ("r_mm", "z_mm", "c_mm", "r_done", "z_done", "t_done"))
        rh_hi, rh_lo, h_hi, h_lo, dv = (s.sem(n) for n in ("rh_hi", "rh_lo", "h_hi", "h_lo", "dv"))
        tile_mm, lg_read, row_done, init = s.sem("tile_mm"), s.sem("lg_read"), s.sem("row_done"), s.sem("init")

        def cols(step):
            return slice(step * BATCH, (step + 1) * BATCH)

        with nc.Block() as block:
            @block.sync
            def _(sp):
                sp.sem_inc(rows_free, 2)
                with sp.Fori(0, NC2) as i:
                    for par in range(2):
                        c = 2 * i + par
                        sp.wait_ge(row_done, c + 2)
                        sp.dma_start(table[bass.ds(c * P, P), 0:2 * D], rows[par][:].bitcast(U16)).then_inc(d_tab, 16)
                        sp.wait_ge(d_tab, 16 * c + 16)
                        sp.sem_inc(rows_free, 1)
                sp.wait_ge(row_done, NT + 2)
                sp.dma_start(table[NT * P:(NT + 1) * P, 0:2 * D], rows[0][:].bitcast(U16)).then_inc(d_tab, 16)
                sp.wait_ge(d_tab, 16 * (NT + 1))

            @block.gpsimd
            def _(pool):
                def fetch(c, par):
                    pool.tensor_copy(xc[par][:, 0], x1h[:, :, bass.ds(c * P, P)])
                    pool.tensor_copy(xc[par][:, 1], x1l[:, :, bass.ds(c * P, P)]).then_inc(xc_ready, 1)
                fetch(0, 0)
                with pool.Fori(0, NC2) as i:
                    for par in range(2):
                        c = 2 * i + par
                        pool.wait_ge(proj_done, c + 1)
                        fetch(c + 1, 1 - par)

            @block.tensor
            def _(pe):
                def share_of_x(par, lo, hi):
                    n = 0
                    for g in range(G):
                        for m in range(K):
                            out = psg[g][par][:, m * P:(m + 1) * P]
                            ms = slice(m * P, (m + 1) * P)
                            todo = [(w, x) for k in range(K) for w, x in
                                    pair_products(wh[:, 1, g, k, ms], wl[:, 1, g, k, ms], xc[par][:, 0, k], xc[par][:, 1, k])]
                            for v in (vh, vl):
                                todo.append((idsc[:], v[:, g * K + m].unsqueeze(1).to_broadcast([P, TILE_STEPS, BATCH])))
                            for j, (w, x) in enumerate(todo):
                                if lo <= n < hi:
                                    o = out.rearrange("p (t b) -> p t b", b=BATCH) if j >= 3 * K else out
                                    ins = pe.matmul(o, w, x, start=(m == 0 and j == 0), stop=True, skip_group_check=True)
                                n += 1
                    if hi == n:
                        ins.then_inc(proj_done, 1)

                def recurrence(g, par, step, high, low, low_ready):
                    outs = [psg[g][par][:, m * P + step * BATCH:m * P + (step + 1) * BATCH] for m in range(K)]
                    for m in range(K):
                        for k in range(K):
                            for w in (wh, wl):
                                pe.matmul(outs[m], w[:, 0, g, k, m * P:(m + 1) * P], high(k), start=False, stop=True,
                                          skip_group_check=True)
                    if low_ready:
                        pe.wait_ge(*low_ready)
                    for m in range(K):
                        for k in range(K):
                            ins = pe.matmul(outs[m], wh[:, 0, g, k, m * P:(m + 1) * P], low(k), start=False, stop=True,
                                            skip_group_check=True)
                    return ins

                def finished_tile(par):
                    for q, h in enumerate((hh[par], hl[par])):
                        for k in range(K):
                            pe.transpose(ps_t[:, (q * K + k) * P:(q * K + k + 1) * P], h[:, k], idh[:])
                    n = 0
                    for k in range(K):
                        for h, w in ((hh, gwh), (hl, gwh), (hh, gwl)):
                            ins = pe.matmul(ps_l[:, 0:E], h[par][:, k], w[:, k], start=(n == 0), stop=(n == 3 * K - 1))
                            n += 1
                    ins.then_inc(tile_mm, 1)

                pe.sem_inc(proj_done, 1)
                pe.wait_ge(xc_ready, 1)
                share_of_x(0, 0, 48)
                with pe.Fori(0, NC2) as i:
                    for par in range(2):
                        c = 2 * i + par
                        for st in range(TILE_STEPS):
                            t = TILE_STEPS * c + st
                            hp, hc = (par, cols(st - 1)) if st else (1 - par, cols(TILE_STEPS - 1))
                            pe.wait_ge(h_hi, t + 1)
                            recurrence(R_, par, st, lambda k: hh[hp][:, k, hc], lambda k: hl[hp][:, k, hc], (h_lo, t + 1))\
                                .then_inc(r_mm, 1)
                            recurrence(Z_, par, st, lambda k: hh[hp][:, k, hc], lambda k: hl[hp][:, k, hc], None)\
                                .then_inc(z_mm, 1)
                            pe.wait_ge(rh_hi, t + 1)
                            recurrence(C_, par, st, lambda k: rhh[:, k], lambda k: rhl[:, k], (rh_lo, t + 1)).then_inc(c_mm, 1)
                            if st == 0:
                                pe.wait_ge(xc_ready, c + 2)
                            if st == 1:
                                pe.wait_ge(lg_read, c + 1)
                                pe.wait_ge(row_done, c + 1)
                                finished_tile(1 - par)
                            else:
                                n = st - (st > 1)
                                share_of_x(1 - par, 7 * n, min(7 * n + 7, 48))
                pe.wait_ge(h_lo, STEPS + 1)
                pe.wait_ge(h_hi, STEPS + 1)
                pe.wait_ge(lg_read, NT + 1)
                pe.wait_ge(row_done, NT + 1)
                finished_tile(1)

            @block.scalar
            def _(act):
                def gate(g, par, st):
                    return psg[g][par][:, 0:K * P].rearrange("p (m t b) -> p m t b", m=K, b=BATCH)[:, :, st]

                def rows_piece(par, q):
                    return act.activation(rows[par][:, q * P:(q + 1) * P], ps_t[:, q * P:(q + 1) * P], ACT.Copy)

                act.sem_inc(row_done, 1)
                with act.Fori(0, NC2) as i:
                    for par in range(2):
                        c = 2 * i + par
                        for st in range(TILE_STEPS):
                            t = TILE_STEPS * c + st
                            act.wait_ge(r_mm, t + 1)
                            act.activation(r[:], gate(R_, par, st), ACT.Sigmoid, scale=INV2).then_inc(r_done, 1)
                            act.wait_ge(z_mm, t + 1)
                            act.activation(z[:], gate(Z_, par, st), ACT.Sigmoid, scale=INV2).then_inc(z_done, 1)
                            if 2 <= st < 6:
                                if st == 2:
                                    act.wait_ge(tile_mm, c + 1)
                                    act.wait_ge(rows_free, c + 1)
                                p = rows_piece(par, st - 2)
                                if st == 5:
                                    p.then_inc(row_done, 1)
                            act.wait_ge(c_mm, t + 1)
                            act.activation(th[:], gate(C_, par, st), ACT.Tanh, scale=INV2).then_inc(t_done, 1)
                act.wait_ge(tile_mm, NT + 1)
                act.wait_ge(rows_free, NT + 1)
                for q in range(2 * K):
                    p = rows_piece(0, q)
                p.then_inc(row_done, 1)

            @block.vector
            def _(dve):
                dve.memset(Hf[:], 0.0).then_inc(init, 1)
                dve.memset(hh[1][:], 0.0).then_inc(init, 1)
                dve.memset(hl[1][:], 0.0).then_inc(init, 1)
                dve.wait_ge(init, 3)
                dve.sem_inc(h_hi, 1)
                dve.sem_inc(h_lo, 1)
                dve.sem_inc(lg_read, 1)

                def logits(c):
                    dve.wait_ge(tile_mm, c + 1)
                    dve.tensor_scalar(Lg[:, bass.ds(c, 1)], ps_l[:, 0:E].unsqueeze(1), INV2, None, ALU.mult).then_inc(lg_read, 1)

                with dve.Fori(0, NC2) as i:
                    for par in range(2):
                        c = 2 * i + par
                        for st in range(TILE_STEPS):
                            t = TILE_STEPS * c + st
                            dve.wait_ge(r_done, t + 1)
                            dve.tensor_tensor(rhh[:], r[:], Hf[:], ALU.mult).then_inc(rh_hi, 1)
                            dve.tensor_tensor(rv[:], r[:], Hf[:], ALU.mult).then_inc(dv, 1)
                            dve.wait_ge(dv, 5 * t + 1)
                            dve.tensor_tensor(rhl[:], rv[:], rhh[:], ALU.subtract).then_inc(rh_lo, 1)
                            dve.wait_ge(z_done, t + 1)
                            dve.tensor_scalar(zc[:], z[:], -1.0, 1.0, ALU.mult, ALU.add).then_inc(dv, 1)
                            dve.wait_ge(dv, 5 * t + 2)
                            dve.tensor_tensor(av[:], zc[:], Hf[:], ALU.mult).then_inc(dv, 1)
                            if st == 3:
                                logits(c)
                            dve.wait_ge(t_done, t + 1)
                            dve.scalar_tensor_tensor(out=mv[:], in0=z[:], scalar=SC, in1=th[:], op0=ALU.mult, op1=ALU.mult)\
                                .then_inc(dv, 1)
                            dve.wait_ge(dv, 5 * t + 4)
                            dve.tensor_tensor(hh[par][:, :, cols(st)], mv[:], av[:], ALU.add).then_inc(h_hi, 1)
                            dve.tensor_tensor(Hf[:], mv[:], av[:], ALU.add).then_inc(dv, 1)
                            dve.wait_ge(dv, 5 * t + 5)
                            dve.tensor_tensor(hl[par][:, :, cols(st)], Hf[:], hh[par][:, :, cols(st)], ALU.subtract)\
                                .then_inc(h_lo, 1)
                logits(NT)
                dve.wait_ge(lg_read, NT + 2)


def stage_route(nc, a, keep):
    cst, Lg, table, gidx, sidx = keep["cst"], keep["Lg"], keep["table"], keep["gidx"], keep["sidx"]
    NQ = TOPK * NT
    QB = 16
    PAD = NT // 2
    with ExitStack() as ctx:
        s = Space(nc, ctx, "rt")
        M = s.sb("M", [P, TOPK, NT, E], F16)
        best = s.sb("best", [P, TOPK, NT], F32)
        first = s.sb("first", [P, TOPK, NT], F32)
        eq, L2 = s.sb("eq", [P, NT, E], F32), s.sb("L2", [P, NT, E], F32)
        pr = s.sb("pr", [P, 4, NT], F32)
        prob, prob2 = s.sb("prob", [P, NT, E], F32), s.sb("prob2", [P, NT, E], F32)
        masks = s.sb("masks", [P, 4, P], F16)
        total, totalf = s.sb("total", [P, TOPK, E], F16), s.sb("totalf", [P, TOPK, E], F32)
        scan = [s.sb(f"scan{i}", [P, TOPK, PAD + NT + 1, E], F16) for i in range(2)]
        rank, V = s.sb("rank", [P, TOPK, NT, E], F32), s.sb("V", [P, TOPK, NT, E], F32)
        slot, own = s.sb("slot", [P, NQ], F32), s.sb("own", [P, NQ], F32)
        hi_i = s.sb("hi_i", [P, NQ], I16)
        lo = s.sb("lo", [P, NQ], F32)
        io16, lo16, hi16, tile16 = (s.sb(n, [P, w], F16) for n, w in (("io16", P), ("lo16", NQ), ("hi16", NQ), ("tile16", NT)))
        onelo = [s.sb(f"onelo{i}", [P, QB, P], F16) for i in range(2)]
        onehi = s.sb("onehi", [P, QB, SLOT_TILES], F16)
        val = [s.sb(f"val{i}", [P, QB, 2, SLOT_TILES], F16) for i in range(2)]
        I, empty = s.sb("I", [P, SLOT_TILES], F32), s.sb("empty", [P, SLOT_TILES], F32)
        gI = s.sb("gI", [P, SLOT_TILES], F32)
        ps_r, ps_i = s.ps("ps_r", [P, BLK]), s.ps("ps_i", [P, BLK])
        ch, exp_in, exp_done, prob_ready, d_prob = (s.sem(n) for n in ("ch", "exp_in", "exp_done", "prob_ready", "d_prob"))
        count_in, ranked, ones_ready, ones_used = (s.sem(n) for n in ("count_in", "ranked", "ones_ready", "ones_used"))
        fcb, pjb, wst, wh, wl = (keep[n] for n in ("fcb", "pjb", "wst", "ewh", "ewl"))
        d_b, d_w, w_hi, w_scaled, w_lo = (s.sem(n) for n in ("d_b", "d_w", "w_hi", "w_scaled", "w_lo"))
        wide = [P, NT, E]
        L = Lg[:, 1:]
        rounds = [1 << d for d in range(NT.bit_length() - 1)]

        with nc.Block() as block:
            @block.sync
            def _(sp):
                sp.dma_start(wst[0][:], a["c_fc"][0].rearrange("(k p) n -> p k n", p=P)).then_inc(d_w, 16)
                sp.dma_start(wst[1][:], a["c_proj"][0].rearrange("(k p) n -> p k n", p=P)).then_inc(d_w, 16)
                sp.dma_start(fcb[:], a["fc_bias"]).then_inc(d_b, 16)
                sp.dma_start(pjb[:], a["proj_bias"].partition_broadcast(P)).then_inc(d_b, 16)
                sp.wait_ge(d_b, 32)
                sp.wait_ge(prob_ready, 1)
                sp.dma_start(table[P:, 2 * D:].rearrange("(i p) c -> p i c", p=P), prob2[:].bitcast(U16)).then_inc(d_prob, 16)
                sp.wait_ge(d_prob, 16)

            @block.scalar
            def _(act):
                act.wait_ge(exp_in, 1)
                act.activation(pr[:, 1], pr[:, 0], ACT.Exp).then_inc(exp_done, 1)
                act.wait_ge(d_w, 32)
                for j in range(2):
                    act.activation(wh[0][j][:], wst[j][:], ACT.Copy, scale=SC).then_inc(w_hi, 1)
                act.wait_ge(w_hi, 2)
                for j in range(2):
                    act.activation(wst[j][:], wst[j][:], ACT.Copy, scale=SC).then_inc(w_scaled, 1)

            @block.gpsimd
            def _(pool):
                for j in range(2):
                    pool.wait_ge(w_scaled, j + 1)
                    pool.tensor_tensor(wl[0][j][:], wst[j][:], wh[0][j][:], ALU.subtract).then_inc(w_lo, 1)
                pool.wait_ge(w_lo, 2)

            @block.tensor
            def _(pe):
                pe.wait_ge(count_in, 1)
                last = scan[len(rounds) % 2]
                pe.matmul(ps_r[:], masks[:, 2], M[:].rearrange("p k i e -> p (k i e)"), start=True, stop=False, skip_group_check=True)
                for k in range(TOPK):
                    out = ps_r[:, k * NT * E:(k + 1) * NT * E].rearrange("p (i e) -> p i e", e=E)
                    pe.matmul(out, masks[:, 1], last[:, k, PAD:PAD + NT], start=False, stop=False, skip_group_check=True)
                    pe.matmul(out, masks[:, 0], total[:, k].unsqueeze(1).to_broadcast(wide), start=False, stop=False,
                              skip_group_check=True)
                pe.matmul(out, masks[:, 3], total[:, 0].unsqueeze(1).to_broadcast(wide), start=False, stop=True,
                          skip_group_check=True).then_inc(ranked, 1)
                for b in range(NQ // QB):
                    pe.wait_ge(ones_ready, b + 1)
                    for q in range(QB):
                        ins = pe.matmul(ps_i[:, 0:2 * SLOT_TILES], onelo[b % 2][:, q], val[b % 2][:, q].rearrange("p a n -> p (a n)"),
                                        start=(b == 0 and q == 0), stop=(b == NQ // QB - 1 and q == QB - 1))
                    ins.then_inc(ones_used, 1)

            @block.vector
            def _(dve):
                c = Chain(dve, ch)

                def row(col, shape):
                    return cst[:, col:col + E].unsqueeze(1).to_broadcast(shape)

                c.link(dve.tensor_copy(masks[:, 0:3], cst[:, C_BLESS:C_BLESS + 3 * P].rearrange("p (a n) -> p a n", a=3)))
                c.link(dve.memset(masks[:, 3], 1.0))
                for i in range(2):
                    c.link(dve.memset(scan[i][:], 0.0))
                c.link(dve.tensor_copy(io16[:], cst[:, C_IOTA:C_IOTA + P]))
                c.link(dve.tensor_copy(tile16[:], cst[:, C_TILE:C_TILE + NT]))
                for k, src in ((0, L), (1, L2[:])):
                    c.step(dve.tensor_reduce(best[:, k], src, X, ALU.max))
                    c.step(dve.tensor_tensor(eq[:], src, best[:, k].unsqueeze(2).to_broadcast(wide), ALU.is_equal))
                    c.step(dve.tensor_tensor(eq[:], eq[:], row(C_EIDX, wide), ALU.mult))
                    c.step(dve.tensor_reduce(first[:, k], eq[:], X, ALU.max))
                    c.step(dve.tensor_tensor(M[:, k], eq[:], first[:, k].unsqueeze(2).to_broadcast(wide), ALU.is_equal))
                    if k == 0:
                        c.step(dve.scalar_tensor_tensor(out=L2[:], in0=M[:, 0], scalar=-3e38, in1=L, op0=ALU.mult, op1=ALU.add))
                dve.tensor_tensor(pr[:, 0], best[:, 1], best[:, 0], ALU.subtract).then_inc(exp_in, 1)
                c.step(dve.tensor_reduce(totalf[:], M[:].rearrange("p k i e -> p k e i"), X, ALU.add))
                c.link(dve.tensor_copy(total[:], totalf[:]))
                for k in range(TOPK):
                    c.link(dve.tensor_copy(scan[0][:, k, PAD + 1:], M[:, k]))
                c.wait()
                for n, d in enumerate(rounds):
                    for k in range(TOPK):
                        c.link(dve.tensor_tensor(scan[(n + 1) % 2][:, k, PAD:PAD + NT], scan[n % 2][:, k, PAD:PAD + NT],
                                                 scan[n % 2][:, k, PAD - d:PAD + NT - d], ALU.add))
                    c.wait()
                dve.sem_inc(count_in, 1)
                dve.wait_ge(exp_done, 1)
                c.step(dve.tensor_scalar(pr[:, 2], pr[:, 1], 1.0, None, ALU.add))
                c.step(dve.reciprocal(pr[:, 3], pr[:, 2]))
                c.step(dve.tensor_tensor(pr[:, 2], pr[:, 1], pr[:, 3], ALU.mult))
                c.link(dve.tensor_tensor(prob[:], M[:, 0], pr[:, 3].unsqueeze(2).to_broadcast(wide), ALU.mult))
                c.step(dve.tensor_tensor(eq[:], M[:, 1], pr[:, 2].unsqueeze(2).to_broadcast(wide), ALU.mult))
                dve.tensor_tensor(prob2[:], prob[:], eq[:], ALU.add).then_inc(prob_ready, 1)
                dve.wait_ge(ranked, 1)
                c.step(dve.tensor_copy(rank[:].rearrange("p k i e -> p (k i e)"), ps_r[:]))
                rq, Vq, Mq = (x[:].rearrange("p k i e -> p (k i) e") for x in (rank, V, M))
                wq = [P, NQ, E]
                c.step(dve.tensor_tensor(Vq, rq, row(C_EOFF, wq), ALU.add))
                c.step(dve.tensor_tensor(Vq, Vq, Mq, ALU.mult))
                c.link(dve.tensor_reduce(slot[:], Vq, X, ALU.add))
                c.step(dve.tensor_tensor(rq, rq, Mq, ALU.mult))
                c.step(dve.tensor_reduce(own[:], rq, X, ALU.add))
                c.step(dve.tensor_scalar(own[:], own[:], float(CAP), 2.0 * E * CAP, ALU.is_ge, ALU.mult))
                c.step(dve.tensor_tensor(slot[:], slot[:], own[:], ALU.add))
                c.step(dve.tensor_scalar(hi_i[:], slot[:], -(P - 1) / 2, 1.0 / P, ALU.add, ALU.mult))
                c.link(dve.tensor_copy(hi16[:], hi_i[:]))
                c.step(dve.scalar_tensor_tensor(out=lo16[:], in0=hi_i[:], scalar=-float(P), in1=slot[:], op0=ALU.mult, op1=ALU.add))
                for b in range(NQ // QB):
                    qs = slice(b * QB, (b + 1) * QB)
                    i0 = b * QB % NT
                    if b >= 2:
                        dve.wait_ge(ones_used, b - 1)
                    c.link(dve.tensor_tensor(onelo[b % 2][:], io16[:].unsqueeze(1).to_broadcast([P, QB, P]),
                                             lo16[:, qs].unsqueeze(2).to_broadcast([P, QB, P]), ALU.is_equal))
                    w = [P, QB, SLOT_TILES]
                    c.step(dve.tensor_tensor(onehi[:], io16[:, 0:SLOT_TILES].unsqueeze(1).to_broadcast(w),
                                             hi16[:, qs].unsqueeze(2).to_broadcast(w), ALU.is_equal))
                    c.link(dve.tensor_tensor(val[b % 2][:, :, 0], onehi[:],
                                             tile16[:, i0:i0 + QB].unsqueeze(2).to_broadcast(w), ALU.mult))
                    c.step(dve.tensor_scalar(val[b % 2][:, :, 1], onehi[:], cst[:, C_P1:C_P1 + 1], None, ALU.mult))
                    dve.sem_inc(ones_ready, 1)
                dve.wait_ge(ones_used, NQ // QB)
                c.step(dve.tensor_copy(gI[:], ps_i[:, SLOT_TILES:2 * SLOT_TILES]))
                c.step(dve.scalar_tensor_tensor(out=I[:], in0=ps_i[:, 0:SLOT_TILES], scalar=float(P), in1=gI[:],
                                                op0=ALU.mult, op1=ALU.add))
                c.link(dve.tensor_scalar(empty[:], I[:], 0.0, cst[:, C_DUM:C_DUM + 1], ALU.is_equal, ALU.mult))
                c.step(dve.tensor_scalar(gI[:], I[:], -1.0, 0.0, ALU.add, ALU.max))
                c.link(dve.tensor_scalar(gidx[:], gI[:], float(P), None, ALU.add))
                c.step(dve.scalar_tensor_tensor(out=sidx[:], in0=I[:], scalar=-1.0, in1=empty[:], op0=ALU.add, op1=ALU.add))


def stage_experts(nc, a, keep):
    table, gidx, sidx, out = keep["table"], keep["gidx"], keep["sidx"], a["out"]
    GROUPS = [(0, 4), (4, 4), (8, CT - 8)]
    RFC, RG, RY = 4, 3, 4
    UNITS = len(GROUPS) * HM
    with ExitStack() as ctx:
        s = Space(nc, ctx, "ex")
        fcb, pjb, idh, wst, wh, wl = (keep[n] for n in ("fcb", "pjb", "idh", "wst", "ewh", "ewl"))
        gi = [s.sb(f"gi{p}", [P, CT], U32) for p in range(2)]
        si = [s.sb(f"si{p}", [P, CT], U32) for p in range(2)]
        got = [s.sb(f"got{p}", [P, CT, ROW], U16) for p in range(2)]
        fb = [s.sb(f"fb{p}", [P, HM], F32) for p in range(2)]
        weight = [s.sb(f"weight{p}", [P, CT, 1], F32) for p in range(2)]
        xg = s.sb("xg", [P, 2, K, CAP], F16)
        gel = [s.sb(f"gel{i}", [P, BLK], F32) for i in range(RG)]
        Gh = [s.sb(f"Gh{i}", [P, HM, BLK], F16) for i in range(2)]
        Gl = [s.sb(f"Gl{i}", [P, HM, BLK], F16) for i in range(2)]
        y1 = [s.sb(f"y1{i}", [P, D], F32) for i in range(2)]
        y = [s.sb(f"y{i}", [P, D], F32) for i in range(RY)]
        ps_x = [s.ps(f"x{i}", [P, 2 * BLK], F16) for i in range(2)]
        ps_f = [s.ps(f"f{i}", [P, BLK]) for i in range(RFC)]
        ps_y = [s.ps(f"y{i}", [P, BLK]) for i in range(2)]
        d_w, d_s = s.sem("d_w"), s.sem("d_s")
        d_g = [[s.sem(f"d_g{p}{g}") for g in range(2)] for p in range(2)]
        idx_in, w_hi, w_lo, xt_mm, xt_done = (s.sem(n) for n in ("idx_in", "w_hi", "w_lo", "xt_mm", "xt_done"))
        fc_mm, gel_done, g_hi, g_lo, y_mm, y1_done, y_done, stored, fb_in, w_in = (
            s.sem(n) for n in ("fc_mm", "gel_done", "g_hi", "g_lo", "y_mm", "y1_done", "y_done", "stored", "fb_in", "w_in"))
        first = GROUPS[0][1]

        def order(fc, proj):
            fc(0), fc(1), proj(0), fc(2), proj(1), proj(2)

        def quarter(bufs, n):
            half = slice(n % 2 * (K // 2), (n % 2 + 1) * (K // 2)) if n < 2 else slice(n % 2 * (HM // 2), (n % 2 + 1) * (HM // 2))
            return bufs[n // 2][:, half].rearrange("p a b -> p (a b)")

        with nc.Block() as block:
            @block.sync
            def _(sp):
                with sp.Fori(0, E) as e:
                    sp.wait_ge(w_lo, 4 * e + 4)
                    n = (e + 1) % E
                    sp.dma_start(wst[0][:], a["c_fc"][bass.ds(n, 1)].squeeze(0).rearrange("(k p) n -> p k n", p=P)).then_inc(d_w, 16)
                    sp.dma_start(wst[1][:], a["c_proj"][bass.ds(n, 1)].squeeze(0).rearrange("(k p) n -> p k n", p=P)).then_inc(d_w, 16)

            @block.gpsimd
            def _(pool):
                def gathers(e, p):
                    n = e % E * CT
                    pool.tensor_copy(gi[p][:], gidx[:, bass.ds(n, CT)]).then_inc(idx_in, 1)
                    pool.tensor_copy(si[p][:], sidx[:, bass.ds(n, CT)]).then_inc(idx_in, 1)
                    pool.wait_ge(idx_in, 2 * e + 2)
                    pool.tensor_copy(fb[p][:], fcb[:, bass.ds(e % E * HM, HM)]).then_inc(fb_in, 1)
                    for t in range(CT):
                        pool.indirect_dma_start(out=got[p][:, t], out_offset=None, in_=table,
                                                in_offset=bass.IndirectOffsetOnAxis(ap=gi[p][:, t:t + 1], axis=0))\
                            .then_inc(d_g[p][t >= first], 16)

                def scatters(e, p):
                    for t in range(CT):
                        n = e * CT + t
                        pool.wait_ge(y_done, n + 3)
                        pool.sem_inc(stored, 1)
                        pool.indirect_dma_start(out=out, out_offset=bass.IndirectOffsetOnAxis(ap=si[p][:, t:t + 1], axis=0),
                                                in_=y[(p * CT + t) % RY][:], in_offset=None, compute_op=ALU.add).then_inc(d_s, 16)
                        pool.wait_ge(d_s, 16 * n + 16)

                def weights(e, visit, p):
                    pool.wait_ge(d_g[p][0], 16 * first * visit)
                    pool.wait_ge(d_g[p][1], 16 * (CT - first) * visit)
                    pool.tensor_copy(weight[p][:], got[p][:, :, 2 * D:].bitcast(F32)[:, :, bass.ds(e % E, 1)]).then_inc(w_in, 1)

                pool.sem_inc(stored, RY - 1)
                gathers(0, 0)
                weights(0, 1, 0)
                with pool.Fori(0, E // 2) as i:
                    for p in range(2):
                        e = 2 * i + p
                        gathers(e + 1, 1 - p)
                        scatters(e, p)
                        weights(e + 1, i + 1 + p, 1 - p)

            @block.tensor
            def _(pe):
                pe.sem_inc(y_mm, CT + 1)

                def T(e, p, t, visit):
                    if t == 0:
                        pe.wait_ge(d_g[p][0], 16 * first * visit)
                    if t == first:
                        pe.wait_ge(d_g[p][1], 16 * (CT - first) * visit)
                    pe.wait_ge(xt_done, CT * e + t + 1)
                    for j in range(2 * K):
                        ins = pe.transpose(ps_x[t % 2][:, j * P:(j + 1) * P], got[p][:, t, j * P:(j + 1) * P].bitcast(F16), idh[:])
                    ins.then_inc(xt_mm, 1)

                for t in range(first):
                    T(0, 0, t, 1)
                with pe.Fori(0, E // 2) as i:
                    for p in range(2):
                        e = 2 * i + p

                        def fc(g):
                            t0, nt = GROUPS[g]
                            pe.wait_ge(xt_done, CT * e + t0 + nt + 2)
                            if g == 0:
                                pe.wait_ge(w_lo, 4 * e + 4)
                            cols = slice(t0 * P, (t0 + nt) * P)
                            for m in range(HM):
                                u = g * HM + m
                                pe.wait_ge(gel_done, UNITS * e + u + 1)
                                ms, n = slice(m * P, (m + 1) * P), 0
                                for k in range(K):
                                    for w, x in pair_products(wh[p][0][:, k, ms], wl[p][0][:, k, ms], xg[:, 0, k, cols], xg[:, 1, k, cols]):
                                        ins = pe.matmul(ps_f[u % RFC][:, 0:nt * P], w, x, start=(n == 0), stop=(n == 3 * K - 1))
                                        n += 1
                                ins.then_inc(fc_mm, 1)
                                if g == 0 and m < CT - first:
                                    T(e, p, first + m, i + 1)

                        def proj(g):
                            t0, nt = GROUPS[g]
                            gb = (p + g) % 2
                            pe.wait_ge(g_lo, UNITS * e + (g + 1) * HM + RG)
                            for t in range(t0, t0 + nt):
                                pe.wait_ge(y1_done, CT * e + t + 1)
                                cs, n = slice((t - t0) * P, (t - t0 + 1) * P), 0
                                for k in range(HM):
                                    for x, w in ((Gh, wh), (Gl, wh), (Gh, wl)):
                                        ins = pe.matmul(ps_y[t % 2][:, 0:D], x[gb][:, k, cs], w[p][1][:, k], start=(n == 0),
                                                        stop=(n == 3 * HM - 1))
                                        n += 1
                                ins.then_inc(y_mm, 1)
                                if g == 1:
                                    T(e + 1, 1 - p, t - t0, i + 1 + p)

                        order(fc, proj)

            @block.scalar
            def _(act):
                def split_high(e, p, n):
                    if n == 0:
                        act.wait_ge(d_w, 32 * e)
                        act.wait_ge(y_mm, CT * e + 1)
                    act.activation(quarter(wh[p], n), quarter(wst, n), ACT.Copy, scale=SC).then_inc(w_hi, 1)

                act.sem_inc(gel_done, RFC)
                act.sem_inc(y_done, 2)
                with act.Fori(0, E // 2) as i:
                    for p in range(2):
                        e = 2 * i + p

                        def fc(g):
                            w = GROUPS[g][1] * P
                            if g == 0:
                                act.wait_ge(fb_in, e + 1)
                            for m in range(HM):
                                u = g * HM + m
                                act.wait_ge(fc_mm, UNITS * e + u + 1)
                                act.wait_ge(g_lo, UNITS * e + u + 1)
                                act.activation(gel[u % RG][:, 0:w], ps_f[u % RFC][:, 0:w], ACT.Gelu, scale=INV2,
                                               bias=fb[p][:, m:m + 1]).then_inc(gel_done, 1)

                        def proj(g):
                            t0, nt = GROUPS[g]
                            if g == 0:
                                act.wait_ge(w_in, e + 1)
                            for t in range(t0, t0 + nt):
                                act.wait_ge(y1_done, CT * e + t + 3)
                                act.wait_ge(stored, CT * e + t + 1)
                                act.activation(y[(p * CT + t) % RY][:], y1[t % 2][:], ACT.Copy,
                                               scale=weight[p][:, t]).then_inc(y_done, 1)
                                if g == 1:
                                    split_high(e + 1, 1 - p, t - t0)

                        order(fc, proj)

            @block.vector
            def _(dve):
                def split_low(e, p, n):
                    dve.wait_ge(w_hi, 4 * e + n - 3)
                    dve.scalar_tensor_tensor(out=quarter(wl[p], n), in0=quarter(wst, n), scalar=SC, in1=quarter(wh[p], n),
                                             op0=ALU.mult, op1=ALU.subtract).then_inc(w_lo, 1)

                def T(e, t):
                    dve.wait_ge(xt_mm, CT * e + t + 1)
                    dve.tensor_copy(xg[:, :, :, t * P:(t + 1) * P],
                                    ps_x[t % 2][:, 0:2 * K * P].rearrange("p (a k n) -> p a k n", a=2, k=K)).then_inc(xt_done, 1)

                dve.sem_inc(w_lo, 4)
                dve.sem_inc(xt_done, 2)
                dve.sem_inc(g_lo, RG)
                dve.sem_inc(y1_done, 2)
                for t in range(first):
                    T(0, t)
                with dve.Fori(0, E // 2) as i:
                    for p in range(2):
                        e = 2 * i + p

                        def fc(g):
                            w, gb = GROUPS[g][1] * P, (p + g) % 2
                            dve.wait_ge(y_mm, 1 + CT * e + (CT - GROUPS[2][1], CT, CT + GROUPS[0][1])[g])
                            for m in range(HM):
                                u = g * HM + m
                                dve.wait_ge(gel_done, UNITS * e + u + 1 + RFC)
                                dve.tensor_scalar(Gh[gb][:, m, 0:w], gel[u % RG][:, 0:w], SC, None, ALU.mult).then_inc(g_hi, 1)
                                dve.wait_ge(g_hi, UNITS * e + u + 1)
                                dve.scalar_tensor_tensor(out=Gl[gb][:, m, 0:w], in0=gel[u % RG][:, 0:w], scalar=SC,
                                                         in1=Gh[gb][:, m, 0:w], op0=ALU.mult, op1=ALU.subtract).then_inc(g_lo, 1)
                                if g == 0 and m < CT - first:
                                    T(e, first + m)

                        def proj(g):
                            t0, nt = GROUPS[g]
                            for t in range(t0, t0 + nt):
                                dve.wait_ge(y_mm, CT * e + t + 2 + CT)
                                dve.wait_ge(y_done, CT * e + t + 1)
                                dve.scalar_tensor_tensor(out=y1[t % 2][:], in0=ps_y[t % 2][:, 0:D], scalar=INV2,
                                                         in1=pjb[:, bass.ds(e * D, D)], op0=ALU.mult, op1=ALU.add).then_inc(y1_done, 1)
                                if g == 1:
                                    T(e + 1, t - t0)
                                    split_low(e + 1, 1 - p, t - t0)

                        order(fc, proj)


def adaln_ffn_moe_kernel(nc, a, stages=99):
    with ExitStack() as ctx:
        s = s0 = Space(nc, ctx, "all")
        keep = {
            "cst": s.sb("cst", [P, C_END], F32),
            "scal": s.sb("scal", [P, S_END], F32),
            "x0h": s.sb("x0h", [P, K, N + P], F16),
            "x0l": s.sb("x0l", [P, K, N + P], F16),
        }
        keep["idh"] = s0.sb("idh", [P, P], F16)
        keep["Lg"] = s0.sb("Lg", [P, NT + 1, E], F32)
        keep["table"] = nc.dram_tensor("state_rows", (P * (NT + 1), ROW), U16, kind="Internal").ap()
        with ExitStack() as mid:
            keep["R"] = Space(nc, mid, "ffn").sb("R", [P, FO, N], F32)
            gru_operands(keep)
            with ExitStack() as inner:
                s = Space(nc, inner, "ffn")
                keep["wTh"] = s.sb("wTh", [P, WCOLS], F16)
                keep["wTl"] = s.sb("wTl", [P, WCOLS], F16)
                stage_logits(nc, a, keep)
                with ExitStack() as inner2:
                    keep["qup"] = Space(nc, inner2, "ffn").sb("qup", [P, FO, N], I16)
                    stage_gate_up(nc, a, keep)
                    stage_product(nc, a, keep)
                stage_down(nc, a, keep)
            if stages > 4:
                stage_gru(nc, a, keep)
        if stages > 4:
            keep["gidx"], keep["sidx"] = (s0.sb(n, [P, SLOT_TILES], U32) for n in ("gidx", "sidx"))
        if stages > 5:
            keep["fcb"] = s0.sb("fcb", [P, E * HM], F32)
            keep["pjb"] = s0.sb("pjb", [P, E * D], F32)
            keep["wst"] = [s0.sb("wst_fc", [P, K, H], F32), s0.sb("wst_pj", [P, HM, D], F32)]
            for part in ("ewh", "ewl"):
                keep[part] = [[s0.sb(f"{part}{p}_fc", [P, K, H], F16), s0.sb(f"{part}{p}_pj", [P, HM, D], F16)] for p in range(2)]
            stage_route(nc, a, keep)
        if stages > 6:
            stage_experts(nc, a, keep)


def laid_out(v):
    c = np.ascontiguousarray
    cols = lambda b: c(b.reshape(-1, P).T)
    return {
        "xT": c(v["x"].transpose(2, 1, 0).reshape(D, N)),
        "condT": c(v["cond_1024"].T),
        "weight_matrix": c(v["L0_cond_weight_matrix"]),
        "W_proj": c(v["L0_cond_W_proj"]),
        "b_proj": cols(v["L0_cond_b_proj"]),
        "w_gate": c(v["L0_ffn_w_gate"]),
        "w_up": c(v["L0_ffn_w_up"]),
        "w_down": c(v["L0_ffn_w_down"]),
        "W_gru": c(np.stack([v["L1_cond_W_r"], v["L1_cond_W_z"], v["L1_cond_W"]])),
        "U_gru": c(np.stack([v["L1_cond_U_r"], v["L1_cond_U_z"], v["L1_cond_U"]])),
        "C_gru": c(np.stack([v["L1_cond_C_r"], v["L1_cond_C_z"], v["L1_cond_C"]])),
        "b_gru": c(np.concatenate([cols(v[n]) for n in ("L1_cond_b_r", "L1_cond_b_z", "L1_cond_b")], axis=1)),
        "gate_w": c(v["L1_ffn_gate_w"]),
        "c_fc": c(v["L1_ffn_c_fc"]),
        "fc_bias": cols(v["L1_ffn_fc_bias"]),
        "c_proj": c(v["L1_ffn_c_proj"]),
        "proj_bias": c(v["L1_ffn_proj_bias"].reshape(1, E * D)),
        "consts": constants(),
    }


def kernel(**inputs):
    import concourse.bacc as bacc
    from concourse.bass_utils import run_bass_kernel_spmd

    nc = bacc.Bacc("TRN2", target_bir_lowering=False, num_devices=1)
    given = laid_out({n: np.asarray(v) for n, v in inputs.items()})
    arrays = {f"in_{n}_dram": v for n, v in given.items()}
    a = {n: nc.dram_tensor(f"in_{n}_dram", v.shape, mybir.dt.from_np(v.dtype), kind="ExternalInput").ap()
         for n, v in given.items()}
    a["out"] = nc.dram_tensor("out_0_dram", (N + DUMMY, D), F32, kind="ExternalOutput").ap()
    adaln_ffn_moe_kernel(nc, a)
    r = run_bass_kernel_spmd(nc, [arrays], core_ids=[0])
    got = r.results[0]["out_0_dram"]
    return np.ascontiguousarray(got[:N].reshape(STEPS, BATCH, D).transpose(1, 0, 2))
```

```python
from contextlib import ExitStack

import numpy as np

import concourse.bass as bass
from concourse import mybir

F32 = mybir.dt.float32
F16 = mybir.dt.float16
I16 = mybir.dt.int16
U16 = mybir.dt.uint16
U32 = mybir.dt.uint32
ALU = mybir.AluOpType
ACT = mybir.ActivationFunctionType
X = mybir.AxisListType.X

P = 128
BATCH, STEPS, D = 16, 256, 256
N = BATCH * STEPS
K = D // P
F = 768
FO = F // P
BLK = 512
NB = N // BLK
NT = N // P
QBLOCK = 32
WCOLS = 3 * K * F
E, TOPK = 8, 2
H = 4 * D
HM = H // P
CAP = int(1.25 * N * TOPK / E)
CT = CAP // P
SLOT_TILES = E * CT
QMAX = 32767.0
TINY = 1e-12
SC = 256.0
INV2 = 1.0 / (SC * SC)
TILE_STEPS = P // BATCH
ROW = 2 * D + 2 * E
DUMMY = P

C_ID, C_EIDX, C_EOFF, C_P1, C_DUM, C_END = np.cumsum([0, P, E, E, 1, 1])
H_ID, H_BLESS, H_BSAME, H_TLESS, H_IOTA, H_TILE, H_END = np.cumsum([0, P, P, P, P, P, NT])


def constants():
    c, h = np.zeros((P, C_END), np.float32), np.zeros((P, H_END), np.float16)
    p = np.arange(P)
    b, t = p % BATCH, p // BATCH
    c[:, C_ID:C_ID + P] = np.eye(P)
    c[:, C_EIDX:C_EIDX + E] = E - np.arange(E)
    c[:, C_EOFF:C_EOFF + E] = CAP * np.arange(E)
    c[:, C_P1] = p + 1
    c[:, C_DUM] = N + 1 + p
    h[:, H_ID:H_ID + P] = np.eye(P)
    h[:, H_BLESS:H_BLESS + P] = b[:, None] < b[None, :]
    h[:, H_BSAME:H_BSAME + P] = b[:, None] == b[None, :]
    h[:, H_TLESS:H_TLESS + P] = (b[:, None] == b[None, :]) & (t[:, None] < t[None, :])
    h[:, H_IOTA:H_IOTA + P] = p[None, :]
    h[:, H_TILE:H_TILE + NT] = np.arange(NT)
    return c, h


class Chain:

    def __init__(self, eng, sem, base=0):
        self.eng, self.sem, self.base, self.n = eng, sem, base, 0

    def link(self, ins):
        ins.then_inc(self.sem, 1)
        self.n += 1

    def wait(self):
        self.eng.wait_ge(self.sem, self.base + self.n)

    def step(self, ins):
        self.link(ins)
        self.wait()


class Space:

    def __init__(self, nc, ctx, tag):
        self.nc, self.ctx, self.tag = nc, ctx, tag

    def sb(self, name, shape, dt):
        return self.ctx.enter_context(self.nc.sbuf_tensor(f"{self.tag}_{name}", shape, dt))

    def ps(self, name, shape, dt=F32):
        return self.ctx.enter_context(self.nc.psum_tensor(f"{self.tag}_ps_{name}", shape, dt))

    def sem(self, name):
        return self.ctx.enter_context(self.nc.semaphore(f"{self.tag}_{name}"))


def pair_products(wh, wl, xh, xl):
    return ((wh, xh), (wl, xh), (wh, xl))


def stage_logits(nc, a, keep):
    x0h, x0l, wTh, wTl, scal, cst = keep["x0h"], keep["x0l"], keep["wTh"], keep["wTl"], keep["scal"], keep["cst"]
    XBUFS = 4
    NG = WCOLS // BLK
    GROUPS_AFTER = {j: range(2 * (j - 3), min(2 * (j - 2), NG)) for j in range(3, NB)}
    with ExitStack() as ctx:
        s = Space(nc, ctx, "lg")
        condT = s.sb("condT", [P, K, BATCH], F32)
        wcond = s.sb("wcond", [P, 2 * K, D], F32)
        wproj = s.sb("wproj", [P, K, D], F32)
        bproj = s.sb("bproj", [P, K], F32)
        uT = s.sb("uT", [P, K, BATCH], F32)
        vT = s.sb("vT", [P, K, BATCH], F32)
        xin = [s.sb(f"xin{i}", [P, K, BLK], F32) for i in range(XBUFS)]
        L = keep["R"][:, 0:K]
        wraw = keep["R"][:].rearrange("p o n -> p (o n)")[:, K * N:K * N + WCOLS]
        wint = s.sb("wint", [P, WCOLS], I16)
        wscale = s.sb("wscale", [P, 4, WCOLS // QBLOCK], F32)
        blkmax = s.sb("blkmax", [P, NB], F32)
        allmax = s.sb("allmax", [P, 2], F32)
        ps_set = s.ps("set", [P, BLK])
        ps_L = [[s.ps(f"ps_L{p}{m}", [P, BLK]) for m in range(K)] for p in range(2)]
        ps_w = [s.ps(f"ps_w{i}", [P, BLK]) for i in range(2)]
        d_small, d_w = s.sem("d_small"), [s.sem(f"d_w{n}") for n in ("up", "gate", "down")]
        d_x = [s.sem(f"d_x{i}") for i in range(XBUFS)]
        w_int = s.sem("w_int")
        u_mm, u_done, v_mm, v_done = s.sem("u_mm"), s.sem("u_done"), s.sem("v_mm"), s.sem("v_done")
        L_mm, L_read, dq, w_deq = s.sem("L_mm"), s.sem("L_read"), s.sem("dq"), s.sem("w_deq")
        w_tr, w_hi, w_lo = s.sem("w_tr"), s.sem("w_hi"), s.sem("w_lo")
        mx_own, mx_all, sc_own, sc_done = s.sem("mx_own"), s.sem("mx_all"), s.sem("sc_own"), s.sem("sc_done")
        pad = s.sem("pad")

        w3 = wraw.rearrange("p (g n) -> p g n", n=QBLOCK)
        i3 = wint[:].rearrange("p (g n) -> p g n", n=QBLOCK)
        wide = [P, WCOLS // QBLOCK, QBLOCK]

        def source(n):
            if n < 2 * K * FO:
                mat, k, o = n // (K * FO), n % (K * FO) // FO, n % FO
                return (mat * FO + o) * D + k * P
            k, o = (n - 2 * K * FO) // K, n % K
            return 2 * FO * D + o * F + k * P

        with nc.Block() as block:
            @block.sync
            def _(sp):
                sp.dma_start(cst[:], a["consts"]).then_inc(d_small, 16)
                sp.dma_start(keep["cst16"][:], a["consts16"]).then_inc(d_small, 16)
                sp.dma_start(condT[:], a["condT"].rearrange("(k p) b -> p k b", p=P)).then_inc(d_small, 16)
                sp.dma_start(wproj[:], a["W_proj"].rearrange("(k p) n -> p k n", p=P)).then_inc(d_small, 16)
                sp.dma_start(wcond[:], a["weight_matrix"].rearrange("(k p) n -> p k n", p=P)).then_inc(d_small, 16)
                sp.dma_start(bproj[:], a["b_proj"]).then_inc(d_small, 16)
                xT = a["xT"].rearrange("(k p) n -> p k n", p=P)
                for j in range(NB):
                    if j >= XBUFS:
                        sp.wait_ge(L_mm, j - XBUFS + 1)
                    sp.dma_start(xin[j % XBUFS][:], xT[:, :, j * BLK:(j + 1) * BLK]).then_inc(d_x[j % XBUFS], 16)

            @block.scalar
            def _(act):
                up = wraw[:, 0:FO * D].rearrange("p (o n) -> p o n", o=FO)
                gate = wraw[:, FO * D:2 * FO * D].rearrange("p (o n) -> p o n", o=FO)
                down = wraw[:, 2 * FO * D:].rearrange("p (o n) -> p o n", o=K)
                act.dma_start(up, a["w_up"].rearrange("(o p) n -> p o n", p=P)).then_inc(d_w[0], 16)
                act.dma_start(gate, a["w_gate"].rearrange("(o p) n -> p o n", p=P)).then_inc(d_w[1], 16)
                act.dma_start(down, a["w_down"].rearrange("(o p) n -> p o n", p=P)).then_inc(d_w[2], 16)
                act.wait_ge(u_mm, 1)
                for m in range(K):
                    act.activation(uT[:, m], ps_set[:, m * BATCH:(m + 1) * BATCH], ACT.Gelu,
                                   bias=bproj[:, m:m + 1]).then_inc(u_done, 1)
                act.wait_ge(v_mm, 1)
                act.activation(vT[:], ps_set[:, K * BATCH:2 * K * BATCH], ACT.Copy).then_inc(v_done, 1)
                for g in range(NG):
                    act.wait_ge(w_tr, g + 1)
                    act.activation(wTh[:, g * BLK:(g + 1) * BLK], ps_w[g % 2][:], ACT.Copy).then_inc(w_hi, 1)

            @block.tensor
            def _(pe):
                def logits(j):
                    pe.wait_ge(d_x[j % XBUFS], 16 * (j // XBUFS) + 16)
                    if j >= 2:
                        pe.wait_ge(L_read, j - 1)
                    for m in range(K):
                        for k in range(K):
                            i = pe.matmul(ps_L[j % 2][m][:], wcond[:, K + k, m * P:(m + 1) * P], xin[j % XBUFS][:, k],
                                          start=(k == 0), stop=(k == K - 1))
                    i.then_inc(L_mm, 1)

                pe.wait_ge(d_small, 96)
                for m in range(K):
                    for k in range(K):
                        i = pe.matmul(ps_set[:, m * BATCH:(m + 1) * BATCH], wproj[:, k, m * P:(m + 1) * P], condT[:, k],
                                      start=(k == 0), stop=(k == K - 1))
                i.then_inc(u_mm, 1)
                logits(0)
                pe.wait_ge(u_done, K)
                for m in range(K):
                    for k in range(K):
                        c0 = (K + m) * BATCH
                        i = pe.matmul(ps_set[:, c0:c0 + BATCH], wcond[:, k, m * P:(m + 1) * P], uT[:, k],
                                      start=(k == 0), stop=(k == K - 1))
                i.then_inc(v_mm, 1)
                for j in range(1, NB):
                    logits(j)
                    for g in GROUPS_AFTER.get(j, ()):
                        if g == 0:
                            pe.wait_ge(w_deq, 1)
                        if g >= 2:
                            pe.wait_ge(w_lo, g - 1)
                        for n in range(4):
                            c0 = source(4 * g + n)
                            i = pe.transpose(ps_w[g % 2][:, n * P:(n + 1) * P], wraw[:, c0:c0 + P], cst[:, C_ID:C_ID + P])
                        i.then_inc(w_tr, 1)

            @block.gpsimd
            def _(pool):
                pool.memset(x0h[:, :, N:N + P], 0.0).then_inc(pad, 1)
                pool.memset(x0l[:, :, N:N + P], 0.0).then_inc(pad, 1)
                pool.wait_ge(mx_own, 1)
                pool.partition_all_reduce(allmax[:, 1:2], allmax[:, 0:1], P, bass.bass_isa.ReduceOp.max).then_inc(mx_all, 1)
                pool.wait_ge(pad, 2)

            @block.vector
            def _(dve):
                c = Chain(dve, dq)

                def low(g):
                    dve.wait_ge(w_hi, g + 1)
                    dve.tensor_tensor(wTl[:, g * BLK:(g + 1) * BLK], ps_w[g % 2][:], wTh[:, g * BLK:(g + 1) * BLK],
                                      ALU.subtract).then_inc(w_lo, 1)

                def logits(j):
                    cols = slice(j * BLK, (j + 1) * BLK)
                    dve.wait_ge(L_mm, j + 1)
                    for m in range(K):
                        out = L[:, m, cols].rearrange("p (t b) -> p t b", b=BATCH)
                        o = dve.tensor_tensor(out, ps_L[j % 2][m][:].rearrange("p (t b) -> p t b", b=BATCH),
                                              vT[:, m].unsqueeze(1).to_broadcast([P, BLK // BATCH, BATCH]), ALU.add)
                    o.then_inc(L_read, 1)
                    dve.wait_ge(L_read, j + 1)
                    dve.tensor_reduce(blkmax[:, j:j + 1], L[:, :, cols], mybir.AxisListType.XY, ALU.max,
                                      apply_absolute_value=True).then_inc(sc_own, 1)

                g3 = WCOLS // QBLOCK // 3
                for n in range(3):
                    dve.wait_ge(d_w[n], 16)
                    c.link(dve.tensor_reduce(wscale[:, 0, n * g3:(n + 1) * g3], w3[:, n * g3:(n + 1) * g3], X, ALU.max,
                                             apply_absolute_value=True))
                c.wait()
                c.step(dve.tensor_scalar(wscale[:, 1], wscale[:, 0], 1.0 / 7.0, TINY, ALU.mult, ALU.max))
                c.link(dve.reciprocal(wscale[:, 2], wscale[:, 1]))
                c.step(dve.tensor_scalar(wscale[:, 3], wscale[:, 1], SC, None, ALU.mult))
                c.step(dve.tensor_tensor(w3, w3, wscale[:, 2].unsqueeze(2).to_broadcast(wide), ALU.mult))
                dve.tensor_scalar(wint[:], wraw, 7.0, -8.0, ALU.min, ALU.max).then_inc(w_int, 1)
                dve.wait_ge(v_done, 1)
                logits(0)
                logits(1)
                dve.wait_ge(w_int, 1)
                dve.tensor_tensor(w3, i3, wscale[:, 3].unsqueeze(2).to_broadcast(wide), ALU.mult).then_inc(w_deq, 1)
                for j in range(2, NB):
                    logits(j)
                    for g in GROUPS_AFTER.get(j, ()):
                        low(g)
                dve.wait_ge(sc_own, NB)
                dve.tensor_reduce(allmax[:, 0:1], blkmax[:], X, ALU.max).then_inc(mx_own, 1)
                dve.wait_ge(mx_all, 1)
                c = Chain(dve, sc_done)
                c.step(dve.tensor_scalar(scal[:, S_X:S_X + 1], allmax[:, 1:2], 1.0 / QMAX, TINY, ALU.mult, ALU.max))
                c.step(dve.reciprocal(scal[:, S_TMP:S_TMP + 1], scal[:, S_X:S_X + 1]))


(S_X, S_TMP, S_PU, S_PG, S_UP, S_GATE, S_CUP, S_CGATE, S_G2, S_C2, S_O, S_CO, S_XU, S_ALLU, S_ALLG, S_US2, S_DN, S_R,
 S_MXA, S_MXB, S_END) = range(21)


def column(scal, n):
    return scal[:, n:n + 1]


def stage_gate_up(nc, a, keep):
    x0h, x0l, wTh, wTl, scal = keep["x0h"], keep["x0l"], keep["wTh"], keep["wTl"], keep["scal"]
    qup, R = keep["qup"], keep["R"]
    L = R[:, 0:K]
    PIECE, DEEP = 3 * BLK, 3
    NP = FO * N // PIECE
    with ExitStack() as ctx:
        s = Space(nc, ctx, "gu")
        unitmax = s.sb("unitmax", [P, NB * FO], F32)
        gq = [s.sb(f"gq{i}", [P, PIECE], I16) for i in range(DEEP)]
        Rf = R[:].rearrange("p o n -> p (o n)")
        ps = [s.ps(f"p{i}", [P, BLK]) for i in range(FO)]
        mm, kept, max_done, gq_done, gq_seen = (s.sem(n) for n in ("mm", "kept", "max_done", "gq_done", "gq_seen"))
        own_max, all_max, v_sc, up_scale, gate_scale, up_int = (
            s.sem(n) for n in ("own_max", "all_max", "v_sc", "up_scale", "gate_scale", "up_int"))
        sig_done, sq_done, R_done, r_max = (s.sem(n) for n in ("sig_done", "sq_done", "R_done", "r_max"))
        q_done, hi_done, lo_done = (s.sem(n) for n in ("q_done", "hi_done", "lo_done"))
        UNITS = NB * FO

        def unit(pe, j, mat, o):
            n = 0
            cols = bass.ds(j * BLK, BLK)
            for k in range(K):
                w0 = (mat * K + k) * F + o * P
                for w, x in pair_products(wTh[:, w0:w0 + P], wTl[:, w0:w0 + P], x0h[:, k, cols], x0l[:, k, cols]):
                    ins = pe.matmul(ps[o][:], w, x, start=(n == 0), stop=(n == 3 * K - 1))
                    n += 1
            ins.then_inc(mm, 1)

        with nc.Block() as block:
            @block.tensor
            def _(pe):
                with pe.Fori(0, NB) as j:
                    pe.wait_ge(lo_done, j + 1)
                    for o in range(FO):
                        pe.wait_ge(kept, FO * j + o + 1)
                        unit(pe, j, 0, o)
                with pe.Fori(0, NB) as j:
                    for o in range(FO):
                        pe.wait_ge(kept, UNITS + FO * j + o + 1)
                        unit(pe, j, 1, o)

            @block.gpsimd
            def _(pool):
                for n, (own, every) in enumerate(((S_PU, S_ALLU), (S_PG, S_ALLG), (S_MXA, S_MXB))):
                    pool.wait_ge(own_max, n + 1)
                    pool.partition_all_reduce(column(scal, every), column(scal, own), P,
                                              bass.bass_isa.ReduceOp.max).then_inc(all_max, 1)

            @block.scalar
            def _(act):
                act.sem_inc(kept, FO)

                def high(j):
                    cols = bass.ds(j * BLK, BLK)
                    act.wait_ge(q_done, j + 1)
                    act.activation(x0h[:, :, cols], qup[:, 0:K, cols], ACT.Copy).then_inc(hi_done, 1)

                def keep_block(j, base):
                    for o in range(FO):
                        act.wait_ge(mm, base + FO * j + o + 1)
                        act.activation(R[:, o, bass.ds(j * BLK, BLK)], ps[o][:], ACT.Copy).then_inc(kept, 1)

                def integers_of_up(j):
                    cols = bass.ds(j * BLK, BLK)
                    act.activation(qup[:, :, cols], R[:, :, cols], ACT.Copy, scale=column(scal, S_CUP)).then_inc(up_int, 1)

                high(0)
                with act.Fori(0, NB - 1) as j:
                    high(j + 1)
                    keep_block(j, 0)
                keep_block(NB - 1, 0)
                act.wait_ge(up_scale, 1)
                integers_of_up(0)
                with act.Fori(0, NB - 1) as j:
                    act.wait_ge(up_int, j + 1)
                    keep_block(j, UNITS)
                    integers_of_up(j + 1)
                act.wait_ge(up_int, NB)
                keep_block(NB - 1, UNITS)
                act.wait_ge(gate_scale, 1)

                def gate_piece(n, d):
                    cols = bass.ds(n * PIECE, PIECE)
                    act.wait_ge(R_done, n + 1)
                    act.activation(gq[d][:], Rf[:, cols], ACT.Copy, scale=column(scal, S_CGATE)).then_inc(gq_done, 1)
                    act.wait_ge(gq_done, n + 1)
                    act.sem_inc(gq_seen, 1)
                    act.activation(Rf[:, cols], gq[d][:], ACT.Sigmoid, scale=column(scal, S_GATE)).then_inc(sig_done, 1)

                with act.Fori(0, NP // DEEP) as i:
                    for d in range(DEEP):
                        gate_piece(DEEP * i + d, d)
                for n in range(NP // DEEP * DEEP, NP):
                    gate_piece(n, n % DEEP)

            @block.vector
            def _(dve):
                c = Chain(dve, v_sc)

                def scale(most, true, factor):
                    c.step(dve.tensor_scalar(column(scal, true), column(scal, most), column(scal, S_XU), 1.0 / QMAX, ALU.mult, ALU.mult))
                    c.step(dve.tensor_scalar(column(scal, true), column(scal, true), TINY, None, ALU.max))
                    c.step(dve.reciprocal(column(scal, factor), column(scal, true)))
                    return dve.tensor_scalar(column(scal, factor), column(scal, factor), column(scal, S_XU), None, ALU.mult)

                dve.sem_inc(R_done, DEEP)

                def integers(j):
                    cols = bass.ds(j * BLK, BLK)
                    dve.tensor_scalar(qup[:, 0:K, cols], L[:, :, cols], column(scal, S_TMP), QMAX, ALU.mult, ALU.min).then_inc(q_done, 1)

                def low(j):
                    cols = bass.ds(j * BLK, BLK)
                    dve.wait_ge(hi_done, j + 1)
                    dve.tensor_tensor(x0l[:, :, cols], qup[:, 0:K, cols], x0h[:, :, cols], ALU.subtract).then_inc(lo_done, 1)

                def max_of_block(j, base):
                    for o in range(FO):
                        u = FO * j + o
                        dve.wait_ge(kept, base + u + 1 + FO)
                        dve.tensor_reduce(unitmax[:, bass.ds(u, 1)], R[:, o, bass.ds(j * BLK, BLK)], X, ALU.max,
                                          apply_absolute_value=True).then_inc(max_done, 1)

                integers(0)
                low(0)
                integers(1)
                with dve.Fori(0, NB - 2) as j:
                    low(j + 1)
                    max_of_block(j, 0)
                    integers(j + 2)
                low(NB - 1)
                max_of_block(NB - 2, 0)
                max_of_block(NB - 1, 0)
                dve.wait_ge(max_done, UNITS)
                dve.tensor_reduce(column(scal, S_PU), unitmax[:], X, ALU.max).then_inc(own_max, 1)
                c.step(dve.tensor_scalar(column(scal, S_XU), column(scal, S_X), 1.0 / SC, None, ALU.mult))
                dve.wait_ge(all_max, 1)
                scale(S_ALLU, S_UP, S_CUP).then_inc(up_scale, 1)
                with dve.Fori(0, NB) as j:
                    max_of_block(j, UNITS)
                dve.wait_ge(max_done, 2 * UNITS)
                dve.tensor_reduce(column(scal, S_PG), unitmax[:], X, ALU.max).then_inc(own_max, 1)
                dve.wait_ge(all_max, 2)
                scale(S_ALLG, S_GATE, S_CGATE).then_inc(gate_scale, 1)

                def max_of_piece(n):
                    dve.wait_ge(R_done, n + 1 + DEEP)
                    dve.tensor_reduce(unitmax[:, bass.ds(n, 1)], Rf[:, bass.ds(n * PIECE, PIECE)], X, ALU.max,
                                      apply_absolute_value=True).then_inc(r_max, 1)

                def product(n, d, between=None):
                    view = Rf[:, bass.ds(n * PIECE, PIECE)]
                    dve.wait_ge(sig_done, n + 1)
                    dve.tensor_scalar(view, view, 128.0, 128.0 + 65535.0 / 65536.0, ALU.add, ALU.min).then_inc(sq_done, 1)
                    if between is not None:
                        max_of_piece(between)
                    dve.wait_ge(sq_done, n + 1)
                    dve.scalar_tensor_tensor(out=view, in0=view, scalar=-128.0, in1=gq[d][:], op0=ALU.add,
                                             op1=ALU.mult).then_inc(R_done, 1)

                product(0, 0)
                with dve.Fori(0, (NP - 1) // DEEP) as i:
                    for d in range(DEEP):
                        n = DEEP * i + d + 1
                        product(n, (d + 1) % DEEP, n - 1)
                assert (NP - 1) % DEEP == 0
                max_of_piece(NP - 1)
                dve.wait_ge(r_max, NP)
                dve.tensor_reduce(column(scal, S_MXA), unitmax[:, 0:NP], X, ALU.max).then_inc(own_max, 1)
                dve.wait_ge(all_max, 3)
                c.step(dve.tensor_scalar(column(scal, S_G2), column(scal, S_MXB), column(scal, S_GATE), 1.0 / QMAX, ALU.mult, ALU.mult))
                c.step(dve.tensor_scalar(column(scal, S_G2), column(scal, S_G2), TINY, None, ALU.max))
                c.step(dve.reciprocal(column(scal, S_R), column(scal, S_G2)))
                c.step(dve.tensor_tensor(column(scal, S_C2), column(scal, S_R), column(scal, S_GATE), ALU.mult))
                c.step(dve.tensor_tensor(column(scal, S_US2), column(scal, S_G2), column(scal, S_UP), ALU.mult))


def stage_product(nc, a, keep):
    scal, qup, R = keep["scal"], keep["qup"], keep["R"]
    PIECE = 1536
    NP = FO * N // PIECE
    with ExitStack() as ctx:
        s = Space(nc, ctx, "pr")
        q2 = [s.sb(f"q2{i}", [P, PIECE], I16) for i in range(2)]
        pmax = s.sb("pmax", [P, NP], F32)
        q2_done, p_done, pm, all_own, all_max, v_sc = (s.sem(n) for n in ("q2_done", "p_done", "pm", "all_own", "all_max", "v_sc"))
        Rf = R[:].rearrange("p o n -> p (o n)")
        uf = qup[:].rearrange("p o n -> p (o n)")
        with nc.Block() as block:
            @block.scalar
            def _(act):
                with act.Fori(0, NP // 2) as i:
                    for par in range(2):
                        n = 2 * i + par
                        act.wait_ge(p_done, n + 1)
                        act.activation(q2[par][:], Rf[:, bass.ds(n * PIECE, PIECE)], ACT.Copy,
                                       scale=column(scal, S_C2)).then_inc(q2_done, 1)

            @block.gpsimd
            def _(pool):
                pool.wait_ge(all_own, 1)
                pool.partition_all_reduce(column(scal, S_MXB), column(scal, S_MXA), P,
                                          bass.bass_isa.ReduceOp.max).then_inc(all_max, 1)

            @block.vector
            def _(dve):
                dve.sem_inc(p_done, 2)

                def product(n, par):
                    cols = bass.ds(n * PIECE, PIECE)
                    dve.wait_ge(q2_done, n + 1)
                    dve.tensor_tensor(Rf[:, cols], q2[par][:], uf[:, cols], ALU.mult).then_inc(p_done, 1)

                def max_of_piece(n):
                    dve.wait_ge(p_done, n + 3)
                    dve.tensor_reduce(pmax[:, bass.ds(n, 1)], Rf[:, bass.ds(n * PIECE, PIECE)], X, ALU.max,
                                      apply_absolute_value=True).then_inc(pm, 1)

                product(0, 0)
                with dve.Fori(0, NP // 2 - 1) as i:
                    for k in range(2):
                        product(2 * i + k + 1, (k + 1) % 2)
                        max_of_piece(2 * i + k)
                product(NP - 1, 1)
                max_of_piece(NP - 2)
                max_of_piece(NP - 1)
                dve.wait_ge(pm, NP)
                dve.tensor_reduce(column(scal, S_MXA), pmax[:], X, ALU.max).then_inc(all_own, 1)
                dve.wait_ge(all_max, 1)
                c = Chain(dve, v_sc)
                c.step(dve.tensor_scalar(column(scal, S_O), column(scal, S_MXB), column(scal, S_US2), 1.0 / QMAX, ALU.mult, ALU.mult))
                c.step(dve.tensor_scalar(column(scal, S_O), column(scal, S_O), TINY, None, ALU.max))
                c.step(dve.reciprocal(column(scal, S_R), column(scal, S_O)))
                c.step(dve.tensor_tensor(column(scal, S_CO), column(scal, S_R), column(scal, S_US2), ALU.mult))
                c.step(dve.tensor_scalar(column(scal, S_DN), column(scal, S_O), 1.0 / SC, None, ALU.mult))


GATES = 3
SHARED = 3 * BLK


def gru_operands(keep):
    def view(o, start, shape, dt=F32):
        width = int(np.prod(shape)) // (2 if dt is F16 else 1)
        assert start + width <= SHARED
        flat = keep["R"][:, o, start:start + width]
        names = " ".join("abcd"[:len(shape)])
        return (flat.bitcast(F16) if dt is F16 else flat).rearrange(f"p ({names}) -> p {names}", **dict(zip("abcd", shape)))

    weight = (GATES, K, D)
    keep["raw"] = [view(n, 0, weight) for n in range(2)]
    keep["cond_w"] = view(2, 0, weight)
    keep["wh"], keep["wl"] = (view(o, 0, (2,) + weight, F16) for o in (3, 4))
    share = (GATES * K, BATCH)
    keep["vf"], keep["vh"], keep["vl"] = view(5, 0, share), view(5, 96, share, F16), view(5, 144, share, F16)
    keep["idsc"], keep["condT"], keep["bias"] = view(5, 192, (P,), F16), view(5, 256, (K, BATCH)), view(5, 288, (GATES * K,))
    keep["gwraw"], keep["gwh"], keep["gwl"] = view(5, 296, (K, E)), view(5, 312, (K, E), F16), view(5, 320, (K, E), F16)
    keep["xc"] = [view(5, 328 + n * K * P, (2, K, P), F16) for n in range(2)]


def stage_down(nc, a, keep):
    raw, cond_w, wh, wl, condT, bias, gwraw, gwh, gwl, idsc, vf, vh, vl = (
        keep[n] for n in ("raw", "cond_w", "wh", "wl", "condT", "bias", "gwraw", "gwh", "gwl", "idsc", "vf", "vh", "vl"))
    x1h, x1l, wTh, wTl, scal, R, cst = (keep[n] for n in ("x0h", "x0l", "wTh", "wTl", "scal", "R", "cst"))
    D0 = 2 * K * F
    with ExitStack() as ctx:
        s = Space(nc, ctx, "dn")
        xin = [s.sb(f"xin{i}", [P, K, BLK], F32) for i in range(2)]
        qo = [s.sb(f"qo{i}", [P, FO, BLK], I16) for i in range(2)]
        qh = [s.sb(f"qh{i}", [P, FO, BLK], F16) for i in range(2)]
        ql = [s.sb(f"ql{i}", [P, FO, BLK], F16) for i in range(2)]
        x1 = [s.sb(f"x1{i}", [P, K, BLK], F32) for i in range(2)]
        rows = s.sb("rows", [P, 4, D], F32)
        ps_d = [[s.ps(f"d{p}{m}", [P, BLK]) for m in range(K)] for p in range(2)]
        ps_t = [s.ps(f"t{i}", [P, 2, D]) for i in range(2)]
        ps_v = s.ps("v", [P, BLK])
        xc0, xc_done = keep["xc"][0], s.sem("xc_done")
        d_g, d_c, g_hi, g_scaled, g_lo, bias_sc, v_mm, v_done = (
            s.sem(n) for n in ("d_g", "d_c", "g_hi", "g_scaled", "g_lo", "bias_sc", "v_mm", "v_done"))
        d_x = [s.sem(f"d_x{i}") for i in range(2)]
        d_out, d_dummy, stored = keep["d_out"], s.sem("d_dummy"), s.sem("stored")
        qo_done, qh_done, ql_done, mm, x1_done, hi_done, lo_done, tr, rows_done = (
            s.sem(n) for n in ("qo_done", "qh_done", "ql_done", "mm", "x1_done", "hi_done", "lo_done", "tr", "rows_done"))

        def blocks(eng, one):
            one(0, 0)
            with eng.Fori(0, (NB - 4) // 2) as i:
                one(2 * i + 1, 1)
                one(2 * i + 2, 0)
            for j in range(NB - 3, NB):
                one(j, j % 2)

        def before(j, n):
            return not isinstance(j, int) or j + n < NB

        with nc.Block() as block:
            @block.sync
            def _(sp):
                xT = a["xT"].rearrange("(k p) n -> p k n", p=P)
                sp.sem_inc(stored, 1)
                for k in range(K):
                    sp.dma_start(a["out"][N:N + DUMMY, k * P:(k + 1) * P], cst[:, 0:P]).then_inc(d_dummy, 16)
                for par in range(2):
                    sp.dma_start(xin[par][:], xT[:, :, par * BLK:(par + 1) * BLK]).then_inc(d_x[par], 16)

                def one(j, par):
                    sp.wait_ge(rows_done, j + 2)
                    sp.dma_start(a["out"][bass.ds(j * BLK, BLK), :].rearrange("(c p) n -> p c n", p=P), rows[:]).then_inc(d_out, 16)
                    if before(j, 2):
                        sp.wait_ge(x1_done, j + 1)
                        sp.dma_start(xin[par][:], xT[:, :, bass.ds((j + 2) * BLK, BLK)]).then_inc(d_x[par], 16)
                    if before(j, 1):
                        sp.wait_ge(d_out, 16 * j + 16)
                        sp.sem_inc(stored, 1)
                blocks(sp, one)
                sp.wait_ge(d_dummy, 16 * K)

            @block.scalar
            def _(act):
                def integers(j, par):
                    act.wait_ge(ql_done, j + 1)
                    act.activation(qo[par][:], R[:, :, bass.ds(j * BLK, BLK)], ACT.Copy, scale=column(scal, S_CO)).then_inc(qo_done, 1)

                def rows_out(j):
                    act.wait_ge(tr, j + 2)
                    act.wait_ge(stored, j + 1)
                    for h in range(2):
                        r = act.activation(rows[:, 2 * h:2 * h + 2], ps_t[h][:], ACT.Copy)
                    r.then_inc(rows_done, 1)

                def one(j, par):
                    if before(j, 2):
                        integers(j + 2, par)
                    act.wait_ge(x1_done, j + 1)
                    act.activation(x1h[:, :, bass.ds(j * BLK, BLK)], x1[par][:], ACT.Copy, scale=SC).then_inc(hi_done, 1)
                    if isinstance(j, int) and j == NB - 2:
                        act.wait_ge(v_mm, 1)
                        act.wait_ge(bias_sc, 1)
                        for n in range(GATES * K):
                            act.activation(vf[:, n], ps_v[:, n * BATCH:(n + 1) * BATCH], ACT.Identity, scale=SC,
                                           bias=bias[:, n:n + 1]).then_inc(v_done, 1)
                    if not isinstance(j, int) or j > 0:
                        rows_out(j - 1)

                act.sem_inc(rows_done, 1)
                integers(0, 0)
                integers(1, 1)
                blocks(act, one)
                rows_out(NB - 1)

            @block.gpsimd
            def _(pool):
                pool.wait_ge(qo_done, SHARED // BLK)
                pool.dma_start(condT[:], a["condT"].rearrange("(k p) b -> p k b", p=P)).then_inc(d_c, 16)
                pool.dma_start(bias[:], a["b_gru"]).then_inc(d_c, 16)
                pool.dma_start(gwraw[:], a["gate_w"].rearrange("(k p) e -> p k e", p=P)).then_inc(d_c, 16)
                pool.tensor_scalar(idsc[:], cst[:, C_ID:C_ID + P], SC, None, ALU.mult).then_inc(g_hi, 1)
                for g in range(GATES):
                    pool.dma_start(cond_w[:, g], a["C_gru"][g].rearrange("(k p) n -> p k n", p=P)).then_inc(d_c, 16)
                for g in range(GATES):
                    pool.dma_start(raw[0][:, g], a["U_gru"][g].rearrange("(k p) n -> p k n", p=P)).then_inc(d_g, 16)
                    pool.dma_start(raw[1][:, g], a["W_gru"][g].rearrange("(k p) n -> p k n", p=P)).then_inc(d_g, 16)
                pool.wait_ge(d_c, 48 + 16 * GATES)
                pool.tensor_scalar(bias[:], bias[:], SC, None, ALU.mult).then_inc(bias_sc, 1)
                pool.wait_ge(d_g, 32 * GATES)
                parts = [(raw[0], wh[:, 0], wl[:, 0]), (raw[1], wh[:, 1], wl[:, 1]), (gwraw[:], gwh[:], gwl[:])]
                for full, high, low in parts:
                    pool.tensor_scalar(high, full, SC, None, ALU.mult).then_inc(g_hi, 1)
                pool.wait_ge(g_hi, 1 + len(parts))
                for full, high, low in parts:
                    pool.tensor_scalar(full, full, SC, None, ALU.mult).then_inc(g_scaled, 1)
                for n, (full, high, low) in enumerate(parts):
                    pool.wait_ge(g_scaled, n + 1)
                    pool.tensor_tensor(low, full, high, ALU.subtract).then_inc(g_lo, 1)
                pool.wait_ge(lo_done, 1)
                pool.tensor_copy(xc0[:, 0], x1h[:, :, 0:P]).then_inc(xc_done, 1)
                pool.tensor_copy(xc0[:, 1], x1l[:, :, 0:P]).then_inc(xc_done, 1)
                pool.wait_ge(v_done, GATES * K)
                pool.tensor_copy(vh[:], vf[:]).then_inc(g_hi, 1)
                pool.wait_ge(g_hi, 2 + len(parts))
                pool.tensor_tensor(vl[:], vf[:], vh[:], ALU.subtract).then_inc(g_lo, 1)
                pool.wait_ge(g_lo, len(parts) + 1)
                pool.wait_ge(xc_done, 2)

            @block.tensor
            def _(pe):
                def rows_back(j, par):
                    pe.wait_ge(x1_done, j + 1)
                    pe.wait_ge(rows_done, j + 1)
                    for c in range(4):
                        for k in range(K):
                            ins = pe.transpose(ps_t[c // 2][:, c % 2, k * P:(k + 1) * P], x1[par][:, k, c * P:(c + 1) * P],
                                               cst[:, C_ID:C_ID + P])
                    ins.then_inc(tr, 1)

                def one(j, par):
                    pe.wait_ge(ql_done, j + 3)
                    for m in range(K):
                        n = 0
                        for k in range(FO):
                            w0 = D0 + k * D + m * P
                            for w, x in pair_products(wTh[:, w0:w0 + P], wTl[:, w0:w0 + P], qh[par][:, k], ql[par][:, k]):
                                ins = pe.matmul(ps_d[par][m][:], w, x, start=(n == 0), stop=(n == 3 * FO - 1))
                                n += 1
                    ins.then_inc(mm, 1)
                    if not isinstance(j, int) or j > 0:
                        rows_back(j - 1, 1 - par)
                    if isinstance(j, int) and j == NB - 3:
                        pe.wait_ge(d_c, 48 + 16 * GATES)
                        for g in range(GATES):
                            for m in range(K):
                                for k in range(K):
                                    c0 = (g * K + m) * BATCH
                                    ins = pe.matmul(ps_v[:, c0:c0 + BATCH], cond_w[:, g, k, m * P:(m + 1) * P], condT[:, k],
                                                    start=(k == 0), stop=(k == K - 1))
                        ins.then_inc(v_mm, 1)

                pe.sem_inc(mm, 1)
                pe.sem_inc(tr, 1)
                blocks(pe, one)
                rows_back(NB - 1, (NB - 1) % 2)

            @block.vector
            def _(dve):
                def split(j, par):
                    dve.wait_ge(qo_done, j + 1)
                    if not isinstance(j, int) or j > 0:
                        dve.wait_ge(mm, j)
                    dve.tensor_copy(qh[par][:], qo[par][:]).then_inc(qh_done, 1)
                    dve.wait_ge(qh_done, j + 1)
                    dve.tensor_tensor(ql[par][:], qo[par][:], qh[par][:], ALU.subtract).then_inc(ql_done, 1)

                def one(j, par):
                    if before(j, 1):
                        split(j + 1, 1 - par)
                    dve.wait_ge(mm, j + 2)
                    dve.wait_ge(d_x[par], 8 * (j - par) + 16)
                    dve.wait_ge(tr, j if not isinstance(j, int) else max(j, 1))
                    for m in range(K):
                        o = dve.scalar_tensor_tensor(out=x1[par][:, m], in0=ps_d[par][m][:], scalar=column(scal, S_DN),
                                                     in1=xin[par][:, m], op0=ALU.mult, op1=ALU.add)
                    o.then_inc(x1_done, 1)
                    dve.wait_ge(x1_done, j + 1)
                    dve.wait_ge(hi_done, j + 1)
                    dve.scalar_tensor_tensor(out=x1l[:, :, bass.ds(j * BLK, BLK)], in0=x1[par][:], scalar=SC,
                                             in1=x1h[:, :, bass.ds(j * BLK, BLK)], op0=ALU.mult, op1=ALU.subtract)\
                       .then_inc(lo_done, 1)

                dve.sem_inc(ql_done, 2)
                split(0, 0)
                blocks(dve, one)
                dve.wait_ge(lo_done, NB)


def stage_gru(nc, a, keep):
    x1h, x1l, Lg = keep["x0h"], keep["x0l"], keep["Lg"]
    table = keep["table"]
    G = GATES
    R_, Z_, C_ = range(G)
    NC2 = NT // 2
    with ExitStack() as ctx:
        s = Space(nc, ctx, "gru")
        wh, wl, gwh, gwl, idsc, vh, vl, xc = (keep[n] for n in ("wh", "wl", "gwh", "gwl", "idsc", "vh", "vl", "xc"))
        idh = keep["cst16"][:, H_ID:H_ID + P]
        hh = [s.sb(f"hh{p}", [P, K, P], F16) for p in range(2)]
        hl = [s.sb(f"hl{p}", [P, K, P], F16) for p in range(2)]
        Hf = s.sb("Hf", [P, K, BATCH], F32)
        r, z, th, rh, zc, kept, gain = (s.sb(n, [P, K, BATCH], F32) for n in ("r", "z", "th", "rh", "zc", "kept", "gain"))
        rhh, rhl, kepth, keptl, gainh, gainl = (
            s.sb(n, [P, K, BATCH], F16) for n in ("rhh", "rhl", "kepth", "keptl", "gainh", "gainl"))
        rows = [s.sb(f"rows{p}", [P, 2 * D], F16) for p in range(2)]
        psg = [[s.ps(f"g{g}{p}", [P, BLK]) for p in range(2)] for g in range(G)]
        ps_t = s.ps("t", [P, 2 * BLK], F16)
        ps_l = s.ps("l", [P, BLK])
        d_tab, rows_free = keep["d_tab"], s.sem("rows_free")
        xc_ready, proj_done = s.sem("xc_ready"), s.sem("proj_done")
        r_mm, z_mm, c_mm, r_done, z_done, t_done = (s.sem(n) for n in ("r_mm", "z_mm", "c_mm", "r_done", "z_done", "t_done"))
        rh_hi, rh_lo, h_hi, h_lo, dv = (s.sem(n) for n in ("rh_hi", "rh_lo", "h_hi", "h_lo", "dv"))
        kept_hi, kept_lo, gain_hi, gain_lo = (s.sem(n) for n in ("kept_hi", "kept_lo", "gain_hi", "gain_lo"))
        tile_mm, lg_read, row_done, init = s.sem("tile_mm"), s.sem("lg_read"), s.sem("row_done"), s.sem("init")

        def cols(step):
            return slice(step * BATCH, (step + 1) * BATCH)

        with nc.Block() as block:
            @block.sync
            def _(sp):
                sp.wait_ge(keep["d_out"], 16 * NB)
                sp.sem_inc(rows_free, 2)
                with sp.Fori(0, NC2) as i:
                    for par in range(2):
                        c = 2 * i + par
                        sp.wait_ge(row_done, c + 2)
                        sp.dma_start(table[bass.ds(c * P, P), 0:2 * D], rows[par][:].bitcast(U16)).then_inc(d_tab, 16)
                        sp.wait_ge(d_tab, 16 * c + 16)
                        sp.sem_inc(rows_free, 1)
                sp.wait_ge(row_done, NT + 2)
                sp.dma_start(table[NT * P:(NT + 1) * P, 0:2 * D], rows[0][:].bitcast(U16)).then_inc(d_tab, 16)

            @block.gpsimd
            def _(pool):
                def fetch(c, par):
                    pool.tensor_copy(xc[par][:, 0], x1h[:, :, bass.ds(c * P, P)])
                    pool.tensor_copy(xc[par][:, 1], x1l[:, :, bass.ds(c * P, P)]).then_inc(xc_ready, 1)
                pool.sem_inc(xc_ready, 1)
                with pool.Fori(0, NC2) as i:
                    for par in range(2):
                        c = 2 * i + par
                        pool.wait_ge(proj_done, c + 1)
                        fetch(c + 1, 1 - par)

            @block.tensor
            def _(pe):
                def share_of_x(par, lo, hi):
                    n = 0
                    for g in range(G):
                        for m in range(K):
                            out = psg[g][par][:, m * P:(m + 1) * P]
                            ms = slice(m * P, (m + 1) * P)
                            todo = [(w, x) for k in range(K) for w, x in
                                    pair_products(wh[:, 1, g, k, ms], wl[:, 1, g, k, ms], xc[par][:, 0, k], xc[par][:, 1, k])]
                            for v in (vh, vl):
                                todo.append((idsc[:], v[:, g * K + m].unsqueeze(1).to_broadcast([P, TILE_STEPS, BATCH])))
                            for j, (w, x) in enumerate(todo):
                                if lo <= n < hi:
                                    o = out.rearrange("p (t b) -> p t b", b=BATCH) if j >= 3 * K else out
                                    ins = pe.matmul(o, w, x, start=(m == 0 and j == 0), stop=True, skip_group_check=True)
                                n += 1
                    if hi == 48:
                        ins.then_inc(proj_done, 1)

                def recurrence(g, par, step, high, low, low_ready, between=lambda: None):
                    outs = [psg[g][par][:, m * P + step * BATCH:m * P + (step + 1) * BATCH] for m in range(K)]
                    for m in range(K):
                        for k in range(K):
                            for w in (wh, wl):
                                pe.matmul(outs[m], w[:, 0, g, k, m * P:(m + 1) * P], high(k), start=False, stop=True,
                                          skip_group_check=True)
                    between()
                    pe.wait_ge(*low_ready)
                    for m in range(K):
                        for k in range(K):
                            ins = pe.matmul(outs[m], wh[:, 0, g, k, m * P:(m + 1) * P], low(k), start=False, stop=True,
                                            skip_group_check=True)
                    return ins

                def finished_tile(par, pieces):
                    for i in pieces:
                        if i < 2 * K:
                            pe.transpose(ps_t[:, i * P:(i + 1) * P], (hh, hl)[i // K][par][:, i % K], idh)
                            continue
                        n = 0
                        for k in range(K):
                            for h, w in ((hh, gwh), (hl, gwh), (hh, gwl)):
                                ins = pe.matmul(ps_l[:, 0:E], h[par][:, k], w[:, k], start=(n == 0), stop=(n == 3 * K - 1))
                                n += 1
                        ins.then_inc(tile_mm, 1)

                pe.sem_inc(proj_done, 1)
                pe.wait_ge(xc_ready, 1)
                share_of_x(0, 0, 48)
                with pe.Fori(0, NC2) as i:
                    for par in range(2):
                        c = 2 * i + par
                        for st in range(TILE_STEPS):
                            t = TILE_STEPS * c + st
                            hp, hc = (par, cols(st - 1)) if st else (1 - par, cols(TILE_STEPS - 1))

                            def beside(first, count):
                                if st == 0:
                                    finished_tile(1 - par, [i - 2 for i in range(first, first + count) if i >= 2])
                                else:
                                    n = 7 * (st - 1) + first
                                    if n < 48:
                                        share_of_x(1 - par, n, min(n + count, 48))

                            if st == 0:
                                pe.wait_ge(lg_read, c + 1)
                                pe.wait_ge(row_done, c + 1)
                            if st == 1:
                                pe.wait_ge(xc_ready, c + 2)
                            pe.wait_ge(gain_hi, t + 1)
                            recurrence(R_, par, st, lambda k: gainh[:, k], lambda k: gainl[:, k], (gain_lo, t + 1),
                                       lambda: beside(0, 1)).then_inc(r_mm, 1)
                            pe.wait_ge(h_hi, t + 1)
                            recurrence(Z_, par, st, lambda k: hh[hp][:, k, hc], lambda k: hl[hp][:, k, hc], (h_lo, t + 1),
                                       lambda: beside(1, 1)).then_inc(z_mm, 1)
                            beside(2, 2)
                            pe.wait_ge(rh_hi, t + 1)
                            recurrence(C_, par, st, lambda k: rhh[:, k], lambda k: rhl[:, k], (rh_lo, t + 1),
                                       lambda: beside(4, 1)).then_inc(c_mm, 1)
                            beside(5, 1)
                            pe.wait_ge(kept_hi, t + 1)
                            np_, ns = (par, st + 1) if st + 1 < TILE_STEPS else (1 - par, 0)
                            recurrence(R_, np_, ns, lambda k: kepth[:, k], lambda k: keptl[:, k], (kept_lo, t + 1),
                                       lambda: beside(6, 1))
                pe.wait_ge(h_lo, STEPS + 1)
                pe.wait_ge(h_hi, STEPS + 1)
                pe.wait_ge(lg_read, NT + 1)
                pe.wait_ge(row_done, NT + 1)
                finished_tile(1, range(2 * K + 1))

            @block.scalar
            def _(act):
                def gate(g, par, st):
                    return psg[g][par][:, 0:K * P].rearrange("p (m t b) -> p m t b", m=K, b=BATCH)[:, :, st]

                def rows_piece(par, q):
                    return act.activation(rows[par][:, q * P:(q + 1) * P], ps_t[:, q * P:(q + 1) * P], ACT.Copy)

                act.sem_inc(row_done, 1)
                with act.Fori(0, NC2) as i:
                    for par in range(2):
                        c = 2 * i + par
                        for st in range(TILE_STEPS):
                            t = TILE_STEPS * c + st
                            act.wait_ge(r_mm, t + 1)
                            act.activation(r[:], gate(R_, par, st), ACT.Sigmoid, scale=INV2).then_inc(r_done, 1)
                            act.wait_ge(z_mm, t + 1)
                            act.activation(z[:], gate(Z_, par, st), ACT.Sigmoid, scale=INV2).then_inc(z_done, 1)
                            if 2 <= st < 6:
                                if st == 2:
                                    act.wait_ge(tile_mm, c + 1)
                                    act.wait_ge(rows_free, c + 1)
                                p = rows_piece(par, st - 2)
                                if st == 5:
                                    p.then_inc(row_done, 1)
                            act.wait_ge(c_mm, t + 1)
                            act.activation(th[:], gate(C_, par, st), ACT.Tanh, scale=INV2).then_inc(t_done, 1)
                act.wait_ge(tile_mm, NT + 1)
                act.wait_ge(rows_free, NT + 1)
                for q in range(2 * K):
                    p = rows_piece(0, q)
                p.then_inc(row_done, 1)

            @block.vector
            def _(dve):
                dve.memset(Hf[:], 0.0).then_inc(init, 1)
                dve.memset(hh[1][:], 0.0).then_inc(init, 1)
                dve.memset(hl[1][:], 0.0).then_inc(init, 1)
                dve.memset(gainh[:], 0.0).then_inc(init, 1)
                dve.memset(gainl[:], 0.0).then_inc(init, 1)
                dve.wait_ge(init, 5)
                dve.sem_inc(gain_hi, 1)
                dve.sem_inc(gain_lo, 1)
                dve.sem_inc(h_hi, 1)
                dve.sem_inc(h_lo, 1)
                dve.sem_inc(lg_read, 1)

                def logits(c):
                    dve.wait_ge(tile_mm, c + 1)
                    dve.tensor_scalar(Lg[:, bass.ds(c, 1)], ps_l[:, 0:E].unsqueeze(1), INV2, None, ALU.mult).then_inc(lg_read, 1)

                with dve.Fori(0, NC2) as i:
                    for par in range(2):
                        c = 2 * i + par
                        for st in range(TILE_STEPS):
                            t = TILE_STEPS * c + st
                            dve.wait_ge(r_done, t + 1)
                            dve.tensor_tensor(rhh[:], r[:], Hf[:], ALU.mult).then_inc(rh_hi, 1)
                            dve.tensor_tensor(rh[:], r[:], Hf[:], ALU.mult).then_inc(dv, 1)
                            dve.wait_ge(dv, 5 * t + 1)
                            dve.tensor_tensor(rhl[:], rh[:], rhh[:], ALU.subtract).then_inc(rh_lo, 1)
                            dve.wait_ge(z_done, t + 1)
                            dve.tensor_scalar(zc[:], z[:], -1.0, 1.0, ALU.mult, ALU.add).then_inc(dv, 1)
                            dve.wait_ge(dv, 5 * t + 2)
                            dve.tensor_tensor(kepth[:], zc[:], Hf[:], ALU.mult).then_inc(kept_hi, 1)
                            dve.tensor_tensor(kept[:], zc[:], Hf[:], ALU.mult).then_inc(dv, 1)
                            dve.wait_ge(dv, 5 * t + 3)
                            dve.tensor_tensor(keptl[:], kept[:], kepth[:], ALU.subtract).then_inc(kept_lo, 1)
                            dve.wait_ge(t_done, t + 1)
                            for out, done in ((gainh, gain_hi), (gain, dv)):
                                dve.scalar_tensor_tensor(out=out[:], in0=z[:], scalar=SC, in1=th[:], op0=ALU.mult, op1=ALU.mult)\
                                    .then_inc(done, 1)
                            dve.wait_ge(dv, 5 * t + 4)
                            dve.tensor_tensor(gainl[:], gain[:], gainh[:], ALU.subtract).then_inc(gain_lo, 1)
                            dve.tensor_tensor(hh[par][:, :, cols(st)], gain[:], kept[:], ALU.add).then_inc(h_hi, 1)
                            dve.tensor_tensor(Hf[:], gain[:], kept[:], ALU.add).then_inc(dv, 1)
                            dve.wait_ge(dv, 5 * t + 5)
                            dve.tensor_tensor(hl[par][:, :, cols(st)], Hf[:], hh[par][:, :, cols(st)], ALU.subtract)\
                                .then_inc(h_lo, 1)
                            if st == 3:
                                logits(c)
                logits(NT)
                dve.wait_ge(lg_read, NT + 2)


def stage_route(nc, a, keep):
    cst, cst16, Lg, table, gidx, sidx = (keep[n] for n in ("cst", "cst16", "Lg", "table", "gidx", "sidx"))
    b_less, b_same, t_less, io16 = (cst16[:, h:h + P] for h in (H_BLESS, H_BSAME, H_TLESS, H_IOTA))
    NQ = TOPK * NT
    QB = 16
    PAD = NT // 2
    with ExitStack() as ctx:
        s = Space(nc, ctx, "rt")
        M = s.sb("M", [P, TOPK, NT, E], F16)
        best = s.sb("best", [P, TOPK, NT], F32)
        first = s.sb("first", [P, TOPK, NT], F32)
        eq, L2 = s.sb("eq", [P, NT, E], F32), s.sb("L2", [P, NT, E], F32)
        pr = s.sb("pr", [P, 4, NT], F32)
        prob, prob2 = s.sb("prob", [P, NT, E], F32), s.sb("prob2", [P, NT, E], F32)
        ones = s.sb("ones", [P, P], F16)
        total, totalf = s.sb("total", [P, TOPK, E], F16), s.sb("totalf", [P, TOPK, E], F32)
        scan = [s.sb(f"scan{i}", [P, TOPK, PAD + NT + 1, E], F16) for i in range(2)]
        rank, V = s.sb("rank", [P, TOPK, NT, E], F32), s.sb("V", [P, TOPK, NT, E], F32)
        slot, own = s.sb("slot", [P, NQ], F32), s.sb("own", [P, NQ], F32)
        hi_i = s.sb("hi_i", [P, NQ], I16)
        lo = s.sb("lo", [P, NQ], F32)
        lo16, hi16 = s.sb("lo16", [P, NQ], F16), s.sb("hi16", [P, NQ], F16)
        onelo = [s.sb(f"onelo{i}", [P, QB, P], F16) for i in range(2)]
        onehi = [s.sb(f"onehi{i}", [P, QB, SLOT_TILES], F16) for i in range(2)]
        val = [s.sb(f"val{i}", [P, QB, 2, SLOT_TILES], F16) for i in range(2)]
        I, empty = s.sb("I", [P, SLOT_TILES], F32), s.sb("empty", [P, SLOT_TILES], F32)
        gI = s.sb("gI", [P, SLOT_TILES], F32)
        ps_r, ps_i = s.ps("ps_r", [P, BLK]), s.ps("ps_i", [P, BLK])
        ch, exp_in, exp_done, prob_ready, d_prob = (s.sem(n) for n in ("ch", "exp_in", "exp_done", "prob_ready", "d_prob"))
        count_in, ranked, ones_ready, ones_used, hot, tile_ready = (
            s.sem(n) for n in ("count_in", "ranked", "ones_ready", "ones_used", "hot", "tile_ready"))
        fcb, pjb, wst, wh, wl = (keep[n] for n in ("fcb", "pjb", "wst", "ewh", "ewl"))
        d_b, d_w, w_hi, w_scaled, w_lo = (s.sem(n) for n in ("d_b", "d_w", "w_hi", "w_scaled", "w_lo"))
        wide = [P, NT, E]
        L = Lg[:, 1:]
        rounds = [1 << d for d in range(NT.bit_length() - 1)]

        with nc.Block() as block:
            @block.sync
            def _(sp):
                sp.dma_start(wst[0][:], a["c_fc"][0].rearrange("(k p) n -> p k n", p=P)).then_inc(d_w, 16)
                sp.dma_start(wst[1][:], a["c_proj"][0].rearrange("(k p) n -> p k n", p=P)).then_inc(d_w, 16)
                sp.dma_start(fcb[:], a["fc_bias"]).then_inc(d_b, 16)
                sp.dma_start(pjb[:], a["proj_bias"].partition_broadcast(P)).then_inc(d_b, 16)
                sp.wait_ge(d_b, 32)
                sp.wait_ge(keep["d_tab"], 16 * (NT + 1))
                sp.wait_ge(prob_ready, 1)
                sp.dma_start(table[P:, 2 * D:].rearrange("(i p) c -> p i c", p=P), prob2[:].bitcast(U16)).then_inc(d_prob, 16)
                sp.wait_ge(d_prob, 16)

            @block.scalar
            def _(act):
                act.wait_ge(exp_in, 1)
                act.activation(pr[:, 1], pr[:, 0], ACT.Exp).then_inc(exp_done, 1)
                act.wait_ge(d_w, 32)
                for j in range(2):
                    act.activation(wh[0][j][:], wst[j][:], ACT.Copy, scale=SC).then_inc(w_hi, 1)
                act.wait_ge(w_hi, 2)
                for j in range(2):
                    act.activation(wst[j][:], wst[j][:], ACT.Copy, scale=SC).then_inc(w_scaled, 1)

            @block.gpsimd
            def _(pool):
                def low(j):
                    pool.wait_ge(w_scaled, j + 1)
                    pool.tensor_tensor(wl[0][j][:], wst[j][:], wh[0][j][:], ALU.subtract).then_inc(w_lo, 1)

                low(0)
                for b in range(NQ // QB):
                    i0 = b * QB % NT
                    pool.wait_ge(hot, b + 1)
                    pool.tensor_tensor(val[b % 2][:, :, 0], onehi[b % 2][:],
                                       cst16[:, H_TILE + i0:H_TILE + i0 + QB].unsqueeze(2).to_broadcast([P, QB, SLOT_TILES]),
                                       ALU.mult).then_inc(tile_ready, 1)
                low(1)
                pool.wait_ge(w_lo, 2)

            @block.tensor
            def _(pe):
                pe.wait_ge(count_in, 1)
                last = scan[len(rounds) % 2]
                pe.matmul(ps_r[:], t_less, M[:].rearrange("p k i e -> p (k i e)"), start=True, stop=False, skip_group_check=True)
                for k in range(TOPK):
                    out = ps_r[:, k * NT * E:(k + 1) * NT * E].rearrange("p (i e) -> p i e", e=E)
                    pe.matmul(out, b_same, last[:, k, PAD:PAD + NT], start=False, stop=False, skip_group_check=True)
                    pe.matmul(out, b_less, total[:, k].unsqueeze(1).to_broadcast(wide), start=False, stop=False,
                              skip_group_check=True)
                pe.matmul(out, ones[:], total[:, 0].unsqueeze(1).to_broadcast(wide), start=False, stop=True,
                          skip_group_check=True).then_inc(ranked, 1)
                for b in range(NQ // QB):
                    pe.wait_ge(ones_ready, b + 1)
                    pe.wait_ge(tile_ready, b + 1)
                    for q in range(QB):
                        ins = pe.matmul(ps_i[:, 0:2 * SLOT_TILES], onelo[b % 2][:, q], val[b % 2][:, q].rearrange("p a n -> p (a n)"),
                                        start=(b == 0 and q == 0), stop=(b == NQ // QB - 1 and q == QB - 1))
                    ins.then_inc(ones_used, 1)

            @block.vector
            def _(dve):
                c = Chain(dve, ch)

                def row(col, shape):
                    return cst[:, col:col + E].unsqueeze(1).to_broadcast(shape)

                c.link(dve.memset(ones[:], 1.0))
                for i in range(2):
                    c.link(dve.memset(scan[i][:], 0.0))
                for k, src in ((0, L), (1, L2[:])):
                    c.step(dve.tensor_reduce(best[:, k], src, X, ALU.max))
                    c.step(dve.tensor_tensor(eq[:], src, best[:, k].unsqueeze(2).to_broadcast(wide), ALU.is_equal))
                    c.step(dve.tensor_tensor(eq[:], eq[:], row(C_EIDX, wide), ALU.mult))
                    c.step(dve.tensor_reduce(first[:, k], eq[:], X, ALU.max))
                    c.step(dve.tensor_tensor(M[:, k], eq[:], first[:, k].unsqueeze(2).to_broadcast(wide), ALU.is_equal))
                    if k == 0:
                        c.step(dve.scalar_tensor_tensor(out=L2[:], in0=M[:, 0], scalar=-3e38, in1=L, op0=ALU.mult, op1=ALU.add))
                dve.tensor_tensor(pr[:, 0], best[:, 1], best[:, 0], ALU.subtract).then_inc(exp_in, 1)
                c.step(dve.tensor_reduce(totalf[:], M[:].rearrange("p k i e -> p k e i"), X, ALU.add))
                c.link(dve.tensor_copy(total[:], totalf[:]))
                for k in range(TOPK):
                    c.link(dve.tensor_copy(scan[0][:, k, PAD + 1:], M[:, k]))
                c.wait()
                for n, d in enumerate(rounds):
                    for k in range(TOPK):
                        c.link(dve.tensor_tensor(scan[(n + 1) % 2][:, k, PAD:PAD + NT], scan[n % 2][:, k, PAD:PAD + NT],
                                                 scan[n % 2][:, k, PAD - d:PAD + NT - d], ALU.add))
                    c.wait()
                dve.sem_inc(count_in, 1)
                dve.wait_ge(exp_done, 1)
                c.step(dve.tensor_scalar(pr[:, 2], pr[:, 1], 1.0, None, ALU.add))
                c.step(dve.reciprocal(pr[:, 3], pr[:, 2]))
                c.step(dve.tensor_tensor(pr[:, 2], pr[:, 1], pr[:, 3], ALU.mult))
                c.link(dve.tensor_tensor(prob[:], M[:, 0], pr[:, 3].unsqueeze(2).to_broadcast(wide), ALU.mult))
                c.step(dve.tensor_tensor(eq[:], M[:, 1], pr[:, 2].unsqueeze(2).to_broadcast(wide), ALU.mult))
                dve.tensor_tensor(prob2[:], prob[:], eq[:], ALU.add).then_inc(prob_ready, 1)
                dve.wait_ge(ranked, 1)
                c.step(dve.tensor_copy(rank[:].rearrange("p k i e -> p (k i e)"), ps_r[:]))
                rq, Vq, Mq = (x[:].rearrange("p k i e -> p (k i) e") for x in (rank, V, M))
                wq = [P, NQ, E]
                c.step(dve.tensor_tensor(Vq, rq, row(C_EOFF, wq), ALU.add))
                c.step(dve.tensor_tensor(Vq, Vq, Mq, ALU.mult))
                c.link(dve.tensor_reduce(slot[:], Vq, X, ALU.add))
                c.step(dve.tensor_tensor(rq, rq, Mq, ALU.mult))
                c.step(dve.tensor_reduce(own[:], rq, X, ALU.add))
                c.step(dve.tensor_scalar(own[:], own[:], float(CAP), 2.0 * E * CAP, ALU.is_ge, ALU.mult))
                c.step(dve.tensor_tensor(slot[:], slot[:], own[:], ALU.add))
                c.step(dve.tensor_scalar(hi_i[:], slot[:], -(P - 1) / 2, 1.0 / P, ALU.add, ALU.mult))
                c.link(dve.tensor_copy(hi16[:], hi_i[:]))
                c.step(dve.scalar_tensor_tensor(out=lo16[:], in0=hi_i[:], scalar=-float(P), in1=slot[:], op0=ALU.mult, op1=ALU.add))
                for b in range(NQ // QB):
                    qs = slice(b * QB, (b + 1) * QB)
                    i0 = b * QB % NT
                    if b >= 2:
                        dve.wait_ge(ones_used, b - 1)
                    w = [P, QB, SLOT_TILES]
                    dve.tensor_tensor(onehi[b % 2][:], io16[:, 0:SLOT_TILES].unsqueeze(1).to_broadcast(w),
                                      hi16[:, qs].unsqueeze(2).to_broadcast(w), ALU.is_equal).then_inc(hot, 1)
                    dve.tensor_tensor(onelo[b % 2][:], io16.unsqueeze(1).to_broadcast([P, QB, P]),
                                      lo16[:, qs].unsqueeze(2).to_broadcast([P, QB, P]), ALU.is_equal)
                    dve.wait_ge(hot, b + 1)
                    dve.tensor_scalar(val[b % 2][:, :, 1], onehi[b % 2][:], cst[:, C_P1:C_P1 + 1], None, ALU.mult)\
                       .then_inc(ones_ready, 1)
                dve.wait_ge(ones_used, NQ // QB)
                c.step(dve.tensor_copy(gI[:], ps_i[:, SLOT_TILES:2 * SLOT_TILES]))
                c.step(dve.scalar_tensor_tensor(out=I[:], in0=ps_i[:, 0:SLOT_TILES], scalar=float(P), in1=gI[:],
                                                op0=ALU.mult, op1=ALU.add))
                c.link(dve.tensor_scalar(empty[:], I[:], 0.0, cst[:, C_DUM:C_DUM + 1], ALU.is_equal, ALU.mult))
                c.step(dve.tensor_scalar(gI[:], I[:], -1.0, 0.0, ALU.add, ALU.max))
                c.link(dve.tensor_scalar(gidx[:], gI[:], float(P), None, ALU.add))
                c.step(dve.scalar_tensor_tensor(out=sidx[:], in0=I[:], scalar=-1.0, in1=empty[:], op0=ALU.add, op1=ALU.add))


def stage_experts(nc, a, keep):
    table, gidx, sidx, out = keep["table"], keep["gidx"], keep["sidx"], a["out"]
    GROUPS = [(0, 4), (4, 4), (8, CT - 8)]
    RFC, RG, RY = 4, 3, 4
    UNITS = len(GROUPS) * HM
    with ExitStack() as ctx:
        s = Space(nc, ctx, "ex")
        fcb, pjb, wst, wh, wl = (keep[n] for n in ("fcb", "pjb", "wst", "ewh", "ewl"))
        idh = keep["cst16"][:, H_ID:H_ID + P]
        gi = [s.sb(f"gi{p}", [P, CT], U32) for p in range(2)]
        si = [s.sb(f"si{p}", [P, CT], U32) for p in range(2)]
        got = [s.sb(f"got{p}", [P, CT, ROW], U16) for p in range(2)]
        fb = [s.sb(f"fb{p}", [P, HM], F32) for p in range(2)]
        weight = [s.sb(f"weight{p}", [P, CT, 1], F32) for p in range(2)]
        xg = s.sb("xg", [P, 2, K, CAP], F16)
        gel = [s.sb(f"gel{i}", [P, BLK], F32) for i in range(RG)]
        Gh = [s.sb(f"Gh{i}", [P, HM, BLK], F16) for i in range(2)]
        Gl = [s.sb(f"Gl{i}", [P, HM, BLK], F16) for i in range(2)]
        y1 = [s.sb(f"y1{i}", [P, D], F32) for i in range(2)]
        y = [s.sb(f"y{i}", [P, D], F32) for i in range(RY)]
        ps_x = [s.ps(f"x{i}", [P, 2 * BLK], F16) for i in range(2)]
        ps_f = [s.ps(f"f{i}", [P, BLK]) for i in range(RFC)]
        ps_y = [s.ps(f"y{i}", [P, BLK]) for i in range(2)]
        d_w, d_s = s.sem("d_w"), s.sem("d_s")
        d_g = [[s.sem(f"d_g{p}{g}") for g in range(2)] for p in range(2)]
        idx_in, w_hi, w_lo, xt_mm, xt_done = (s.sem(n) for n in ("idx_in", "w_hi", "w_lo", "xt_mm", "xt_done"))
        fc_mm, gel_done, g_hi, g_lo, y_mm, y1_done, y_done, stored, fb_in, w_in = (
            s.sem(n) for n in ("fc_mm", "gel_done", "g_hi", "g_lo", "y_mm", "y1_done", "y_done", "stored", "fb_in", "w_in"))
        first = GROUPS[0][1]

        def order(fc, proj):
            fc(0), fc(1), proj(0), fc(2), proj(1), proj(2)

        def quarter(bufs, n):
            half = slice(n % 2 * (K // 2), (n % 2 + 1) * (K // 2)) if n < 2 else slice(n % 2 * (HM // 2), (n % 2 + 1) * (HM // 2))
            return bufs[n // 2][:, half].rearrange("p a b -> p (a b)")

        with nc.Block() as block:
            @block.sync
            def _(sp):
                with sp.Fori(0, E) as e:
                    sp.wait_ge(w_lo, 4 * e + 4)
                    n = (e + 1) % E
                    sp.dma_start(wst[0][:], a["c_fc"][bass.ds(n, 1)].squeeze(0).rearrange("(k p) n -> p k n", p=P)).then_inc(d_w, 16)
                    sp.dma_start(wst[1][:], a["c_proj"][bass.ds(n, 1)].squeeze(0).rearrange("(k p) n -> p k n", p=P)).then_inc(d_w, 16)

            @block.gpsimd
            def _(pool):
                def gathers(e, p):
                    n = e % E * CT
                    pool.tensor_copy(gi[p][:], gidx[:, bass.ds(n, CT)]).then_inc(idx_in, 1)
                    pool.tensor_copy(si[p][:], sidx[:, bass.ds(n, CT)]).then_inc(idx_in, 1)
                    pool.wait_ge(idx_in, 2 * e + 2)
                    pool.tensor_copy(fb[p][:], fcb[:, bass.ds(e % E * HM, HM)]).then_inc(fb_in, 1)
                    for t in range(CT):
                        pool.indirect_dma_start(out=got[p][:, t], out_offset=None, in_=table,
                                                in_offset=bass.IndirectOffsetOnAxis(ap=gi[p][:, t:t + 1], axis=0))\
                            .then_inc(d_g[p][t >= first], 16)

                def scatters(e, p):
                    for t in range(CT):
                        n = e * CT + t
                        pool.wait_ge(y_done, n + 3)
                        pool.sem_inc(stored, 1)
                        pool.indirect_dma_start(out=out, out_offset=bass.IndirectOffsetOnAxis(ap=si[p][:, t:t + 1], axis=0),
                                                in_=y[(p * CT + t) % RY][:], in_offset=None, compute_op=ALU.add).then_inc(d_s, 16)
                        pool.wait_ge(d_s, 16 * n + 16)

                def weights(e, visit, p):
                    pool.wait_ge(d_g[p][0], 16 * first * visit)
                    pool.wait_ge(d_g[p][1], 16 * (CT - first) * visit)
                    pool.tensor_copy(weight[p][:], got[p][:, :, 2 * D:].bitcast(F32)[:, :, bass.ds(e % E, 1)]).then_inc(w_in, 1)

                pool.sem_inc(stored, RY - 1)
                gathers(0, 0)
                weights(0, 1, 0)
                with pool.Fori(0, E // 2) as i:
                    for p in range(2):
                        e = 2 * i + p
                        gathers(e + 1, 1 - p)
                        scatters(e, p)
                        weights(e + 1, i + 1 + p, 1 - p)

            @block.tensor
            def _(pe):
                pe.sem_inc(y_mm, CT + 1)

                def T(e, p, t, visit):
                    if t == 0:
                        pe.wait_ge(d_g[p][0], 16 * first * visit)
                    if t == first:
                        pe.wait_ge(d_g[p][1], 16 * (CT - first) * visit)
                    pe.wait_ge(xt_done, CT * e + t + 1)
                    for j in range(2 * K):
                        ins = pe.transpose(ps_x[t % 2][:, j * P:(j + 1) * P], got[p][:, t, j * P:(j + 1) * P].bitcast(F16), idh)
                    ins.then_inc(xt_mm, 1)

                for t in range(first):
                    T(0, 0, t, 1)
                with pe.Fori(0, E // 2) as i:
                    for p in range(2):
                        e = 2 * i + p

                        def fc(g):
                            t0, nt = GROUPS[g]
                            pe.wait_ge(xt_done, CT * e + t0 + nt + 2)
                            if g == 0:
                                pe.wait_ge(w_lo, 4 * e + 4)
                            cols = slice(t0 * P, (t0 + nt) * P)
                            for m in range(HM):
                                u = g * HM + m
                                pe.wait_ge(gel_done, UNITS * e + u + 1)
                                ms, n = slice(m * P, (m + 1) * P), 0
                                for k in range(K):
                                    for w, x in pair_products(wh[p][0][:, k, ms], wl[p][0][:, k, ms], xg[:, 0, k, cols], xg[:, 1, k, cols]):
                                        ins = pe.matmul(ps_f[u % RFC][:, 0:nt * P], w, x, start=(n == 0), stop=(n == 3 * K - 1))
                                        n += 1
                                ins.then_inc(fc_mm, 1)
                                if g == 0 and m < CT - first:
                                    T(e, p, first + m, i + 1)

                        def proj(g):
                            t0, nt = GROUPS[g]
                            gb = (p + g) % 2
                            pe.wait_ge(g_lo, UNITS * e + (g + 1) * HM + RG)
                            for t in range(t0, t0 + nt):
                                pe.wait_ge(y1_done, CT * e + t + 1)
                                cs, n = slice((t - t0) * P, (t - t0 + 1) * P), 0
                                for k in range(HM):
                                    for x, w in ((Gh, wh), (Gl, wh), (Gh, wl)):
                                        ins = pe.matmul(ps_y[t % 2][:, 0:D], x[gb][:, k, cs], w[p][1][:, k], start=(n == 0),
                                                        stop=(n == 3 * HM - 1))
                                        n += 1
                                ins.then_inc(y_mm, 1)
                                if g == 1:
                                    T(e + 1, 1 - p, t - t0, i + 1 + p)

                        order(fc, proj)

            @block.scalar
            def _(act):
                def split_high(e, p, n):
                    if n == 0:
                        act.wait_ge(d_w, 32 * e)
                        act.wait_ge(y_mm, CT * e + 1)
                    act.activation(quarter(wh[p], n), quarter(wst, n), ACT.Copy, scale=SC).then_inc(w_hi, 1)

                act.sem_inc(gel_done, RFC)
                act.sem_inc(y_done, 2)
                with act.Fori(0, E // 2) as i:
                    for p in range(2):
                        e = 2 * i + p

                        def fc(g):
                            w = GROUPS[g][1] * P
                            if g == 0:
                                act.wait_ge(fb_in, e + 1)
                            for m in range(HM):
                                u = g * HM + m
                                act.wait_ge(fc_mm, UNITS * e + u + 1)
                                act.wait_ge(g_lo, UNITS * e + u + 1)
                                act.activation(gel[u % RG][:, 0:w], ps_f[u % RFC][:, 0:w], ACT.Gelu, scale=INV2,
                                               bias=fb[p][:, m:m + 1]).then_inc(gel_done, 1)

                        def proj(g):
                            t0, nt = GROUPS[g]
                            if g == 0:
                                act.wait_ge(w_in, e + 1)
                            for t in range(t0, t0 + nt):
                                act.wait_ge(y1_done, CT * e + t + 3)
                                act.wait_ge(stored, CT * e + t + 1)
                                act.activation(y[(p * CT + t) % RY][:], y1[t % 2][:], ACT.Copy,
                                               scale=weight[p][:, t]).then_inc(y_done, 1)
                                if g == 1:
                                    split_high(e + 1, 1 - p, t - t0)

                        order(fc, proj)

            @block.vector
            def _(dve):
                def split_low(e, p, n):
                    dve.wait_ge(w_hi, 4 * e + n - 3)
                    dve.scalar_tensor_tensor(out=quarter(wl[p], n), in0=quarter(wst, n), scalar=SC, in1=quarter(wh[p], n),
                                             op0=ALU.mult, op1=ALU.subtract).then_inc(w_lo, 1)

                def T(e, t):
                    dve.wait_ge(xt_mm, CT * e + t + 1)
                    dve.tensor_copy(xg[:, :, :, t * P:(t + 1) * P],
                                    ps_x[t % 2][:, 0:2 * K * P].rearrange("p (a k n) -> p a k n", a=2, k=K)).then_inc(xt_done, 1)

                dve.sem_inc(w_lo, 4)
                dve.sem_inc(xt_done, 2)
                dve.sem_inc(g_lo, RG)
                dve.sem_inc(y1_done, 2)
                for t in range(first):
                    T(0, t)
                with dve.Fori(0, E // 2) as i:
                    for p in range(2):
                        e = 2 * i + p

                        def fc(g):
                            w, gb = GROUPS[g][1] * P, (p + g) % 2
                            dve.wait_ge(y_mm, 1 + CT * e + (CT - GROUPS[2][1], CT, CT + GROUPS[0][1])[g])
                            for m in range(HM):
                                u = g * HM + m
                                dve.wait_ge(gel_done, UNITS * e + u + 1 + RFC)
                                dve.tensor_scalar(Gh[gb][:, m, 0:w], gel[u % RG][:, 0:w], SC, None, ALU.mult).then_inc(g_hi, 1)
                                dve.wait_ge(g_hi, UNITS * e + u + 1)
                                dve.scalar_tensor_tensor(out=Gl[gb][:, m, 0:w], in0=gel[u % RG][:, 0:w], scalar=SC,
                                                         in1=Gh[gb][:, m, 0:w], op0=ALU.mult, op1=ALU.subtract).then_inc(g_lo, 1)
                                if g == 0 and m < CT - first:
                                    T(e, first + m)

                        def proj(g):
                            t0, nt = GROUPS[g]
                            for t in range(t0, t0 + nt):
                                dve.wait_ge(y_mm, CT * e + t + 2 + CT)
                                dve.wait_ge(y_done, CT * e + t + 1)
                                dve.scalar_tensor_tensor(out=y1[t % 2][:], in0=ps_y[t % 2][:, 0:D], scalar=INV2,
                                                         in1=pjb[:, bass.ds(e * D, D)], op0=ALU.mult, op1=ALU.add).then_inc(y1_done, 1)
                                if g == 1:
                                    T(e + 1, t - t0)
                                    split_low(e + 1, 1 - p, t - t0)

                        order(fc, proj)


def adaln_ffn_moe_kernel(nc, a, stages=99):
    with ExitStack() as ctx:
        s = s0 = Space(nc, ctx, "all")
        keep = {
            "cst": s.sb("cst", [P, C_END], F32),
            "cst16": s.sb("cst16", [P, H_END], F16),
            "scal": s.sb("scal", [P, S_END], F32),
            "x0h": s.sb("x0h", [P, K, N + P], F16),
            "x0l": s.sb("x0l", [P, K, N + P], F16),
        }
        keep["d_out"], keep["d_tab"] = s0.sem("d_out"), s0.sem("d_tab")
        keep["Lg"] = s0.sb("Lg", [P, NT + 1, E], F32)
        keep["table"] = nc.dram_tensor("state_rows", (P * (NT + 1), ROW), U16, kind="Internal").ap()
        with ExitStack() as mid:
            keep["R"] = Space(nc, mid, "ffn").sb("R", [P, FO, N], F32)
            gru_operands(keep)
            with ExitStack() as inner:
                s = Space(nc, inner, "ffn")
                keep["wTh"] = s.sb("wTh", [P, WCOLS], F16)
                keep["wTl"] = s.sb("wTl", [P, WCOLS], F16)
                stage_logits(nc, a, keep)
                with ExitStack() as inner2:
                    keep["qup"] = Space(nc, inner2, "ffn").sb("qup", [P, FO, N], I16)
                    stage_gate_up(nc, a, keep)
                    stage_product(nc, a, keep)
                stage_down(nc, a, keep)
            if stages > 4:
                stage_gru(nc, a, keep)
        if stages > 4:
            keep["gidx"], keep["sidx"] = (s0.sb(n, [P, SLOT_TILES], U32) for n in ("gidx", "sidx"))
        if stages > 5:
            keep["fcb"] = s0.sb("fcb", [P, E * HM], F32)
            keep["pjb"] = s0.sb("pjb", [P, E * D], F32)
            keep["wst"] = [s0.sb("wst_fc", [P, K, H], F32), s0.sb("wst_pj", [P, HM, D], F32)]
            for part in ("ewh", "ewl"):
                keep[part] = [[s0.sb(f"{part}{p}_fc", [P, K, H], F16), s0.sb(f"{part}{p}_pj", [P, HM, D], F16)] for p in range(2)]
            stage_route(nc, a, keep)
        if stages > 6:
            stage_experts(nc, a, keep)


def laid_out(v):
    c = np.ascontiguousarray
    cols = lambda b: c(b.reshape(-1, P).T)
    return {
        "xT": c(v["x"].transpose(2, 1, 0).reshape(D, N)),
        "condT": c(v["cond_1024"].T),
        "weight_matrix": c(v["L0_cond_weight_matrix"]),
        "W_proj": c(v["L0_cond_W_proj"]),
        "b_proj": cols(v["L0_cond_b_proj"]),
        "w_gate": c(v["L0_ffn_w_gate"]),
        "w_up": c(v["L0_ffn_w_up"]),
        "w_down": c(v["L0_ffn_w_down"]),
        "W_gru": c(np.stack([v["L1_cond_W_r"], v["L1_cond_W_z"], v["L1_cond_W"]])),
        "U_gru": c(np.stack([v["L1_cond_U_r"], v["L1_cond_U_z"], v["L1_cond_U"]])),
        "C_gru": c(np.stack([v["L1_cond_C_r"], v["L1_cond_C_z"], v["L1_cond_C"]])),
        "b_gru": c(np.concatenate([cols(v[n]) for n in ("L1_cond_b_r", "L1_cond_b_z", "L1_cond_b")], axis=1)),
        "gate_w": c(v["L1_ffn_gate_w"]),
        "c_fc": c(v["L1_ffn_c_fc"]),
        "fc_bias": cols(v["L1_ffn_fc_bias"]),
        "c_proj": c(v["L1_ffn_c_proj"]),
        "proj_bias": c(v["L1_ffn_proj_bias"].reshape(1, E * D)),
        "consts": constants()[0],
        "consts16": constants()[1],
    }


def kernel(**inputs):
    import concourse.bacc as bacc
    from concourse.bass_utils import run_bass_kernel_spmd

    nc = bacc.Bacc("TRN2", target_bir_lowering=False, num_devices=1)
    given = laid_out({n: np.asarray(v) for n, v in inputs.items()})
    arrays = {f"in_{n}_dram": v for n, v in given.items()}
    a = {n: nc.dram_tensor(f"in_{n}_dram", v.shape, mybir.dt.from_np(v.dtype), kind="ExternalInput").ap()
         for n, v in given.items()}
    a["out"] = nc.dram_tensor("out_0_dram", (N + DUMMY, D), F32, kind="ExternalOutput").ap()
    adaln_ffn_moe_kernel(nc, a)
    r = run_bass_kernel_spmd(nc, [arrays], core_ids=[0])
    got = r.results[0]["out_0_dram"]
    return np.ascontiguousarray(got[:N].reshape(STEPS, BATCH, D).transpose(1, 0, 2))
```
